# Optimizing a Trainium2 kernel written in Bass

```python
import numpy as np
import jax
import jax.numpy as jnp

def _softmax(x, axis=-1):
    return jax.nn.softmax(x, axis=axis)

def _gelu(x):
    return jax.nn.gelu(x, approximate=True)

def _silu(x):
    return jax.nn.silu(x)

def _sigmoid(x):
    return jax.nn.sigmoid(x)

def _layernorm(x, axis=-1, eps=1e-05):
    m = jnp.mean(x, axis=axis, keepdims=True)
    v = jnp.var(x, axis=axis, keepdims=True)
    return (x - m) / jnp.sqrt(v + eps)

def _scatter_add(tgt, idx, src, axis=0):
    return tgt.at[idx].add(src)

def _segment_sum(src, seg, n):
    return jax.ops.segment_sum(src, seg, n)
kernel_name = 'mk_decoder_postln_d1_seqx_r2_c14687'

def setup_inputs(seed: int=0):
    np.random.seed(seed)
    _w = jnp.asarray

    def _rec_inputs():
        import jax
        import jax.numpy as jnp
        _rk = jax.random.key(seed)
        x = 7.22e-05 + 1 * jax.random.normal(jax.random.fold_in(_rk, 1), (4, 1024, 512), jnp.float32)
        _lenS = 1024 - jax.random.randint(jax.random.fold_in(_rk, 7), (4,), 0, max(1, 1024 // 4) + 1, jnp.int32)
        _lenS2 = 2048 - jax.random.randint(jax.random.fold_in(_rk, 8), (4,), 0, max(1, 2048 // 4) + 1, jnp.int32)
        _ctx_768P = jax.random.normal(jax.random.fold_in(_rk, 11), (4, 16, 384), jnp.float32)
        _ctx_768c = jax.random.dirichlet(jax.random.fold_in(_rk, 511), 0.3 * jnp.ones((16,), jnp.float32), (4, 2048))
        _ctx_768t = jnp.einsum('bsk,bkd->bsd', _ctx_768c, _ctx_768P)
        _ctx_768t = _ctx_768t * jax.lax.rsqrt(jnp.mean(jnp.square(_ctx_768t)) + 1e-12) * 0.953939
        ctx_768 = 3.88148e-05 + 0.999967 * (_ctx_768t + 0.3 * jax.random.normal(jax.random.fold_in(_rk, 611), (4, 2048, 384), jnp.float32))
        _validS = jnp.arange(1024)[None, :] < _lenS[:, None]
        _validS2 = jnp.arange(2048)[None, :] < _lenS2[:, None]
        _causal = jnp.tril(jnp.ones((1024, 1024), dtype=bool))
        mask_BxS_bf1 = jnp.ones((4, 1024), dtype=bool)
        mask_BxS2_bf1 = jnp.ones((4, 2048), dtype=bool)
        return (x, ctx_768, mask_BxS_bf1, mask_BxS2_bf1)
    x, ctx_768, mask_BxS_bf1, mask_BxS2_bf1 = _rec_inputs()

    def _L0_attn_setup():
        import jax, jax.numpy as jnp
        import numpy as np
        from jax import lax
        N_EMBD = 512
        N_HEAD = 16
        HEAD_DIM = N_EMBD // N_HEAD
        EPS = 1e-06
        B, T = (4, 1024)

        def _feature_map(x):
            return jax.nn.elu(x) + 1.0
        key = jax.random.key(seed)
        ks = jax.random.split(key, 5)
        scale = 1.0 / np.sqrt(N_EMBD)
        return {'x': jax.random.normal(ks[0], (B, T, N_EMBD), jnp.float32), 'W_attn': jax.random.normal(ks[1], (N_EMBD, 3 * N_EMBD), jnp.float32) * scale, 'b_attn': jax.random.normal(ks[2], (3 * N_EMBD,), jnp.float32) * 0.01, 'W_proj': jax.random.normal(ks[3], (N_EMBD, N_EMBD), jnp.float32) * scale, 'b_proj': jax.random.normal(ks[4], (N_EMBD,), jnp.float32) * 0.01}
    _L0_attn_all = _L0_attn_setup()
    _L0_attn_in = {k: v for k, v in _L0_attn_all.items() if k in ('W_attn', 'b_attn', 'W_proj', 'b_proj')}
    del _L0_attn_all

    def _L0_xattn_setup():
        import jax, jax.numpy as jnp
        import numpy as np
        B, T, DT, G, DV = (16, 256, 512, 288, 384)
        H, DH = (4, 32)
        INNER = H * DH
        HID = 4 * DT
        N_STATE = 64
        K_TOP = 32

        def layernorm(x, g, b, eps=1e-05):
            m = x.mean(-1, keepdims=True)
            v = x.var(-1, keepdims=True)
            return (x - m) * jax.lax.rsqrt(v + eps) * g + b

        def s4d(x, log_dt, A_re, A_im, C_re, C_im, D_skip):
            Bb, L, D = x.shape
            dt = jnp.exp(log_dt)
            A = A_re + 1j * A_im
            C = C_re + 1j * C_im
            dtA = dt[:, None] * A
            dC = C * (jnp.exp(dtA) - 1.0) / A
            powers = jnp.exp(dtA[:, :, None] * jnp.arange(L))
            K = 2.0 * jnp.einsum('dn,dnl->dl', dC, powers).real
            n = 2 * L
            Kf = jnp.fft.rfft(K, n=n, axis=-1)
            xf = jnp.fft.rfft(x, n=n, axis=1)
            y = jnp.fft.irfft(xf * Kf.T[None], n=n, axis=1)[:, :L]
            return y + x * D_skip
        key = jax.random.key(seed)
        ks = jax.random.split(key, 16)
        s = 0.02
        inp = {'x_text': jax.random.normal(ks[0], (B, T, DT), jnp.float32), 'x_vision': jax.random.normal(ks[1], (B, G, DV), jnp.float32), 'text_mask': jnp.ones((B, T), bool), 'vision_mask': jnp.ones((B, G), bool), 'Wq': jax.random.normal(ks[2], (DT, INNER), jnp.float32) * s, 'Wk': jax.random.normal(ks[3], (DV, INNER), jnp.float32) * s, 'Wv': jax.random.normal(ks[4], (DV, DT), jnp.float32) * s, 'W_film_in': jax.random.normal(ks[5], (DT, 2 * DT), jnp.float32) * s, 'b_film_in': jnp.zeros((2 * DT,), jnp.float32), 'W_film_out': jax.random.normal(ks[6], (DT, 2 * DT), jnp.float32) * s, 'b_film_out': jnp.zeros((2 * DT,), jnp.float32), 'g_norm_in': jnp.ones((DT,), jnp.float32), 'b_norm_in': jnp.zeros((DT,), jnp.float32), 'g_norm_out': jnp.ones((DT,), jnp.float32), 'b_norm_out': jnp.zeros((DT,), jnp.float32), 'g_ffn': jnp.ones((DT,), jnp.float32), 'b_ffn': jnp.zeros((DT,), jnp.float32), 'W1': jax.random.normal(ks[7], (DT, HID), jnp.float32) * s, 'b1': jnp.zeros((HID,), jnp.float32), 'W2': jax.random.normal(ks[8], (HID, DT), jnp.float32) * s, 'b2': jnp.zeros((DT,), jnp.float32), 'log_dt': jnp.log(0.001) + jax.random.uniform(ks[9], (DT,), jnp.float32) * (jnp.log(0.1) - jnp.log(0.001)), 'A_re': -0.5 * jnp.ones((DT, N_STATE), jnp.float32), 'A_im': jnp.tile(jnp.pi * jnp.arange(N_STATE, dtype=jnp.float32), (DT, 1)), 'C_re': jax.random.normal(ks[10], (DT, N_STATE), jnp.float32) * 0.5 ** 0.5, 'C_im': jax.random.normal(ks[11], (DT, N_STATE), jnp.float32) * 0.5 ** 0.5, 'D_skip': jax.random.normal(ks[12], (DT,), jnp.float32), 'mod_gate': jnp.array(0.5, jnp.float32)}
        return inp
    _L0_xattn_all = _L0_xattn_setup()
    _L0_xattn_in = {k: v for k, v in _L0_xattn_all.items() if k in ('Wq', 'Wk', 'Wv', 'W_film_in', 'b_film_in', 'W_film_out', 'b_film_out', 'g_norm_in', 'b_norm_in', 'g_norm_out', 'b_norm_out', 'g_ffn', 'b_ffn', 'W1', 'b1', 'W2', 'b2', 'log_dt', 'A_re', 'A_im', 'C_re', 'C_im', 'D_skip', 'mod_gate')}
    del _L0_xattn_all

    def _L0_ffn_setup():
        import jax, jax.numpy as jnp
        import numpy as np
        B, S, D_MODEL, D_HIDDEN = (4, 1024, 512, 2048)

        def act_quant(x):
            scale = 127.0 / jnp.clip(jnp.max(jnp.abs(x), axis=-1, keepdims=True), 1e-05)
            return jnp.clip(jnp.round(x * scale), -128, 127) / scale

        def weight_quant(w):
            scale = 1.0 / jnp.clip(jnp.mean(jnp.abs(w)), 1e-05)
            return jnp.clip(jnp.round(w * scale), -1, 1) / scale

        def bit_linear(x, w):
            xq = x + jax.lax.stop_gradient(act_quant(x) - x)
            wq = w + jax.lax.stop_gradient(weight_quant(w) - w)
            return jnp.einsum('bsd,hd->bsh', xq, wq)

        def depthwise_conv1d(x_bcl, w, b):
            y = jax.lax.conv_general_dilated(x_bcl, w, window_strides=(1,), padding=[(1, 1)], dimension_numbers=('NCH', 'OIH', 'NCH'), feature_group_count=x_bcl.shape[1])
            return y + b[None, :, None]
        key = jax.random.key(seed)
        ks = jax.random.split(key, 5)
        lim1 = 1.0 / np.sqrt(D_MODEL)
        lim2 = 1.0 / np.sqrt(D_HIDDEN)
        limc = 1.0 / np.sqrt(3.0)
        return {'x': jax.random.normal(ks[0], (B, S, D_MODEL), dtype=jnp.float32), 'w1': jax.random.uniform(ks[1], (D_HIDDEN, D_MODEL), jnp.float32, -lim1, lim1), 'conv_w': jax.random.uniform(ks[2], (D_HIDDEN, 1, 3), jnp.float32, -limc, limc), 'conv_b': jax.random.uniform(ks[3], (D_HIDDEN,), jnp.float32, -limc, limc), 'w2': jax.random.uniform(ks[4], (D_MODEL, D_HIDDEN), jnp.float32, -lim2, lim2)}
    _L0_ffn_all = _L0_ffn_setup()
    _L0_ffn_in = {k: v for k, v in _L0_ffn_all.items() if k in ('w1', 'conv_w', 'conv_b', 'w2')}
    del _L0_ffn_all
    return {'x': x, 'ctx_768': ctx_768, 'mask_BxS_bf1': mask_BxS_bf1, 'mask_BxS2_bf1': mask_BxS2_bf1, 'L0_attn_W_attn': _L0_attn_in['W_attn'], 'L0_attn_b_attn': _L0_attn_in['b_attn'], 'L0_attn_W_proj': _L0_attn_in['W_proj'], 'L0_attn_b_proj': _L0_attn_in['b_proj'], 'L0_xattn_Wq': _L0_xattn_in['Wq'], 'L0_xattn_Wk': _L0_xattn_in['Wk'], 'L0_xattn_Wv': _L0_xattn_in['Wv'], 'L0_xattn_W_film_in': _L0_xattn_in['W_film_in'], 'L0_xattn_b_film_in': _L0_xattn_in['b_film_in'], 'L0_xattn_W_film_out': _L0_xattn_in['W_film_out'], 'L0_xattn_b_film_out': _L0_xattn_in['b_film_out'], 'L0_xattn_g_norm_in': _L0_xattn_in['g_norm_in'], 'L0_xattn_b_norm_in': _L0_xattn_in['b_norm_in'], 'L0_xattn_g_norm_out': _L0_xattn_in['g_norm_out'], 'L0_xattn_b_norm_out': _L0_xattn_in['b_norm_out'], 'L0_xattn_g_ffn': _L0_xattn_in['g_ffn'], 'L0_xattn_b_ffn': _L0_xattn_in['b_ffn'], 'L0_xattn_W1': _L0_xattn_in['W1'], 'L0_xattn_b1': _L0_xattn_in['b1'], 'L0_xattn_W2': _L0_xattn_in['W2'], 'L0_xattn_b2': _L0_xattn_in['b2'], 'L0_xattn_log_dt': _L0_xattn_in['log_dt'], 'L0_xattn_A_re': _L0_xattn_in['A_re'], 'L0_xattn_A_im': _L0_xattn_in['A_im'], 'L0_xattn_C_re': _L0_xattn_in['C_re'], 'L0_xattn_C_im': _L0_xattn_in['C_im'], 'L0_xattn_D_skip': _L0_xattn_in['D_skip'], 'L0_xattn_mod_gate': _L0_xattn_in['mod_gate'], 'L0_ffn_w1': _L0_ffn_in['w1'], 'L0_ffn_conv_w': _L0_ffn_in['conv_w'], 'L0_ffn_conv_b': _L0_ffn_in['conv_b'], 'L0_ffn_w2': _L0_ffn_in['w2']}

def reference(x, ctx_768, mask_BxS_bf1, mask_BxS2_bf1, L0_attn_W_attn, L0_attn_b_attn, L0_attn_W_proj, L0_attn_b_proj, L0_xattn_Wq, L0_xattn_Wk, L0_xattn_Wv, L0_xattn_W_film_in, L0_xattn_b_film_in, L0_xattn_W_film_out, L0_xattn_b_film_out, L0_xattn_g_norm_in, L0_xattn_b_norm_in, L0_xattn_g_norm_out, L0_xattn_b_norm_out, L0_xattn_g_ffn, L0_xattn_b_ffn, L0_xattn_W1, L0_xattn_b1, L0_xattn_W2, L0_xattn_b2, L0_xattn_log_dt, L0_xattn_A_re, L0_xattn_A_im, L0_xattn_C_re, L0_xattn_C_im, L0_xattn_D_skip, L0_xattn_mod_gate, L0_ffn_w1, L0_ffn_conv_w, L0_ffn_conv_b, L0_ffn_w2):
    import jax
    import jax.numpy as jnp

    def _L0_attn_ref(x, W_attn, b_attn, W_proj, b_proj):
        import jax, jax.numpy as jnp
        import numpy as np
        from jax import lax
        N_EMBD = 512
        N_HEAD = 16
        HEAD_DIM = N_EMBD // N_HEAD
        EPS = 1e-06
        B, T = (4, 1024)

        def _feature_map(x):
            return jax.nn.elu(x) + 1.0
        Bb, Tt, C = x.shape
        qkv = x @ W_attn + b_attn
        q, k, v = jnp.split(qkv, 3, axis=-1)

        def to_heads(t):
            return t.reshape(Bb, Tt, N_HEAD, HEAD_DIM).transpose(1, 0, 2, 3)
        q = _feature_map(to_heads(q))
        k = _feature_map(to_heads(k))
        v = to_heads(v)

        def step(carry, inp):
            kv, ksum = carry
            qt, kt, vt = inp
            kv = kv + kt[..., :, None] * vt[..., None, :]
            ksum = ksum + kt
            num = jnp.einsum('bhi,bhij->bhj', qt, kv)
            den = jnp.einsum('bhi,bhi->bh', qt, ksum)[..., None] + EPS
            return ((kv, ksum), num / den)
        init = (jnp.zeros((Bb, N_HEAD, HEAD_DIM, HEAD_DIM), x.dtype), jnp.zeros((Bb, N_HEAD, HEAD_DIM), x.dtype))
        _, y = lax.scan(step, init, (q, k, v))
        y = y.transpose(1, 0, 2, 3).reshape(Bb, Tt, C)
        return y @ W_proj + b_proj

    def _L0_xattn_ref(x_text, x_vision, text_mask, vision_mask, Wq, Wk, Wv, W_film_in, b_film_in, W_film_out, b_film_out, g_norm_in, b_norm_in, g_norm_out, b_norm_out, g_ffn, b_ffn, W1, b1, W2, b2, log_dt, A_re, A_im, C_re, C_im, D_skip, mod_gate):
        import jax, jax.numpy as jnp
        import numpy as np
        B, T, DT, G, DV = (16, 256, 512, 288, 384)
        H, DH = (4, 32)
        INNER = H * DH
        HID = 4 * DT
        N_STATE = 64
        K_TOP = 32

        def layernorm(x, g, b, eps=1e-05):
            m = x.mean(-1, keepdims=True)
            v = x.var(-1, keepdims=True)
            return (x - m) * jax.lax.rsqrt(v + eps) * g + b

        def s4d(x, log_dt, A_re, A_im, C_re, C_im, D_skip):
            Bb, L, D = x.shape
            dt = jnp.exp(log_dt)
            A = A_re + 1j * A_im
            C = C_re + 1j * C_im
            dtA = dt[:, None] * A
            dC = C * (jnp.exp(dtA) - 1.0) / A
            powers = jnp.exp(dtA[:, :, None] * jnp.arange(L))
            K = 2.0 * jnp.einsum('dn,dnl->dl', dC, powers).real
            n = 2 * L
            Kf = jnp.fft.rfft(K, n=n, axis=-1)
            xf = jnp.fft.rfft(x, n=n, axis=1)
            y = jnp.fft.irfft(xf * Kf.T[None], n=n, axis=1)[:, :L]
            return y + x * D_skip
        Bb, Tt, D = x_text.shape
        Gg = x_vision.shape[1]
        Q = (x_text @ Wq).reshape(Bb, Tt, H, DH)
        K = (x_vision @ Wk).reshape(Bb, Gg, H, DH)
        scores = jnp.einsum('bthd,bghd->bhtg', Q, K) / np.sqrt(DH).astype(np.float32)
        scores = jnp.where(vision_mask[:, None, None, :], scores, -jnp.inf)
        topv, topi = jax.lax.top_k(scores, K_TOP)
        probs = jax.nn.softmax(topv, axis=-1)
        bi = jnp.arange(Bb)[:, None, None, None]
        hi = jnp.arange(H)[None, :, None, None]
        ti = jnp.arange(Tt)[None, None, :, None]
        attn = jnp.zeros_like(scores).at[bi, hi, ti, topi].set(probs)
        attn_mean = attn.mean(axis=1)
        V = x_vision @ Wv
        c_t = jnp.einsum('btg,bgd->btd', attn_mean, V)
        c_t = c_t * text_mask[..., None]
        x = layernorm(x_text, g_norm_in, b_norm_in)
        scale_in, shift_in = jnp.split(c_t @ W_film_in + b_film_in, 2, axis=-1)
        x = x * (1.0 + mod_gate * scale_in) + mod_gate * shift_in
        y = s4d(x, log_dt, A_re, A_im, C_re, C_im, D_skip)
        scale_out, shift_out = jnp.split(c_t @ W_film_out + b_film_out, 2, axis=-1)
        y = y * (1.0 + mod_gate * scale_out) + mod_gate * shift_out
        xt = x_text + y
        h = layernorm(xt, g_ffn, b_ffn)
        h = jax.nn.gelu(h @ W1 + b1, approximate=False) @ W2 + b2
        xt = xt + h
        return layernorm(xt, g_norm_out, b_norm_out)

    def _L0_ffn_ref(x, w1, conv_w, conv_b, w2):
        import jax, jax.numpy as jnp
        import numpy as np
        B, S, D_MODEL, D_HIDDEN = (4, 1024, 512, 2048)

        def act_quant(x):
            scale = 127.0 / jnp.clip(jnp.max(jnp.abs(x), axis=-1, keepdims=True), 1e-05)
            return jnp.clip(jnp.round(x * scale), -128, 127) / scale

        def weight_quant(w):
            scale = 1.0 / jnp.clip(jnp.mean(jnp.abs(w)), 1e-05)
            return jnp.clip(jnp.round(w * scale), -1, 1) / scale

        def bit_linear(x, w):
            xq = x + jax.lax.stop_gradient(act_quant(x) - x)
            wq = w + jax.lax.stop_gradient(weight_quant(w) - w)
            return jnp.einsum('bsd,hd->bsh', xq, wq)

        def depthwise_conv1d(x_bcl, w, b):
            y = jax.lax.conv_general_dilated(x_bcl, w, window_strides=(1,), padding=[(1, 1)], dimension_numbers=('NCH', 'OIH', 'NCH'), feature_group_count=x_bcl.shape[1])
            return y + b[None, :, None]
        h = bit_linear(x, w1)
        h = depthwise_conv1d(h.transpose(0, 2, 1), conv_w, conv_b)
        h = h.transpose(0, 2, 1)
        h = jax.nn.silu(h)
        return bit_linear(h, w2)
    x = _layernorm(x + _L0_attn_ref(x, L0_attn_W_attn, L0_attn_b_attn, L0_attn_W_proj, L0_attn_b_proj), axis=-1)
    x = _layernorm(x + _L0_xattn_ref(x, ctx_768, mask_BxS_bf1, mask_BxS2_bf1, L0_xattn_Wq, L0_xattn_Wk, L0_xattn_Wv, L0_xattn_W_film_in, L0_xattn_b_film_in, L0_xattn_W_film_out, L0_xattn_b_film_out, L0_xattn_g_norm_in, L0_xattn_b_norm_in, L0_xattn_g_norm_out, L0_xattn_b_norm_out, L0_xattn_g_ffn, L0_xattn_b_ffn, L0_xattn_W1, L0_xattn_b1, L0_xattn_W2, L0_xattn_b2, L0_xattn_log_dt, L0_xattn_A_re, L0_xattn_A_im, L0_xattn_C_re, L0_xattn_C_im, L0_xattn_D_skip, L0_xattn_mod_gate), axis=-1)
    x = _layernorm(x + _L0_ffn_ref(x, L0_ffn_w1, L0_ffn_conv_w, L0_ffn_conv_b, L0_ffn_w2), axis=-1)
    return x

_drawn_inputs = setup_inputs


def setup_inputs(seed=0):
    import zlib

    import numpy as np

    out = dict(_drawn_inputs(seed))
    spreads = {'L0_xattn_b_film_in': (0.0, 0.1),
     'L0_xattn_b_film_out': (0.0, 0.279),
     'L0_xattn_g_norm_in': (1.0, 0.2),
     'L0_xattn_b_norm_in': (0.0, 0.1),
     'L0_xattn_g_norm_out': (1.0, 0.2),
     'L0_xattn_b_norm_out': (0.0, 0.1),
     'L0_xattn_g_ffn': (1.0, 0.6),
     'L0_xattn_b_ffn': (0.0, 0.8),
     'L0_xattn_b1': (0.0, 0.516),
     'L0_xattn_b2': (0.0, 0.281),
     'L0_xattn_A_re': (-0.5, 0.2)}
    factors = {'L0_attn_b_attn': 4.903, 'L0_attn_b_proj': 4.989}
    for name, (base, spread) in spreads.items():
        noise = np.random.default_rng([zlib.crc32(name.encode()), seed]).standard_normal(out[name].shape)
        drawn = base * np.exp(spread * noise) if base else spread * noise
        out[name] = jnp.asarray(drawn.astype(out[name].dtype))
    for name, factor in factors.items():
        out[name] = (out[name] * factor).astype(out[name].dtype)
    return out
```

```python
import math
from contextlib import ExitStack

import concourse.bass as bass
import numpy as np
from concourse import mybir

ALU = mybir.AluOpType
ACT = mybir.ActivationFunctionType
AX = mybir.AxisListType
F32 = mybir.dt.float32
BF16 = mybir.dt.bfloat16
U8 = mybir.dt.uint8

P = 128
B, S, D = 4, 1024, 512
TOK = B * S
CH = S // P
KD = D // P
H, DH = 16, 32
G = H // 4
VW = DH + 1
LN_EPS = 1e-5


class Steps:

    def __init__(self, eng, sem, base):
        self.eng, self.sem, self.base, self.n = eng, sem, base, 0

    def mark(self, ins):
        self.n += 1
        ins.then_inc(self.sem, 1)

    def wait(self):
        self.eng.wait_ge(self.sem, self.base + self.n)

    def link(self, ins):
        self.mark(ins)
        self.wait()


def stand(eng, passed):
    eng.sem_inc(passed, 1)


class Alloc:

    def __init__(self, nc, ctx, tag):
        self.nc, self.ctx, self.tag, self.sems = nc, ctx, tag, []
        ctx.callback(self.finish)

    def sb(self, name, shape, dt=F32):
        return self.ctx.enter_context(self.nc.sbuf_tensor(self.tag + name, shape, dt))

    def ps(self, name, shape, dt=F32):
        return self.ctx.enter_context(self.nc.psum_tensor(self.tag + name, shape, dt))

    def sem(self, name):
        self.sems.append(self.nc.alloc_semaphore(self.tag + name))
        return self.sems[-1]

    def finish(self):
        self.nc.clear_and_free_semaphores(self.sems)
        self.nc.all_engine_barrier()

    def store_sem(self, name):
        return self.nc.alloc_semaphore(self.tag + name)


def rows(ap, t):
    return ap[bass.ds(t * P, P), :]


def attention(nc, x, xT, W_attn, b_attn, W_proj, b_proj, tri, blockdiag, eye, x1):
    with ExitStack() as ctx:
        m = Alloc(nc, ctx, "a_")
        w = m.sb("w", [P, KD, 3 * D])
        wp = m.sb("wp", [P, KD, D])
        ba = m.sb("ba", [1, 3 * D])
        bp = m.sb("bp", [1, D])
        trib = m.sb("trib", [P, P])
        bd = m.sb("bd", [P, 4 * VW])
        ident = m.sb("ident", [P, P])
        ones = m.sb("ones", [1, P])
        eps = m.sb("eps", [P, 1])
        xt = m.sb("xt", [P, 2, KD, P])
        xr = m.sb("xr", [P, 2, D])
        neg = m.sb("neg", [P, 8, P])
        ex = m.sb("ex", [P, 8, P])
        phi = m.sb("phi", [P, 8, P])
        kk = m.sb("kk", [P, D])
        vv = m.sb("vv", [P, H, VW])
        am = m.sb("am", [P, 4, 4, P])
        kv = m.sb("kv", [P, G, 4 * VW])
        kvn = m.sb("kvn", [P, G, 4 * VW])
        den = m.sb("den", [P, H])
        y = m.sb("y", [P, D])
        yT = m.sb("yT", [P, KD, P])
        res = m.sb("res", [P, D])
        stats = m.sb("stats", [P, 6])
        mv = m.sb("mv", [P, 2])
        std = m.sb("std", [P, 1])
        rstd = m.sb("rstd", [P, 1])
        out = m.sb("out", [P, 2, D])
        p_z = m.ps("p_z", [P, 8, P])
        p_v = m.ps("p_v", [P, D])
        p_k = m.ps("p_k", [P, D])
        p_a = m.ps("p_a", [P, 4, 4, P])
        p_n = p_z[:, :, :].rearrange("p a b -> p (a b)").rearrange("p (u n) -> p u n", u=2)
        p_kv = p_a[:, 0:2, :, :].rearrange("p a b c -> p a (b c)")
        p_yT = p_v
        p_o = p_k

        (weights_in, consts, z_done, neg_done, exp_done, phi_done, v_done, v_copied, kT_done, k_copied,
         a_done, a_masked, num_done, y_ready, kv_done, kv_ready, kv_clear, yT_done, yT_copied, o_done,
         var_ready, std_ready, out_ready, dve_step, passed) = [
            m.sem(n) for n in (
                "weights_in consts z_done neg_done exp_done phi_done v_done v_copied kT_done k_copied "
                "a_done a_masked num_done y_ready kv_done kv_ready kv_clear yT_done yT_copied o_done "
                "var_ready std_ready out_ready dve_step passed").split()]
        x_in = [m.sem(f"x_in{u}") for u in range(2)]
        x1_out = [m.store_sem(f"x1_out{u}") for u in range(2)]
        PAIRS = TOK // P // 2
        block = ctx.enter_context(nc.Block())

        @block.sync
        def _(sp):
            def load(u, col):
                sp.dma_start(xt[:, u], xT.rearrange("(k p) n -> p k n", p=P)[:, :, bass.ds(col, P)]).then_inc(x_in[u], 16)
                sp.dma_start(xr[:, u, :], x[bass.ds(col, P), :]).then_inc(x_in[u], 16)

            for u in range(2):
                load(u, u * P)
            for dst, src in ((w[:], W_attn.rearrange("(k p) n -> p k n", p=P)),
                             (wp[:], W_proj.rearrange("(k p) n -> p k n", p=P)),
                             (ba[:], b_attn.rearrange("(a n) -> a n", a=1)),
                             (bp[:], b_proj.rearrange("(a n) -> a n", a=1)),
                             (trib[:], tri), (bd[:], blockdiag), (ident[:], eye)):
                sp.dma_start(dst, src).then_inc(weights_in, 16)
            with sp.Fori(0, PAIRS - 1) as i:
                for u in range(2):
                    done = sp.snap(i * 2 + (u + 1))
                    col = sp.snap(i * (2 * P) + (u + 2) * P)
                    sp.wait_ge(var_ready, done)
                    load(u, col)

        @block.gpsimd
        def _(pool):
            pool.memset(ones[:], 1.0).then_inc(consts, 1)
            pool.memset(eps[:], LN_EPS).then_inc(consts, 1)
            pool.memset(vv[:], 1.0).then_inc(consts, 1)
            with pool.Fori(0, PAIRS) as i:
                for u in range(2):
                    pool.wait_ge(out_ready, i * 2 + (u + 1))
                    pool.dma_start(x1[bass.ds(i * (2 * P) + u * P, P), :], out[:, u, :]).then_inc(x1_out[u], 16)
            for u in range(2):
                pool.wait_ge(x1_out[u], 16 * PAIRS)

        @block.tensor
        def _(pe):
            pe.wait_ge(weights_in, 16 * 7)
            pe.wait_ge(consts, 3)
            mm = nc.tensor.matmul

            def tile(b, i, u):
                t = i * 2 + u
                pe.wait_ge(x_in[u], i * 32 + 32)
                pe.wait_ge(y_ready, t)
                for f in range(8):
                    for k in range(KD):
                        mm(p_z[:, f, :], w[:, k, f * P:(f + 1) * P], xt[:, u, k, :],
                           start=(f % 4 == 0 and k == 0), stop=False, skip_group_check=True)
                    last = mm(p_z[:, f, :], ba[:, f * P:(f + 1) * P], ones[:], start=False,
                              stop=(f % 4 == 3), skip_group_check=True)
                last.then_inc(z_done, 1)
                pe.wait_ge(yT_copied, t)
                for k in range(KD):
                    mm(p_v[:], xt[:, u, k, :], w[:, k, 2 * D:], start=(k == 0), stop=False)
                mm(p_v[:], ones[:], ba[:, 2 * D:], start=False, stop=True).then_inc(v_done, 1)
                pe.wait_ge(phi_done, t + 1)
                pe.wait_ge(var_ready, t)
                for g in range(G):
                    last = nc.tensor.transpose(p_k[:, g * P:(g + 1) * P], phi[:, 4 + g, :], ident[:])
                last.then_inc(kT_done, 1)
                pe.wait_ge(kv_ready, t)
                for g in range(G):
                    for r in range(4):
                        last = mm(p_a[:, r, g, :], phi[32 * r:32 * r + 32, 4 + g, :],
                                  phi[32 * r:32 * r + 32, g, :], start=True, stop=True,
                                  skip_group_check=True)
                last.then_inc(a_done, 1)
                pe.wait_ge(kv_clear, b + 1)
                for g in range(G):
                    mm(p_n[:, g // 2, (g % 2) * 4 * VW:(g % 2 + 1) * 4 * VW], phi[:, g, :], kv[:, g, :],
                       start=(g % 2 == 0), stop=False, skip_group_check=True)
                pe.wait_ge(v_copied, t + 1)
                pe.wait_ge(a_masked, t + 1)
                for h in range(H):
                    last = mm(p_n[:, h // 8, (h % 8) * VW:(h % 8 + 1) * VW], am[:, h % 4, h // 4, :],
                              vv[:, h, :], start=False, stop=(h % 8 == 7), skip_group_check=True)
                last.then_inc(num_done, 1)
                pe.wait_ge(k_copied, t + 1)
                for g in range(G):
                    last = mm(p_kv[:, g // 2, (g % 2) * 4 * VW:(g % 2 + 1) * 4 * VW],
                              kk[:, g * P:(g + 1) * P], vv[:, 4 * g:4 * g + 4, :],
                              start=(g % 2 == 0), stop=(g % 2 == 1), skip_group_check=True)
                last.then_inc(kv_done, 1)
                pe.wait_ge(y_ready, t + 1)
                for g in range(KD):
                    last = nc.tensor.transpose(p_yT[:, g * P:(g + 1) * P], y[:, g * P:(g + 1) * P], ident[:])
                last.then_inc(yT_done, 1)
                pe.wait_ge(yT_copied, t + 1)
                for k in range(KD):
                    mm(p_o[:], yT[:, k, :], wp[:, k, :], start=(k == 0), stop=False)
                mm(p_o[:], ones[:], bp[:], start=False, stop=True).then_inc(o_done, 1)

            with pe.Fori(0, B) as b:
                with pe.Fori(0, CH // 2) as c:
                    for u in range(2):
                        tile(b, b * (CH // 2) + c, u)

        @block.scalar
        def _(act):
            act.wait_ge(consts, 3)
            with act.Fori(0, TOK // P) as t:
                act.wait_ge(neg_done, t + 1)
                nc.scalar.activation(ex[:], neg[:], ACT.Exp).then_inc(exp_done, 1)
                act.wait_ge(v_done, t + 1)
                act.wait_ge(kv_done, t)
                nc.scalar.activation(vv[:, :, 0:DH], p_v[:].rearrange("p (h d) -> p h d", h=H),
                                     ACT.Copy).then_inc(v_copied, 1)
                act.wait_ge(kT_done, t + 1)
                nc.scalar.activation(kk[:], p_k[:], ACT.Copy).then_inc(k_copied, 1)
                act.wait_ge(yT_done, t + 1)
                act.wait_ge(o_done, t)
                nc.scalar.activation(yT[:].rearrange("p a b -> p (a b)"), p_yT[:], ACT.Copy).then_inc(yT_copied, 1)
                act.wait_ge(var_ready, t + 1)
                nc.scalar.activation(std[:], mv[:, 1:2], ACT.Sqrt, bias=eps[:]).then_inc(std_ready, 1)

        @block.vector
        def _(dve):
            v = nc.vector
            dve.wait_ge(weights_in, 16 * 7)
            dve.wait_ge(consts, 3)
            NSTEP = 8

            def tile(i, u):
                t = i * 2 + u
                s = Steps(dve, dve_step, t * NSTEP)
                dve.wait_ge(z_done, t + 1)
                v.tensor_scalar(neg[:], p_z[:], 0.0, None, ALU.min).then_inc(neg_done, 1)
                dve.wait_ge(exp_done, t + 1)
                v.scalar_tensor_tensor(phi[:], p_z[:], 0.0, ex[:], ALU.max, ALU.add).then_inc(phi_done, 1)
                dve.wait_ge(a_done, t + 1)
                v.tensor_tensor(am[:].rearrange("p a b c -> p (a b) c"),
                                p_a[:].rearrange("p a b c -> p (a b) c"),
                                trib[:].unsqueeze(1).to_broadcast([P, 16, P]),
                                ALU.mult).then_inc(a_masked, 1)
                dve.wait_ge(num_done, t + 1)
                nd = p_n[:, :, 0:8 * VW].rearrange("p u (h e) -> p u h e", e=VW)
                dv = den[:].rearrange("p (u h) -> p u h", u=2)
                s.link(v.tensor_scalar(dv, nd[:, :, :, DH], 1e-6, None, ALU.add))
                s.link(v.reciprocal(den[:], den[:]))
                for q in range(2):
                    last = v.tensor_tensor(y[:, 256 * q:256 * q + 256].rearrange("p (h d) -> p h d", d=DH),
                                           nd[:, q, :, 0:DH],
                                           den[:, 8 * q:8 * q + 8].unsqueeze(2).to_broadcast([P, 8, DH]), ALU.mult)
                    if q == 0:
                        s.link(last)
                last.then_inc(y_ready, 1)
                dve.wait_ge(kv_done, t + 1)
                for q in range(2):
                    s.link(v.tensor_tensor(kvn[:, 2 * q:2 * q + 2, :],
                                           p_kv[:, q, 0:8 * VW].rearrange("p (a b) -> p a b", a=2),
                                           bd[:].unsqueeze(1).to_broadcast([P, 2, 4 * VW]), ALU.mult))
                v.tensor_tensor(kv[:], kv[:], kvn[:], ALU.add).then_inc(kv_ready, 1)
                dve.wait_ge(o_done, t + 1)
                s.link(v.tensor_tensor(res[:], p_o[:], xr[:, u, :], ALU.add))
                s.link(v.bn_stats(stats[:], res[:]))
                stand(dve, passed)
                v.bn_aggr(mv[:], stats[:]).then_inc(var_ready, 1)
                dve.wait_ge(std_ready, t + 1)
                s.link(v.reciprocal(rstd[:], std[:]))
                dve.wait_ge(x1_out[u], i * 16)
                v.tensor_scalar(out[:, u, :], res[:], mv[:, 0:1], rstd[:], ALU.subtract,
                                ALU.mult).then_inc(out_ready, 1)
                dve.wait_ge(out_ready, t + 1)
                dve.wait_ge(kv_ready, t + 1)
                assert s.n == NSTEP, s.n

            with dve.Fori(0, B) as b:
                v.memset(kv[:], 0.0).then_inc(kv_clear, 1)
                dve.wait_ge(kv_clear, b + 1)
                stand(dve, passed)
                with dve.Fori(0, CH // 2) as c:
                    for u in range(2):
                        tile(b * (CH // 2) + c, u)


N2, DV, NH2 = 2048, 384, 4
KV3 = DV // P
HS = P // NH2
GB = N2 // P
NEG = -3.0e38


def at_least(eng, sem, count):
    if isinstance(count, int) and count <= 0:
        return
    eng.wait_ge(sem, count)


def prepare(nc, ctxT, Wk, WvT, W_film_in, b_film_in, W_film_out, b_film_out, gate, mask2, keysT, film_w, film_b, mask_row):
    with ExitStack() as ctx:
        m = Alloc(nc, ctx, "p_")
        wk = m.sb("wk", [P, KV3, P])
        ct = m.sb("ct", [P, 2, KV3, 512])
        ko = m.sb("ko", [P, 2, 512])
        wv = m.sb("wv", [P, KD, DV])
        wf = m.sb("wf", [P, KD, 4 * D])
        fo = m.sb("fo", [P, KV3, 4 * D])
        g = m.sb("g", [P, 1])
        fb = m.sb("fb", [1, 4 * D])
        m8 = m.sb("m8", [B, N2], U8)
        mf = m.sb("mf", [B, N2])
        mb = m.sb("mb", [B, N2], BF16)
        p_k = m.ps("p_k", [P, 2, 512])
        p_f = m.ps("p_f", [P, 2, 512])
        weights_in, k_done, k_copied, f_done, f_copied, m_step = [
            m.sem(n) for n in "weights_in k_done k_copied f_done f_copied m_step".split()]
        stored = m.store_sem("stored")
        c_in = [m.sem(f"c_in{u}") for u in range(2)]
        k_out = [m.store_sem(f"k_out{u}") for u in range(2)]
        NC = B * N2 // 512
        block = ctx.enter_context(nc.Block())

        @block.sync
        def _(sp):
            src = ctxT.rearrange("(k p) n -> p k n", p=P)
            sp.dma_start(wk[:], Wk.rearrange("(k p) n -> p k n", p=P)).then_inc(weights_in, 16)
            for u in range(2):
                sp.dma_start(ct[:, u], src[:, :, 512 * u:512 * u + 512]).then_inc(c_in[u], 16)
            sp.dma_start(wv[:], WvT.rearrange("(k p) n -> p k n", p=P)).then_inc(weights_in, 16)
            sp.dma_start(wf[:, :, 0:2 * D], W_film_in.rearrange("(k p) n -> p k n", p=P)).then_inc(weights_in, 16)
            sp.dma_start(wf[:, :, 2 * D:], W_film_out.rearrange("(k p) n -> p k n", p=P)).then_inc(weights_in, 16)
            sp.dma_start(g[:], gate.to_broadcast([P, 1])).then_inc(weights_in, 16)
            sp.dma_start(fb[:, 0:2 * D], b_film_in.rearrange("(a n) -> a n", a=1)).then_inc(weights_in, 16)
            sp.dma_start(fb[:, 2 * D:], b_film_out.rearrange("(a n) -> a n", a=1)).then_inc(weights_in, 16)
            sp.dma_start(m8[:], mask2).then_inc(weights_in, 16)
            with sp.Fori(0, NC // 2 - 1) as i:
                for u in range(2):
                    done = sp.snap(i * 2 + (u + 1))
                    col = sp.snap(i * 1024 + (u + 2) * 512)
                    sp.wait_ge(k_done, done)
                    sp.dma_start(ct[:, u], src[:, :, bass.ds(col, 512)]).then_inc(c_in[u], 16)

        @block.gpsimd
        def _(pool):
            with pool.Fori(0, NC // 2) as i:
                for u in range(2):
                    pool.wait_ge(k_copied, i * 2 + (u + 1))
                    pool.dma_start(keysT[:, bass.ds(i * 1024 + u * 512, 512)], ko[:, u, :]).then_inc(k_out[u], 16)
            pool.wait_ge(m_step, 4)
            pool.dma_start(film_b, fb[:]).then_inc(stored, 16)
            pool.dma_start(mask_row, mb[:]).then_inc(stored, 16)
            pool.wait_ge(f_copied, 12)
            pool.dma_start(film_w.rearrange("(k p) n -> p k n", p=P), fo[:]).then_inc(stored, 16)
            pool.wait_ge(stored, 48)
            for u in range(2):
                pool.wait_ge(k_out[u], 16 * (NC // 2))

        @block.tensor
        def _(pe):
            mm = nc.tensor.matmul
            pe.wait_ge(weights_in, 128)
            with pe.Fori(0, NC // 2) as i:
                for u in range(2):
                    pe.wait_ge(c_in[u], i * 16 + 16)
                    pe.wait_ge(k_copied, i * 2)
                    for k in range(KV3):
                        last = mm(p_k[:, u, :], wk[:, k, :], ct[:, u, k, :], start=(k == 0), stop=(k == KV3 - 1))
                    last.then_inc(k_done, 1)
            for n in range(12):
                r, c = n // 4, n % 4
                at_least(pe, f_copied, n - 1)
                for k in range(KD):
                    last = mm(p_f[:, n % 2, :], wv[:, k, r * P:(r + 1) * P], wf[:, k, c * 512:(c + 1) * 512],
                              start=(k == 0), stop=(k == KD - 1))
                last.then_inc(f_done, 1)

        @block.scalar
        def _(act):
            with act.Fori(0, NC // 2) as i:
                for u in range(2):
                    act.wait_ge(k_done, i * 2 + (u + 1))
                    act.wait_ge(k_out[u], i * 16)
                    nc.scalar.activation(ko[:, u, :], p_k[:, u, :], ACT.Copy).then_inc(k_copied, 1)

        @block.vector
        def _(dve):
            v = nc.vector
            dve.wait_ge(weights_in, 128)
            v.tensor_scalar(fb[:], fb[:], g[0:1, :], None, ALU.mult).then_inc(m_step, 1)
            v.tensor_copy(mf[:], m8[:]).then_inc(m_step, 1)
            dve.wait_ge(m_step, 2)
            v.tensor_scalar(mf[:], mf[:], -1.0, 3e38, ALU.add, ALU.mult).then_inc(m_step, 1)
            dve.wait_ge(m_step, 3)
            v.tensor_scalar(mb[:], mf[:], 10.0, None, ALU.mult).then_inc(m_step, 1)
            for n in range(12):
                dve.wait_ge(f_done, n + 1)
                v.tensor_scalar(fo[:, n // 4, (n % 4) * 512:(n % 4 + 1) * 512], p_f[:, n % 2, :], g[:], None,
                                ALU.mult).then_inc(f_copied, 1)


def cross(nc, x1, keysT, values, film_w, film_b, mask_row, text_mask, Wq, g_in, b_in, eye, xm, mod_out):
    with ExitStack() as ctx:
        m = Alloc(nc, ctx, "c_")
        SCALE = float(HS) ** -0.5
        wq = m.sb("wq", [P, KD, P])
        kt = m.sb("kt", [P, N2])
        vals = m.sb("vals", [P, GB, DV])
        wf = m.sb("wf", [P, KV3, 4 * D])
        fb = m.sb("fb", [1, 4 * D])
        mrow = m.sb("mrow", [P, N2], BF16)
        oneb = m.sb("oneb", [P, P], BF16)
        ones = m.sb("ones", [1, P])
        eps = m.sb("eps", [P, 1])
        tm8 = m.sb("tm8", [P, TOK // P], U8)
        tm = m.sb("tm", [P, TOK // P])
        gb = m.sb("gb", [P, 2, D])
        ident = m.sb("ident", [P, P])
        xt = m.sb("xt", [P, 2, D])
        xT = m.sb("xT", [P, D])
        qT = m.sb("qT", [P, P])
        s = m.sb("s", [P, 2, N2])
        z = m.sb("z", [P, 2, N2])
        e = m.sb("e", [P, 2, N2])
        ez = m.sb("ez", [P, N2])
        top = m.sb("top", [P, 2, 32])
        topx = m.sb("topx", [P, 32])
        nb = m.sb("nb", [P, 2])
        den = m.sb("den", [P, 2])
        rd = m.sb("rd", [P, 1])
        diag = m.sb("diag", [P, 2, P])
        aT = m.sb("aT", [P, GB, P])
        uT = m.sb("uT", [P, KV3, P])
        fi = m.sb("fi", [P, 2, D])
        fo = m.sb("fo", [P, 2, 2 * D])
        xl = m.sb("xl", [P, D])
        xo = m.sb("xo", [P, 2, D])
        stats = m.sb("stats", [P, 6])
        mv = m.sb("mv", [P, 2])
        std = m.sb("std", [P, 1])
        rstd = m.sb("rstd", [P, 1])
        p_s = m.ps("p_s", [P, 2, 512])
        p_a = m.ps("p_a", [P, GB, P])
        p_m = m.ps("p_m", [P, 2, 512])

        (weights_in, consts, keys_in, values_in, s_done, s_copied, s_read, nb_ready, z_done, e_done, ez_done,
         sum_done, w_ready, diag_ready, attn_done, aT_copied, uT_done, uT_copied, xT_done, xT_copied,
         q_done, q_copied, fi_done, fi_copied, fo_done, fo_copied, var_ready, std_ready, ln_done,
         xm_ready, passed, dve_step, pool_step) = [
            m.sem(n) for n in (
                "weights_in consts keys_in values_in s_done s_copied s_read nb_ready z_done e_done ez_done "
                "sum_done w_ready diag_ready attn_done aT_copied uT_done uT_copied xT_done xT_copied "
                "q_done q_copied fi_done fi_copied fo_done fo_copied var_ready std_ready ln_done "
                "xm_ready passed dve_step pool_step").split()]
        x_in = [m.sem(f"x_in{u}") for u in range(2)]
        fo_out = [m.store_sem(f"fo_out{u}") for u in range(2)]
        xm_out = [m.store_sem(f"xm_out{u}") for u in range(2)]
        TILES = TOK // P
        PAIRS = TILES // 2
        block = ctx.enter_context(nc.Block())

        def pairs(eng, pair):
            pair(0)
            with eng.Fori(1, PAIRS - 1) as i:
                pair(i)
            pair(PAIRS - 1)

        @block.sync
        def _(sp):
            def bc(ap, n):
                return ap.rearrange("(a n) -> a n", a=1).to_broadcast([P, n])
            for dst, src in ((wq[:], Wq.rearrange("(k p) n -> p k n", p=P)),
                             (wf[:], film_w.rearrange("(k p) n -> p k n", p=P)), (fb[:], film_b),
                             (tm8[:], text_mask), (gb[:, 0, :], bc(g_in, D)), (gb[:, 1, :], bc(b_in, D)),
                             (ident[:], eye)):
                sp.dma_start(dst, src).then_inc(weights_in, 16)
            vsrc = values.rearrange("(b j p) n -> b p j n", p=P, j=GB)

            def load_x(u, free, row):
                at_least(sp, ln_done, free)
                sp.dma_start(xt[:, u, :], x1[bass.ds(row, P), :]).then_inc(x_in[u], 16)

            def batch(b):
                snap = (lambda a: a) if isinstance(b, int) else sp.snap
                used, col = snap(b * (CH * NH2 * 4)), snap(b * N2)
                at_least(sp, s_done, used)
                sp.dma_start(kt[:], keysT[:, bass.ds(col, N2)]).then_inc(keys_in, 16)
                for h in range(NH2):
                    sp.dma_start(mrow[HS * h:HS * h + 1, :], mask_row[bass.ds(b, 1), :]).then_inc(keys_in, 16)
                got = snap(b * 80 + 80)
                sp.wait_ge(keys_in, got)
                sp.wait_ge(weights_in, 16 * 7)
                load_x(0, snap(b * CH - 1), snap(b * S))
                used, row = snap(b * CH), snap(b * N2)
                at_least(sp, uT_done, used)
                sp.dma_start(vals[:], vsrc[b] if isinstance(b, int) else vsrc[bass.ds(b, 1)].squeeze(0) ).then_inc(values_in, 16)
                got = snap(b * 16 + 16)
                sp.wait_ge(values_in, got)
                sp.wait_ge(weights_in, 16 * 7)
                load_x(1, snap(b * CH), snap(b * S + P))
                with sp.Fori(1, CH // 2) as c:
                    for u in range(2):
                        load_x(u, sp.snap(c * 2 + (b * CH + (u - 1))), sp.snap(c * (2 * P) + (b * S + u * P)))

            for b in range(B):
                batch(b)

        @block.tensor
        def _(pe):
            mm = nc.tensor.matmul
            pe.wait_ge(weights_in, 16 * 7)
            pe.wait_ge(consts, 4)

            def queries(t, i, u):
                pe.wait_ge(x_in[u], i * 16 + 16)
                at_least(pe, fo_copied, t - 1)
                for k in range(KD):
                    last = nc.tensor.transpose(p_m[:, 0, k * P:(k + 1) * P], xt[:, u, k * P:(k + 1) * P], ident[:])
                last.then_inc(xT_done, 1)
                pe.wait_ge(xT_copied, t + 1)
                for k in range(KD):
                    last = mm(p_m[:, 1, 0:P], wq[:, k, :], xT[:, k * P:(k + 1) * P], start=(k == 0), stop=(k == KD - 1))
                last.then_inc(q_done, 1)
                pe.wait_ge(q_copied, t + 1)

            def scores(j, h):
                for c in range(4):
                    at_least(pe, s_copied, j * 4 + (c - 1))
                    mm(p_s[:, c % 2, :], qT[HS * h:HS * h + HS, :], kt[HS * h:HS * h + HS, c * 512:(c + 1) * 512],
                       start=True, stop=False)
                    mm(p_s[:, c % 2, :], oneb[HS * h:HS * h + 1, :], mrow[HS * h:HS * h + 1, c * 512:(c + 1) * 512],
                       start=False, stop=True).then_inc(s_done, 1)

            def attn(t, j, h):
                pe.wait_ge(diag_ready, j + 1)
                pe.wait_ge(w_ready, j + 1)
                at_least(pe, aT_copied, t)
                for n in range(GB):
                    last = mm(p_a[:, n, :], e[:, h % 2, n * P:(n + 1) * P], diag[:, h % 2, :],
                              start=(h == 0 and n % 4 == 0), stop=(h == NH2 - 1 and n % 4 == 3),
                              skip_group_check=True)
                last.then_inc(attn_done, 1)

            def context(t):
                pe.wait_ge(aT_copied, t + 1)
                for k in range(KV3):
                    for n in range(GB):
                        last = mm(p_m[:, 0, k * P:(k + 1) * P], vals[:, n, k * P:(k + 1) * P], aT[:, n, :],
                                  start=(k == 0 and n == 0), stop=(k == KV3 - 1 and n == GB - 1),
                                  skip_group_check=True)
                last.then_inc(uT_done, 1)

            def film(t, part):
                if part == 0:
                    pe.wait_ge(uT_copied, t + 1)
                else:
                    pe.wait_ge(fi_copied, t + 1)
                for n in range(2):
                    c = 2 * part + n
                    for k in range(KV3):
                        mm(p_m[:, n, :], uT[:, k, :], wf[:, k, c * D:(c + 1) * D], start=(k == 0), stop=False)
                    last = mm(p_m[:, n, :], ones[:], fb[:, c * D:(c + 1) * D], start=False, stop=True)
                last.then_inc(fo_done if part else fi_done, 1)

            def extra(t, h):
                if h == 0:
                    context(t)
                elif h < 3:
                    film(t, h - 1)

            def pair(i):
                for u in range(2):
                    t = i * 2 + u
                    for h in range(NH2):
                        j = t * 4 + h
                        if h < NH2 - 1:
                            scores(j + 1, h + 1)
                        elif not (isinstance(t, int) and t == TILES - 1):
                            queries(t + 1, i + u, 1 - u)
                            scores(j + 1, 0)
                        if not (isinstance(t, int) and t == 0):
                            extra(t - 1, h)
                        attn(t, j, h)

            queries(0, 0, 0)
            scores(0, 0)
            pairs(pe, pair)
            for h in range(3):
                extra(TILES - 1, h)

        @block.scalar
        def _(act):
            a = nc.scalar.activation
            act.wait_ge(consts, 4)

            def copy_q(t):
                act.wait_ge(xT_done, t + 1)
                a(xT[:], p_m[:, 0, :], ACT.Copy).then_inc(xT_copied, 1)
                act.wait_ge(q_done, t + 1)
                a(qT[:], p_m[:, 1, 0:P], ACT.Copy).then_inc(q_copied, 1)

            def copy_s(j, par):
                at_least(act, s_read, j - 1)
                for c in range(4):
                    act.wait_ge(s_done, j * 4 + (c + 1))
                    a(s[:, par, c * 512:(c + 1) * 512], p_s[:, c % 2, :], ACT.Copy).then_inc(s_copied, 1)

            def exps(j, par):
                act.wait_ge(nb_ready, j + 1)
                at_least(act, attn_done, j - 1)
                a(e[:, par, :], s[:, par, :], ACT.Exp, bias=nb[:, par:par + 1], scale=SCALE).then_inc(e_done, 1)
                act.wait_ge(z_done, j + 1)
                at_least(act, w_ready, j)
                a(ez[:], z[:, par, :], ACT.Exp, bias=nb[:, par:par + 1], scale=SCALE).then_inc(ez_done, 1)
                at_least(act, diag_ready, j - 1)
                a(topx[:], top[:, par, :], ACT.Exp, bias=nb[:, par:par + 1], scale=SCALE,
                  accum_out=den[:, par:par + 1]).then_inc(sum_done, 1)

            def extra(t, i, u, h):
                if h == 0:
                    act.wait_ge(uT_done, t + 1)
                    a(uT[:].rearrange("p a b -> p (a b)"), p_m[:, 0, 0:DV], ACT.Copy).then_inc(uT_copied, 1)
                elif h == 1:
                    act.wait_ge(fi_done, t + 1)
                    at_least(act, xm_ready, t)
                    a(fi[:], p_m[:], ACT.Copy).then_inc(fi_copied, 1)
                elif h == 2:
                    act.wait_ge(fo_done, t + 1)
                    at_least(act, fo_out[u], i * 16)
                    a(fo[:, u, :].rearrange("p (a b) -> p a b", a=2), p_m[:], ACT.Copy).then_inc(fo_copied, 1)

            def pair(i):
                for u in range(2):
                    t = i * 2 + u
                    for h in range(NH2):
                        j = t * 4 + h
                        if h < NH2 - 1:
                            copy_s(j + 1, (h + 1) % 2)
                        elif not (isinstance(t, int) and t == TILES - 1):
                            copy_q(t + 1)
                            copy_s(j + 1, 0)
                        exps(j, h % 2)
                        if h == 3:
                            act.wait_ge(attn_done, t * 4 + 4)
                            a(aT[:], p_a[:], ACT.Copy).then_inc(aT_copied, 1)
                        elif not (isinstance(t, int) and t == 0):
                            extra(t - 1, i - (1 - u), 1 - u, h)
                        if h == 2:
                            act.wait_ge(var_ready, t + 1)
                            a(std[:], mv[:, 1:2], ACT.Sqrt, bias=eps[:]).then_inc(std_ready, 1)

            copy_q(0)
            copy_s(0, 0)
            pairs(act, pair)
            for h in range(3):
                extra(TILES - 1, PAIRS - 1, 1, h)

        @block.vector
        def _(dve):
            v = nc.vector
            v.memset(oneb[:], 1.0).then_inc(consts, 1)
            v.memset(ones[:], 1.0).then_inc(consts, 1)
            v.memset(eps[:], LN_EPS).then_inc(consts, 1)
            dve.wait_ge(weights_in, 16 * 7)
            v.tensor_copy(tm[:], tm8[:]).then_inc(consts, 1)
            dve.wait_ge(consts, 4)
            HSTEP = 9
            TSTEP = NH2 * HSTEP + 2

            def scale_last(st, t, j, par):
                dve.wait_ge(sum_done, j + 1)
                st.link(v.reciprocal(rd[:], den[:, par:par + 1]))
                st.link(v.tensor_scalar(rd[:], rd[:], 1.0 / NH2, tm[:, t:t + 1] if isinstance(t, int) else tm[:, bass.ds(t, 1)],
                                        ALU.mult, ALU.mult))
                at_least(dve, attn_done, j - 1)
                v.tensor_scalar(diag[:, par, :], ident[:], rd[:], None, ALU.mult).then_inc(diag_ready, 1)

            def pair(i):
                for u in range(2):
                    t = i * 2 + u
                    for h in range(NH2):
                        j = t * 4 + h
                        par = h % 2
                        st = Steps(dve, dve_step, t * TSTEP + (HSTEP * h + (2 if h == 3 else 0)))
                        best = lambda n: top[:, par, 8 * n:8 * n + 8]
                        dve.wait_ge(s_copied, j * 4 + 4)
                        stand(dve, passed)
                        st.link(v.max(best(0), s[:, par, :]))
                        v.tensor_scalar(nb[:, par:par + 1], best(0)[:, 0:1], -SCALE, None, ALU.mult).then_inc(nb_ready, 1)
                        at_least(dve, ez_done, j - 1)
                        stand(dve, passed)
                        v.match_replace(z[:, par, :], best(0), s[:, par, :], NEG).then_inc(s_read, 1)
                        dve.wait_ge(s_read, j + 1)
                        if not (isinstance(j, int) and j == 0):
                            scale_last(st, t - 1 if h == 0 else t, j - 1, 1 - par)
                        else:
                            st.link(v.memset(rd[:], 0.0))
                            st.link(v.memset(rd[:], 0.0))
                        for n in range(1, 4):
                            stand(dve, passed)
                            st.link(v.max(best(n), z[:, par, :]))
                            stand(dve, passed)
                            last = v.match_replace(z[:, par, :], best(n), z[:, par, :], NEG)
                            if n < 3:
                                st.link(last)
                        last.then_inc(z_done, 1)
                        assert st.n == HSTEP - 1, st.n
                        st.link(v.tensor_copy(rd[:], rd[:]))
                        if h == 2:
                            dve.wait_ge(x_in[u], i * 16 + 16)
                            st.link(v.bn_stats(stats[:], xt[:, u, :]))
                            stand(dve, passed)
                            v.bn_aggr(mv[:], stats[:]).then_inc(var_ready, 1)
                            dve.wait_ge(std_ready, t + 1)
                            st.link(v.reciprocal(rstd[:], std[:]))
                            at_least(dve, xm_ready, t)
                            v.tensor_scalar(xl[:], xt[:, u, :], mv[:, 0:1], rstd[:], ALU.subtract, ALU.mult).then_inc(ln_done, 1)
                            dve.wait_ge(ln_done, t + 1)

            pairs(dve, pair)
            st = Steps(dve, dve_step, TILES * TSTEP)
            scale_last(st, TILES - 1, TILES * 4 - 1, 1)

        @block.gpsimd
        def _(pool):
            pool.wait_ge(weights_in, 16 * 7)

            def modulate(t, i, u):
                st = Steps(pool, pool_step, t * 4)
                pool.wait_ge(ln_done, t + 1)
                st.link(pool.tensor_tensor(xl[:], xl[:], gb[:, 0, :], ALU.mult))
                st.link(pool.tensor_tensor(xl[:], xl[:], gb[:, 1, :], ALU.add))
                pool.wait_ge(fi_copied, t + 1)
                at_least(pool, xm_out[u], i * 16)
                st.link(pool.tensor_tensor(xo[:, u, :], xl[:], fi[:, 0, :], ALU.mult))
                st.link(pool.tensor_tensor(xo[:, u, :], xo[:, u, :], fi[:, 1, :], ALU.add))
                pool.tensor_tensor(xo[:, u, :], xo[:, u, :], xl[:], ALU.add).then_inc(xm_ready, 1)
                pool.wait_ge(xm_ready, t + 1)
                pool.dma_start(xm[bass.ds(t * P, P), :], xo[:, u, :]).then_inc(xm_out[u], 16)

            def store_mod(t, u):
                pool.wait_ge(fo_copied, t + 1)
                pool.dma_start(mod_out[bass.ds(t * P, P), :], fo[:, u, :]).then_inc(fo_out[u], 16)

            def pair(i):
                for u in range(2):
                    t = i * 2 + u
                    for h in range(NH2):
                        j = t * 4 + h
                        pool.wait_ge(e_done, j + 1)
                        pool.wait_ge(ez_done, j + 1)
                        pool.tensor_tensor(e[:, h % 2, :], e[:, h % 2, :], ez[:], ALU.subtract).then_inc(w_ready, 1)
                        if not (isinstance(t, int) and t == 0):
                            if h == 1:
                                modulate(t - 1, i - (1 - u), 1 - u)
                            if h == 2:
                                store_mod(t - 1, 1 - u)

            pairs(pool, pair)
            modulate(TILES - 1, PAIRS - 1, 1)
            store_mod(TILES - 1, 1)
            for u in range(2):
                pool.wait_ge(xm_out[u], 16 * PAIRS)
                pool.wait_ge(fo_out[u], 16 * PAIRS)


NS = 64
HALF = S // 32
DCH = 64
LOG = 10
LN2_HI = 0.693145751953125
MAGIC = 12582912.0
TWO_PI = 6.283185


def ssm_kernel(nc, log_dt, A_re, A_im, C_re, C_im, cst, conv_k):
    with ExitStack() as ctx:
        m = Alloc(nc, ctx, "k_")
        ld = m.sb("ld", [P, D])
        are, aim, cre, cim = (m.sb(n, [P, D]) for n in "are aim cre cim".split())
        cs = m.sb("cs", [P, 6 + 64])
        t = [m.sb(f"t{n}", [P, D]) for n in range(8)]
        th = m.sb("th", [P, 2, D])
        grow = m.sb("grow", [P, LOG, D])
        ar, tau, dcr, dci = (m.sb(n, [P, D]) for n in "ar tau dcr dci".split())
        x = m.sb("x", [P, DCH, 32])
        f = [m.sb(f"f{n}", [P, DCH, 32]) for n in range(3)]
        ea = m.sb("ea", [P, 2, DCH, 32])
        sn = [m.sb(f"sn{n}", [P, DCH, 32]) for n in range(3)]
        U = m.sb("U", [P, DCH, 32])
        W = m.sb("W", [P, DCH, 32])
        W2 = m.sb("W2", [P, DCH, 32])
        ko = m.sb("ko", [32, DCH, 32])
        p_k = m.ps("p_k", [32, DCH, 32])
        params_in, act_in, act_out, step, u_ready, w_ready, uw_used, k_done, k_copied, k_out, arg_ready, sin_done, th_done, th_used, w_half, passed = [
            m.sem(n) for n in "params_in act_in act_out step u_ready w_ready uw_used k_done k_copied k_out arg_ready sin_done th_done th_used w_half passed".split()]
        NCHUNK = D // DCH
        offs = {"u": cs[:, 0:1], "w1": cs[:, 1:2], "w2": cs[:, 2:3]}
        bias = {"u": cs[:, 3:4], "w1": cs[:, 4:5], "w2": cs[:, 5:6]}
        la, lb = cs[:, 6:38], cs[:, 38:70]
        block = ctx.enter_context(nc.Block())

        @block.sync
        def _(sp):
            sp.dma_start(ld[:], log_dt.rearrange("(a n) -> a n", a=1).to_broadcast([P, D])).then_inc(params_in, 16)
            for dst, src in ((are, A_re), (aim, A_im), (cre, C_re), (cim, C_im)):
                for part in range(2):
                    sp.dma_start(dst[NS * part:NS * part + NS, :], src).then_inc(params_in, 16)
            sp.dma_start(cs[:], cst).then_inc(params_in, 16)
            with sp.Fori(0, NCHUNK) as c:
                done, row = sp.snap(c + 1), sp.snap(c * DCH)
                sp.wait_ge(k_copied, done)
                sp.dma_start(conv_k[bass.ds(row, DCH), :].rearrange("d (a b) -> a d b", b=32), ko[:]).then_inc(k_out, 16)
            sp.wait_ge(k_out, 16 * NCHUNK)

        @block.scalar
        def _(act):
            a = nc.scalar.activation
            act.wait_ge(params_in, 160)
            act.wait_ge(act_in, 1)
            for k in range(LOG):
                at_least(act, th_used, k - 1)
                a(th[:, k % 2, :], ar[:], ACT.Tanh, scale=0.5 * 2 ** k).then_inc(th_done, 1)
            act.wait_ge(act_in, 4)
            for n in (1, 2, 7):
                a(t[n][:], t[n][:], ACT.Sin, scale=TWO_PI).then_inc(act_out, 1)
            with act.Fori(0, NCHUNK) as c:
                for n, key in enumerate(("u", "w1", "w2")):
                    act.wait_ge(arg_ready, c * 3 + (n + 1))
                    a(sn[n][:], f[n][:], ACT.Sin, bias=bias[key], scale=-TWO_PI).then_inc(sin_done, 1)
                act.wait_ge(k_out, c * 16)
                act.wait_ge(k_done, c + 1)
                a(ko[:], p_k[:], ACT.Copy).then_inc(k_copied, 1)

        @block.tensor
        def _(pe):
            with pe.Fori(0, NCHUNK) as c:
                pe.wait_ge(u_ready, c + 1)
                pe.wait_ge(w_ready, c + 1)
                pe.wait_ge(k_copied, c)
                for d in range(DCH):
                    last = nc.tensor.matmul(p_k[:, d, :], U[:, d, :], W[:, d, :], start=True, stop=True,
                                            skip_group_check=True)
                last.then_inc(k_done, 1)

        @block.vector
        def _(dve):
            v = nc.vector
            dve.wait_ge(params_in, 160)
            st = Steps(dve, step, 0)
            tt, ts = v.tensor_tensor, v.tensor_scalar
            ki = t[6][:].bitcast(mybir.dt.int32)
            st.link(ts(t[3][:], ld[:], 1.0 / math.log(2.0), MAGIC, ALU.mult, ALU.add))
            st.link(ts(t[3][:], t[3][:], MAGIC, None, ALU.subtract))
            st.link(v.scalar_tensor_tensor(t[4][:], t[3][:], -LN2_HI, ld[:], ALU.mult, ALU.add))
            st.link(v.scalar_tensor_tensor(t[4][:], t[3][:], LN2_HI - math.log(2.0), t[4][:], ALU.mult, ALU.add))
            st.link(ts(t[5][:], t[4][:], 1.0 / math.factorial(8), None, ALU.mult))
            for n in range(7, 0, -1):
                st.link(v.scalar_tensor_tensor(t[5][:], t[5][:], 1.0 / math.factorial(n), t[4][:], ALU.add, ALU.mult))
            st.link(ts(ki, t[3][:], 127.0, None, ALU.add))
            st.link(ts(ki, ki, 23, None, ALU.logical_shift_left))
            st.link(v.scalar_tensor_tensor(ld[:], t[5][:], 1.0, t[6][:], ALU.add, ALU.mult))
            tt(ar[:], ld[:], are[:], ALU.mult).then_inc(act_in, 1)
            st.link(tt(tau[:], ld[:], aim[:], ALU.mult))
            st.link(ts(tau[:], tau[:], 1.0 / (2.0 * math.pi), None, ALU.mult))
            st.link(ts(t[3][:], tau[:], 0.25, None, ALU.add))
            st.link(ts(t[5][:], tau[:], 0.5, None, ALU.mult))
            for n, (src, dst) in enumerate(((t[3], t[1]), (tau, t[2]), (t[5], t[7]))):
                st.link(ts(t[4][:], src[:], MAGIC, MAGIC, ALU.add, ALU.subtract))
                tt(dst[:], src[:], t[4][:], ALU.subtract).then_inc(act_in, 1)
                dve.wait_ge(act_in, n + 2)
            for k in range(LOG):
                dve.wait_ge(th_done, k + 1)
                u = th[:, k % 2, :]
                st.link(ts(t[3][:], u, -1.0, 1.0, ALU.mult, ALU.add))
                st.link(v.reciprocal(t[3][:], t[3][:]))
                if k == 0:
                    st.link(tt(t[0][:], u, t[3][:], ALU.mult))
                v.scalar_tensor_tensor(grow[:, k, :], u, 1.0, t[3][:], ALU.add, ALU.mult).then_inc(th_used, 1)
                dve.wait_ge(th_used, k + 1)
            dve.wait_ge(act_out, 3)
            st.link(ts(t[0][:], t[0][:], 2.0, None, ALU.mult))
            st.link(tt(t[1][:], t[0][:], t[1][:], ALU.mult))
            st.link(tt(t[7][:], t[7][:], t[7][:], ALU.mult))
            st.link(ts(t[7][:], t[7][:], 2.0, None, ALU.mult))
            st.link(tt(t[1][:], t[1][:], t[7][:], ALU.subtract))
            st.link(ts(t[0][:], t[0][:], 1.0, None, ALU.add))
            st.link(tt(t[2][:], t[0][:], t[2][:], ALU.mult))
            st.link(tt(t[3][:], are[:], are[:], ALU.mult))
            st.link(tt(t[4][:], aim[:], aim[:], ALU.mult))
            st.link(tt(t[3][:], t[3][:], t[4][:], ALU.add))
            st.link(v.reciprocal(t[3][:], t[3][:]))
            st.link(tt(t[4][:], t[1][:], are[:], ALU.mult))
            st.link(tt(t[5][:], t[2][:], aim[:], ALU.mult))
            st.link(tt(t[4][:], t[4][:], t[5][:], ALU.add))
            st.link(tt(t[4][:], t[4][:], t[3][:], ALU.mult))
            st.link(tt(t[5][:], t[2][:], are[:], ALU.mult))
            st.link(tt(t[6][:], t[1][:], aim[:], ALU.mult))
            st.link(tt(t[5][:], t[5][:], t[6][:], ALU.subtract))
            st.link(tt(t[5][:], t[5][:], t[3][:], ALU.mult))
            st.link(tt(t[6][:], cre[:], t[4][:], ALU.mult))
            st.link(tt(t[7][:], cim[:], t[5][:], ALU.mult))
            st.link(tt(dcr[:], t[6][:], t[7][:], ALU.subtract))
            st.link(ts(dcr[:], dcr[:], 2.0, None, ALU.mult))
            st.link(tt(t[6][:], cre[:], t[5][:], ALU.mult))
            st.link(tt(t[7][:], cim[:], t[4][:], ALU.mult))
            st.link(tt(dci[:], t[6][:], t[7][:], ALU.add))
            st.link(ts(dci[:], dci[:], 2.0, None, ALU.mult))
            st.link(v.memset(ea[:], 1.0))
            n0 = st.n
            NSTEP = 17

            with dve.Fori(0, NCHUNK) as c:
                st = Steps(dve, step, c * NSTEP + n0)

                def per_channel(small):
                    return small[:, bass.ds(c * DCH, DCH)].unsqueeze(2).to_broadcast([P, DCH, 32])

                def per_l(vec):
                    return vec.unsqueeze(1).to_broadcast([P, DCH, 32])

                dve.wait_ge(k_done, c)
                for k in range(5):
                    n = 2 ** k
                    for part, power in ((0, 5 + k), (1, k)):
                        g = grow[:, power, bass.ds(c * DCH, DCH)].unsqueeze(2).to_broadcast([P, DCH, n])
                        last = tt(ea[:, part, :, n:2 * n], ea[:, part, :, 0:n], g, ALU.mult)
                        st.mark(last)
                    st.wait()

                def argument(key, out):
                    st.link(ts(out[:], x[:], offs[key], MAGIC, ALU.add, ALU.add))
                    v.scalar_tensor_tensor(out[:], out[:], MAGIC, x[:], ALU.subtract, ALU.subtract).then_inc(arg_ready, 1)

                st.link(tt(x[:], per_channel(tau), per_l(la), ALU.mult))
                argument("u", f[0])
                dve.wait_ge(arg_ready, c * 3 + 1)
                st.link(tt(x[:], per_channel(tau), per_l(lb), ALU.mult))
                argument("w1", f[1])
                argument("w2", f[2])
                dve.wait_ge(sin_done, c * 3 + 1)
                tt(U[:], sn[0][:], ea[:, 0], ALU.mult).then_inc(u_ready, 1)
                st.link(tt(W[:], ea[:, 1], per_channel(dcr), ALU.mult))
                dve.wait_ge(arg_ready, c * 3 + 3)
                st.link(tt(x[:], ea[:, 1], per_channel(dci), ALU.mult))
                dve.wait_ge(sin_done, c * 3 + 3)
                tt(W[:], W[:], sn[1][:], ALU.mult).then_inc(w_half, 1)
                tt(W2[:], x[:], sn[2][:], ALU.mult).then_inc(w_half, 1)
                dve.wait_ge(w_half, c * 2 + 2)
                tt(W[:], W[:], W2[:], ALU.add).then_inc(w_ready, 1)
                dve.wait_ge(w_ready, c + 1)
                dve.wait_ge(u_ready, c + 1)
                stand(dve, passed)
                assert st.n == NSTEP, st.n


def convolve(nc, xm, conv_k, D_skip, dft, idft, eye, ys):
    with ExitStack() as ctx:
        m = Alloc(nc, ctx, "s_")
        KT = S // P
        ident = m.sb("ident", [P, P])
        kl = m.sb("kl", [P, KT, D])
        dsk = m.sb("dsk", [1, D])
        xs = m.sb("xs", [P, 2 * KT, D])
        ksp = m.sb("ksp", [P, KT, 2, D])
        Y = m.sb("Y", [P, KT, 4, D])
        kd = Y[:, 0:2, :, :].rearrange("p a b c -> p (a b c)").rearrange("p (t l) -> p t l", l=S)
        fm = m.sb("fm", [P, 2, 2, KT, P])
        t4 = m.sb("t4", [P, 4, D])
        yo = m.sb("yo", [P, 2, D])
        p_k = m.ps("p_k", [P, 2, D])
        p_x = m.ps("p_x", [P, 2, 2, D])
        p_y = m.ps("p_y", [P, 2, D])
        (k_in, const_in, kt_done, kt_copied, kl_ready, xs_in, kf_done, kf_copied, x_done, prod_ready, y_ready,
         inv_done, inv_copied, step, mat_used) = [
            m.sem(n) for n in ("k_in const_in kt_done kt_copied kl_ready xs_in kf_done kf_copied x_done prod_ready y_ready "
                               "inv_done inv_copied step mat_used").split()]
        m_in = [m.sem(f"m_in{u}") for u in range(2)]
        yo_out = [m.store_sem(f"yo_out{u}") for u in range(2)]
        block = ctx.enter_context(nc.Block())
        xv = xm.rearrange("(t p) n -> p t n", p=P)

        @block.sync
        def _(sp):
            sp.dma_start(kd, conv_k.rearrange("(t p) l -> p t l", p=P)).then_inc(k_in, 16)
            sp.dma_start(ident[:], eye).then_inc(const_in, 16)
            sp.dma_start(dsk[:], D_skip.rearrange("(a n) -> a n", a=1)).then_inc(const_in, 16)
            for half in range(2):
                if half:
                    sp.wait_ge(mat_used, KT)
                sp.dma_start(xs[:], xv[:, 16 * half:16 * half + 16, :]).then_inc(xs_in, 16)
                for way, src in ((0, dft), (1, idft)):
                    base = (half * 2 + way) * KT
                    if half + way == 0:
                        for u in range(2):
                            sp.dma_start(fm[:, u], src[u]).then_inc(m_in[u], 16)
                    with sp.Fori(1 if half + way == 0 else 0, KT // 2) as i:
                        for u in range(2):
                            used, row = sp.snap(i * 2 + (base + u - 1)), sp.snap(i * 2 + u)
                            sp.wait_ge(mat_used, used)
                            sp.dma_start(fm[:, u], src[bass.ds(row, 1)].squeeze(0)).then_inc(m_in[u], 16)

        @block.tensor
        def _(pe):
            mm = nc.tensor.matmul
            pe.wait_ge(const_in, 32)
            pe.wait_ge(k_in, 16)
            for c in range(KT):
                at_least(pe, kt_copied, c - 1)
                for d in range(4):
                    last = nc.tensor.transpose(p_k[:, c % 2, d * P:(d + 1) * P], kd[:, d, c * P:(c + 1) * P], ident[:])
                last.then_inc(kt_done, 1)
            pe.wait_ge(kl_ready, 1)
            for half in range(2):
                pe.wait_ge(xs_in, 16 * half + 16)
                with pe.Fori(0, KT // 2) as i:
                    for u in range(2):
                        n = i * 2 + (half * KT + u)
                        pe.wait_ge(m_in[u], i * 16 + (half * 2 * (KT // 2) * 16 + 16))
                        if half == 0:
                            pe.wait_ge(kf_copied, i * 2 + u)
                            for r in range(2):
                                for c in range(KT):
                                    last = mm(p_k[:, r, :], fm[:, u, r, c, :], kl[:, c, :], start=(c == 0), stop=(c == KT - 1))
                            last.then_inc(kf_done, 1)
                        for q in range(2):
                            pe.wait_ge(prod_ready, n * 8 - 4 + 4 * q if False else n * 8)
                            for r in range(2):
                                for c in range(KT):
                                    last = mm(p_x[:, q, r, :], fm[:, u, r, c, :], xs[:, q * KT + c, :], start=(c == 0), stop=(c == KT - 1))
                            if q == 1:
                                last.then_inc(mat_used, 1)
                            else:
                                last.then_inc(x_done, 1)
                with pe.Fori(0, KT // 2) as i:
                    for u in range(2):
                        pe.wait_ge(m_in[u], i * 16 + ((half * 2 + 1) * (KT // 2) * 16 + 16))
                        pe.wait_ge(y_ready, (half + 1) * 32)
                        for q in range(2):
                            pe.wait_ge(inv_copied, i * 4 + (half * 16 + u * 2 + (q - 2 if False else 0)))
                            for r in range(2):
                                for k in range(KT):
                                    last = mm(p_y[:, q, :], fm[:, u, r, k, :], Y[:, k, 2 * q + r, :],
                                              start=(r == 0 and k == 0), stop=(r == 1 and k == KT - 1))
                            last.then_inc(inv_done, 1)
                        nc.tensor.matmul(p_k[0:1, 0, 0:1], ident[:, 0:1], ident[:, 0:1], start=True, stop=True).then_inc(mat_used, 1)

        @block.scalar
        def _(act):
            a = nc.scalar.activation
            for c in range(KT):
                act.wait_ge(kt_done, c + 1)
                a(kl[:, c, :], p_k[:, c % 2, :], ACT.Copy).then_inc(kt_copied, 1)
            for half in range(2):
                if half == 0:
                    with act.Fori(0, KT) as k:
                        act.wait_ge(kf_done, k + 1)
                        a(ksp[:, bass.ds(k, 1)].squeeze(1), p_k[:], ACT.Copy).then_inc(kf_copied, 1)
                with act.Fori(0, KT) as l:
                    for q in range(2):
                        act.wait_ge(inv_done, l * 2 + (half * 16 + q + 1))
                        act.wait_ge(yo_out[q], l * 16 + half * 128)
                        a(yo[:, q, :], p_y[:, q, :], ACT.Copy).then_inc(inv_copied, 1)

        @block.vector
        def _(dve):
            v = nc.vector
            dve.wait_ge(const_in, 32)
            dve.wait_ge(kt_copied, KT)
            v.tensor_tensor(kl[0:1, 0, :], kl[0:1, 0, :], dsk[:], ALU.add).then_inc(kl_ready, 1)
            for half in range(2):
                with dve.Fori(0, KT) as k:
                    if half == 0:
                        dve.wait_ge(kf_copied, k + 1)
                    n = k + half * KT
                    for q in range(2):
                        if q == 0:
                            dve.wait_ge(x_done, n + 1)
                        else:
                            dve.wait_ge(mat_used, k + (half * 2 * KT + 1))
                        kr, ki = (ksp[:, bass.ds(k, 1), r, :].squeeze(1) for r in range(2))
                        dve.wait_ge(y_ready, n * 4 + 2 * q)
                        for d, (xr_, k_) in enumerate(((0, kr), (1, ki), (0, ki), (1, kr))):
                            v.tensor_tensor(t4[:, d, :], p_x[:, q, xr_, :], k_, ALU.mult).then_inc(prod_ready, 1)

        @block.gpsimd
        def _(pool):
            for half in range(2):
                with pool.Fori(0, KT) as k:
                    n = k + half * KT
                    if half:
                        pool.wait_ge(inv_done, 16)
                    for q in range(2):
                        pool.wait_ge(prod_ready, n * 8 + (4 * q + 4))
                        for r in range(2):
                            pool.tensor_tensor(Y[:, bass.ds(k, 1), 2 * q + r, :].squeeze(1), t4[:, 2 * r, :], t4[:, 2 * r + 1, :],
                                               ALU.add if r else ALU.subtract).then_inc(y_ready, 1)
                with pool.Fori(0, KT) as l:
                    for q in range(2):
                        pool.wait_ge(inv_copied, l * 2 + (half * 16 + q + 1))
                        pool.dma_start(ys[bass.ds(l * P + (2 * half + q) * S, P), :], yo[:, q, :]).then_inc(yo_out[q], 16)
            for q in range(2):
                pool.wait_ge(yo_out[q], 16 * 16)


F = 2048
FT = F // P
FW = 4
WB = 2 * P


def quantize_weights(nc, w1T, w2T, w1q, w2q, wmean):
    with ExitStack() as ctx:
        m = Alloc(nc, ctx, "q_")
        w = m.sb("w", [P, 2, 16, 512])
        wb = m.sb("wb", [P, 2, 16, 512], BF16)
        part = m.sb("part", [P, 2, 16])
        tot = m.sb("tot", [P, 2])
        ones = m.sb("ones", [P, P])
        mean = m.sb("mean", [P, 2])
        sc = m.sb("sc", [P, 2])
        p_t = m.ps("p_t", [P, 2])
        w_in = [m.sem(f"w_in{n}") for n in range(2)]
        step, tot_ready, sum_done, q_ready, stored = [m.sem(n) for n in "step tot_ready sum_done q_ready stored".split()]
        block = ctx.enter_context(nc.Block())

        @block.sync
        def _(sp):
            for n, src in enumerate((w1T, w2T)):
                sp.dma_start(w[:, n].rearrange("p a b -> p (a b)"), src).then_inc(w_in[n], 16)
            for n, dst in enumerate((w1q, w2q)):
                sp.wait_ge(q_ready, n + 1)
                sp.dma_start(dst, wb[:, n].rearrange("p a b -> p (a b)")).then_inc(stored, 16)
            sp.dma_start(wmean, mean[:]).then_inc(stored, 16)
            sp.wait_ge(stored, 48)

        @block.tensor
        def _(pe):
            pe.wait_ge(tot_ready, 1)
            nc.tensor.matmul(p_t[:], ones[:], tot[:], start=True, stop=True).then_inc(sum_done, 1)

        @block.vector
        def _(dve):
            v = nc.vector
            st = Steps(dve, step, 0)
            st.link(v.memset(ones[:], 1.0))
            for n in range(2):
                dve.wait_ge(w_in[n], 16)
                st.link(v.tensor_reduce(part[:, n], w[:, n], AX.X, ALU.add, apply_absolute_value=True))
            v.tensor_reduce(tot[:], part[:], AX.X, ALU.add).then_inc(tot_ready, 1)
            dve.wait_ge(sum_done, 1)
            st.link(v.tensor_scalar(mean[:], p_t[:], 1.0 / (D * F), 1e-5, ALU.mult, ALU.max))
            st.link(v.reciprocal(sc[:], mean[:]))
            for n in range(2):
                st.link(v.tensor_scalar(w[:, n], w[:, n], sc[:, n:n + 1], MAGIC, ALU.mult, ALU.add))
                st.link(v.tensor_scalar(w[:, n], w[:, n], MAGIC, 1.0, ALU.subtract, ALU.min))
                v.tensor_scalar(wb[:, n], w[:, n], -1.0, None, ALU.max).then_inc(q_ready, 1)


def feed_forward(nc, x1, ys, mod_out, W1, b1T, W2, b2, g_ffn, b_ffn, g_out, b_out, eye, x2, q1T, inv_rows):
    with ExitStack() as ctx:
        m = Alloc(nc, ctx, "f_")
        w1 = m.sb("w1", [P, KD, F])
        w2 = m.sb("w2", [P, FT, D])
        b1c = m.sb("b1c", [P, FT])
        bc = m.sb("bc", [P, 5, D])
        ident = m.sb("ident", [P, P])
        identb = m.sb("identb", [P, P], BF16)
        eps = m.sb("eps", [P, 1])
        xr = m.sb("xr", [P, 2, D])
        yr = m.sb("yr", [P, 2, D])
        mr = m.sb("mr", [P, 2, 2 * D])
        xt = m.sb("xt", [P, 2, D])
        h = m.sb("h", [P, D])
        hT = m.sb("hT", [P, D])
        gT = m.sb("gT", [P, FT, P])
        r2 = m.sb("r2", [P, D])
        r3 = m.sb("r3", [P, D])
        xo = m.sb("xo", [P, 2, D])
        qf = m.sb("qf", [P, D])
        qb = m.sb("qb", [P, D], BF16)
        qT = m.sb("qT", [P, 2, KD, P], BF16)
        stats = m.sb("stats", [P, 3, 6])
        mv = m.sb("mv", [P, 3, 2])
        std = m.sb("std", [P, 3])
        rstd = m.sb("rstd", [P, 3])
        am = m.sb("am", [P, 1])
        qs = m.sb("qs", [P, 1])
        inv = m.sb("inv", [P, TOK // P])
        invT = m.sb("invT", [TOK // P, P])
        p_g = m.ps("p_g", [P, FT, P])
        p_h = m.ps("p_h", [P, D])
        p_o = m.ps("p_o", [P, D])
        p_q = m.ps("p_q", [P, 2 * KD, P], BF16)[:, 0:KD, :]
        (weights_in, consts, h_ready, hT_done, hT_copied, g_done, g_copied, o_done, mod_done, step, pstep, qb_ready,
         qT_done, qT_copied, x2_ready, r3_ready, inv_out, out_norm, inv_done, inv_copied, passed, ln_head, invT_out) = [
            m.sem(n) for n in (
                "weights_in consts h_ready hT_done hT_copied g_done g_copied o_done mod_done step pstep qb_ready "
                "qT_done qT_copied x2_ready r3_ready inv_out out_norm inv_done inv_copied passed ln_head invT_out").split()]
        var = [m.sem(f"var{n}") for n in range(3)]
        stdr = [m.sem(f"stdr{n}") for n in range(3)]
        t_in = [m.sem(f"t_in{u}") for u in range(2)]
        x2_out = [m.store_sem(f"x2_out{u}") for u in range(2)]
        q_out = [m.store_sem(f"q_out{u}") for u in range(2)]
        TILES = TOK // P
        PAIRS = TILES // 2
        block = ctx.enter_context(nc.Block())

        def pairs(eng, pair):
            pair(0)
            with eng.Fori(1, PAIRS - 1) as i:
                pair(i)
            pair(PAIRS - 1)

        def is_last(t):
            return isinstance(t, int) and t == TILES - 1

        def is_first(t):
            return isinstance(t, int) and t == 0

        @block.sync
        def _(sp):
            def bcast(ap):
                return ap.rearrange("(a n) -> a n", a=1).to_broadcast([P, D])

            def load(u, row):
                sp.dma_start(xr[:, u, :], x1[bass.ds(row, P), :]).then_inc(t_in[u], 16)
                sp.dma_start(yr[:, u, :], ys[bass.ds(row, P), :]).then_inc(t_in[u], 16)
                sp.dma_start(mr[:, u, :], mod_out[bass.ds(row, P), :]).then_inc(t_in[u], 16)

            for u in range(2):
                load(u, u * P)
            for dst, src in [(w1[:], W1.rearrange("(k p) n -> p k n", p=P)), (w2[:], W2.rearrange("(k p) n -> p k n", p=P)),
                             (b1c[:], b1T), (ident[:], eye)] + [
                             (bc[:, n, :], bcast(ap)) for n, ap in enumerate((g_ffn, b_ffn, b2, g_out, b_out))]:
                sp.dma_start(dst, src).then_inc(weights_in, 16)
            with sp.Fori(0, PAIRS - 1) as i:
                for u in range(2):
                    done, row = sp.snap(i * 2 + (u + 1)), sp.snap(i * (2 * P) + (u + 2) * P)
                    sp.wait_ge(r3_ready, done)
                    load(u, row)

        @block.tensor
        def _(pe):
            mm = nc.tensor.matmul
            pe.wait_ge(weights_in, 16 * 9)
            pe.wait_ge(consts, 2)

            def turn_h(t):
                pe.wait_ge(h_ready, t + 1)
                for k in range(KD):
                    last = nc.tensor.transpose(p_h[:, k * P:(k + 1) * P], h[:, k * P:(k + 1) * P], ident[:])
                last.then_inc(hT_done, 1)

            def turn_q(t):
                pe.wait_ge(qb_ready, t + 1)
                at_least(pe, qT_copied, t)
                for k in range(KD):
                    last = nc.tensor.transpose(p_q[:, k, :], qb[:, k * P:(k + 1) * P], identb[:])
                last.then_inc(qT_done, 1)

            def slot(t):
                pe.wait_ge(hT_copied, t + 1)
                for f in range(FT):
                    if f % 4 == 0:
                        at_least(pe, g_copied, t * FT - (FT - 4 - f) if not isinstance(t, int) or t else 0)
                    for k in range(KD):
                        last = mm(p_g[:, f, :], w1[:, k, f * P:(f + 1) * P], hT[:, k * P:(k + 1) * P],
                                  start=(k == 0 and f % 4 == 0), stop=(k == KD - 1 and f % 4 == 3), skip_group_check=True)
                    last.then_inc(g_done, 1)
                if not is_first(t):
                    turn_q(t - 1)
                at_least(pe, var[1], t)
                for f in range(FT):
                    pe.wait_ge(g_copied, t * FT + (f + 1))
                    last = mm(p_o[:], gT[:, f, :], w2[:, f, :], start=(f == 0), stop=(f == FT - 1))
                last.then_inc(o_done, 1)
                if not is_last(t):
                    turn_h(t + 1)

            def pair(i):
                for u in range(2):
                    slot(i * 2 + u)

            turn_h(0)
            pairs(pe, pair)
            turn_q(TILES - 1)
            pe.wait_ge(inv_done, TILES)
            nc.tensor.transpose(p_h[0:TILES, 0:P], inv[:], ident[:]).then_inc(inv_copied, 1)

        @block.scalar
        def _(act):
            a = nc.scalar.activation
            act.wait_ge(consts, 2)
            act.wait_ge(weights_in, 16 * 9)

            def root(n, t):
                act.wait_ge(var[n], t + 1)
                a(std[:, n:n + 1], mv[:, n, 1:2], ACT.Sqrt, bias=eps[:]).then_inc(stdr[n], 1)

            def copy_h(t):
                act.wait_ge(hT_done, t + 1)
                a(hT[:], p_h[:], ACT.Copy).then_inc(hT_copied, 1)

            def slot(t):
                at_least(act, o_done, t)
                for f in range(FT):
                    if f % 4 == 0:
                        act.wait_ge(g_done, t * FT + (f + 4))
                    a(gT[:, f, :], p_g[:, f, :], ACT.Gelu, bias=b1c[:, f:f + 1]).then_inc(g_copied, 1)
                if not is_last(t):
                    root(0, t + 1)
                    copy_h(t + 1)
                root(1, t)
                root(2, t)

            def pair(i):
                for u in range(2):
                    slot(i * 2 + u)

            root(0, 0)
            copy_h(0)
            pairs(act, pair)
            act.wait_ge(inv_copied, 1)
            a(invT[:], p_h[0:TILES, 0:P], ACT.Copy).then_inc(invT_out, 1)
            act.wait_ge(invT_out, 1)
            act.dma_start(inv_rows.rearrange("a (t p) -> (a t) p", p=P), invT[:]).then_inc(inv_out, 16)
            act.wait_ge(inv_out, 16)

        @block.vector
        def _(dve):
            v = nc.vector
            v.memset(eps[:], LN_EPS).then_inc(consts, 1)
            dve.wait_ge(weights_in, 16 * 9)
            v.tensor_copy(identb[:], ident[:]).then_inc(consts, 1)
            dve.wait_ge(consts, 2)
            NSTEP = 12

            def norm(st, n, t, src, dst, sem, free=None):
                st.link(v.bn_stats(stats[:, n, :], src))
                stand(dve, passed)
                v.bn_aggr(mv[:, n, :], stats[:, n, :]).then_inc(var[n], 1)
                dve.wait_ge(stdr[n], t + 1)
                st.link(v.reciprocal(rstd[:, n:n + 1], std[:, n:n + 1]))
                if free:
                    free()
                v.tensor_scalar(dst, src, mv[:, n, 0:1], rstd[:, n:n + 1], ALU.subtract, ALU.mult).then_inc(sem, 1)

            def head(st, t, u):
                dve.wait_ge(mod_done, t + 1)
                norm(st, 0, t, xt[:, u, :], h[:], ln_head, lambda: at_least(dve, hT_done, t))

            def tail(st, t, i, u):
                dve.wait_ge(o_done, t + 1)
                st.link(v.tensor_tensor(r2[:], p_o[:], xt[:, u, :], ALU.add))
                norm(st, 1, t, r2[:], r2[:], out_norm)
                dve.wait_ge(r3_ready, t + 1)
                norm(st, 2, t, r3[:], xo[:, u, :], x2_ready, lambda: at_least(dve, x2_out[u], i * 16))
                dve.wait_ge(x2_ready, t + 1)
                st.link(v.tensor_reduce(am[:], xo[:, u, :], AX.X, ALU.max, apply_absolute_value=True))
                st.link(v.tensor_scalar(am[:], am[:], 1e-5, None, ALU.max))
                st.link(v.reciprocal(qs[:], am[:]))
                st.link(v.tensor_scalar(qs[:], qs[:], 127.0, None, ALU.mult))
                v.reciprocal(inv[:, t:t + 1] if isinstance(t, int) else inv[:, bass.ds(t, 1)], qs[:]).then_inc(inv_done, 1)
                st.link(v.tensor_scalar(qf[:], xo[:, u, :], qs[:], MAGIC, ALU.mult, ALU.add))
                at_least(dve, qT_done, t)
                v.tensor_scalar(qb[:], qf[:], MAGIC, None, ALU.subtract).then_inc(qb_ready, 1)
                dve.wait_ge(qT_done, t + 1)
                at_least(dve, q_out[u], i * 16)
                v.tensor_copy(qT[:, u], p_q).then_inc(qT_copied, 1)

            def pair(i):
                for u in range(2):
                    t = i * 2 + u
                    st = Steps(dve, step, t * NSTEP + 2)
                    if not is_last(t):
                        head(st, t + 1, 1 - u)
                    tail(st, t, i, u)
                    assert is_last(t) or st.n == NSTEP, st.n

            head(Steps(dve, step, 0), 0, 0)
            pairs(dve, pair)

        @block.gpsimd
        def _(pool):
            tt = pool.tensor_tensor
            pool.wait_ge(weights_in, 16 * 9)
            NSTEP = 7

            def modulate(st, t, i, u):
                pool.wait_ge(t_in[u], i * 48 + 48)
                at_least(pool, r3_ready, t - 1)
                st.link(tt(xt[:, u, :], yr[:, u, :], mr[:, u, 0:D], ALU.mult))
                st.link(tt(yr[:, u, :], yr[:, u, :], mr[:, u, D:], ALU.add))
                st.link(tt(xt[:, u, :], xt[:, u, :], yr[:, u, :], ALU.add))
                tt(xt[:, u, :], xt[:, u, :], xr[:, u, :], ALU.add).then_inc(mod_done, 1)
                pool.wait_ge(ln_head, t + 1)
                st.link(tt(h[:], h[:], bc[:, 0, :], ALU.mult))
                tt(h[:], h[:], bc[:, 1, :], ALU.add).then_inc(h_ready, 1)
                st.link(tt(xt[:, u, :], xt[:, u, :], bc[:, 2, :], ALU.add))

            def finish(st, t, u):
                pool.wait_ge(out_norm, t + 1)
                st.link(tt(r3[:], r2[:], bc[:, 3, :], ALU.mult))
                st.link(tt(r3[:], r3[:], bc[:, 4, :], ALU.add))
                tt(r3[:], r3[:], xr[:, u, :], ALU.add).then_inc(r3_ready, 1)

            def store(t, u):
                pool.wait_ge(x2_ready, t + 1)
                pool.dma_start(x2[bass.ds(t * P, P), :], xo[:, u, :]).then_inc(x2_out[u], 16)
                pool.wait_ge(qT_copied, t + 1)
                pool.dma_start(q1T.rearrange("(k p) n -> p k n", p=P)[:, :, bass.ds(t * P, P)], qT[:, u]).then_inc(q_out[u], 16)

            def pair(i):
                for u in range(2):
                    t = i * 2 + u
                    st = Steps(pool, pstep, t * NSTEP + 5)
                    if not is_last(t):
                        modulate(st, t + 1, i + u, 1 - u)
                    finish(st, t, u)
                    assert is_last(t) or st.n == NSTEP, st.n
                    store(t, u)

            st = Steps(pool, pstep, 0)
            modulate(st, 0, 0, 0)
            pairs(pool, pair)
            for u in range(2):
                pool.wait_ge(x2_out[u], 16 * PAIRS)
                pool.wait_ge(q_out[u], 16 * PAIRS)


def bit_ffn(nc, x2, q1T, inv_rows, w1q, w2q, wmean, conv_w, conv_b, eye, out):
    with ExitStack() as ctx:
        m = Alloc(nc, ctx, "b_")
        w1 = m.sb("w1", [P, KD, F], BF16)
        w2 = m.sb("w2", [P, FT, D], BF16)
        wm = m.sb("wm", [P, 2])
        cw = m.sb("cw", [P, FT, 3])
        cb = m.sb("cb", [P, FT])
        ident = m.sb("ident", [P, P])
        ones = m.sb("ones", [P, P])
        eps = m.sb("eps", [P, 1])
        qb = m.sb("qb", [P, 2, KD, WB + 2], BF16)
        rs = m.sb("rs", [P, 2, WB + 2])
        xr = m.sb("xr", [P, 2, 2, D])
        hs = m.sb("hs", [P, 2, WB + 2])
        c1 = m.sb("c1", [P, 2, WB])
        c2 = m.sb("c2", [P, 2, WB])
        c3 = m.sb("c3", [P, 2, WB])
        sl = m.sb("sl", [P, FT, WB])
        sq = m.sb("sq", [P, FT, WB])
        q2 = m.sb("q2", [P, FT, WB], BF16)
        mx = m.sb("mx", [P, WB])
        a2 = m.sb("a2", [P, 2])
        s2 = m.sb("s2", [P, 2])
        i2 = m.sb("i2", [P, 2, 2])
        dg = m.sb("dg", [P, 2, P])
        res = m.sb("res", [P, 2, D])
        stats = m.sb("stats", [P, 2, 6])
        mv = m.sb("mv", [P, 2, 2])
        std = m.sb("std", [P, 2])
        rstd = m.sb("rstd", [P, 2])
        xo = m.sb("xo", [P, 2, D])
        p_h = m.ps("p_h", [P, 2, 512])
        p_m = m.ps("p_m", [P, 512])[:, 0:WB].rearrange("p (u n) -> p u n", u=2)
        p_b = m.ps("p_b", [P, 512])[:, 0:WB]
        p_o = m.ps("p_o", [P, 2, D])
        (weights_in, consts, h_done, hs_ready, c1_ready, c3_ready, sl_ready, mx_ready, mt_done, dg_ready, b_done,
         sq_ready, q2_ready, o_done, res_ready, var_ready, std_ready, out_ready, step, conv_step, passed, pstep) = [
            m.sem(n) for n in (
                "weights_in consts h_done hs_ready c1_ready c3_ready sl_ready mx_ready mt_done dg_ready b_done "
                "sq_ready q2_ready o_done res_ready var_ready std_ready out_ready step conv_step passed pstep").split()]
        t_in = [m.sem(f"t_in{u}") for u in range(2)]
        x_out = [m.store_sem(f"x_out{u}") for u in range(2)]
        PB = S // WB
        NB = B * PB
        block = ctx.enter_context(nc.Block())

        def halo(k):
            return (1 if k == 0 else 0), (WB + 1 if k == PB - 1 else WB + 2)

        @block.sync
        def _(sp):
            for dst, src in ((w1[:].rearrange("p a b -> p (a b)"), w1q), (w2[:].rearrange("p a b -> p (a b)"), w2q),
                             (wm[:], wmean), (cw[:], conv_w), (cb[:], conv_b), (ident[:], eye)):
                sp.dma_start(dst, src).then_inc(weights_in, 16)
            qv = q1T.rearrange("(k p) n -> p k n", p=P)
            xv = x2.rearrange("(t p) n -> p t n", p=P)

            def load(b, k):
                snap = (lambda a: a) if isinstance(b, int) else sp.snap
                u = k % 2
                lo, hi = halo(k)
                used = snap(b * PB + (k - 1))
                col = snap(b * S + (k * WB - 1 + lo))
                tile_ = snap(b * CH + 2 * k)
                at_least(sp, res_ready, used)
                sp.dma_start(qb[:, u, :, lo:hi], qv[:, :, bass.ds(col, hi - lo)]).then_inc(t_in[u], 16)
                sp.dma_start(rs[:, u, lo:hi], inv_rows[:, bass.ds(col, hi - lo)].to_broadcast([P, hi - lo])).then_inc(t_in[u], 16)
                sp.dma_start(xr[:, u], xv[:, bass.ds(tile_, 2), :]).then_inc(t_in[u], 16)

            for k in range(PB):
                load(0, k)
            with sp.Fori(1, B) as b:
                for k in range(PB):
                    load(b, k)

        def blocks(eng, body):
            for k in range(PB):
                body(0, k, k)
            with eng.Fori(1, B) as b:
                for k in range(PB):
                    body(b, k, b * PB + k)

        @block.tensor
        def _(pe):
            mm = nc.tensor.matmul
            pe.wait_ge(weights_in, 96)
            pe.wait_ge(consts, 5)

            def project(n, u):
                if u == 0:
                    pe.wait_ge(q2_ready, n + 1)
                at_least(pe, res_ready, n)
                for f in range(FT):
                    last = mm(p_o[:, u, :], q2[:, f, u * P:(u + 1) * P], w2[:, f, :], start=(f == 0), stop=(f == FT - 1))
                last.then_inc(o_done, 1)

            def body(b, k, n):
                u = k % 2
                lo, hi = halo(k)
                pe.wait_ge(t_in[u], b * (PB // 2 * 48) + (k // 2 * 48 + 48))
                for f in range(FT):
                    at_least(pe, hs_ready, n * FT + (f - 1))
                    for d in range(KD):
                        last = mm(p_h[:, f % 2, lo:hi], w1[:, d, f * P:(f + 1) * P], qb[:, u, d, lo:hi],
                                  start=(d == 0), stop=(d == KD - 1))
                    last.then_inc(h_done, 1)
                    if f in (3, 7) and not (isinstance(n, int) and n == 0):
                        project(n - 1, f // 4)
                pe.wait_ge(mx_ready, n + 1)
                for w in range(2):
                    last = nc.tensor.transpose(p_m[:, w, :], mx[:, w * P:(w + 1) * P], ident[:])
                last.then_inc(mt_done, 1)
                pe.wait_ge(dg_ready, n + 1)
                last = mm(p_b, ones[:], dg[:].rearrange("p a b -> p (a b)"), start=True, stop=True)
                last.then_inc(b_done, 1)

            blocks(pe, body)
            for u in range(2):
                project(NB - 1, u)

        @block.scalar
        def _(act):
            a = nc.scalar.activation
            act.wait_ge(consts, 5)

            def root(n):
                act.wait_ge(var_ready, n * 2 + 2)
                a(std[:], mv[:, :, 1], ACT.Sqrt, bias=eps[:]).then_inc(std_ready, 1)

            def body(b, k, n):
                def taps(f):
                    j = n * FT + f
                    act.wait_ge(hs_ready, j + 1)
                    at_least(act, c3_ready, j - 1)
                    a(c1[:, f % 2, :], hs[:, f % 2, 1:WB + 1], ACT.Identity, bias=cb[:, f:f + 1], scale=cw[:, f, 1:2]).then_inc(c1_ready, 1)

                def silu(f):
                    j = n * FT + f
                    act.wait_ge(c3_ready, j + 1)
                    if f == 0:
                        at_least(act, sq_ready, n)
                    a(sl[:, f, :], c3[:, f % 2, :], ACT.Silu).then_inc(sl_ready, 1)

                taps(0)
                for f in range(FT):
                    if f + 1 < FT:
                        taps(f + 1)
                    silu(f)
                    if f == 14 and not (isinstance(n, int) and n == 0):
                        root(n - 1)

            blocks(act, body)
            root(NB - 1)

        @block.vector
        def _(dve):
            v = nc.vector
            v.memset(eps[:], LN_EPS).then_inc(consts, 1)
            v.memset(ones[:], 1.0).then_inc(consts, 1)
            v.memset(hs[:], 0.0).then_inc(consts, 1)
            dve.wait_ge(weights_in, 96)
            v.tensor_scalar(cw[:], cw[:], wm[:, 0:1], None, ALU.mult).then_inc(consts, 1)
            v.memset(i2[:], 0.0).then_inc(consts, 1)
            dve.wait_ge(consts, 5)
            NSTEP = 12
            TAIL = 4

            def tail_a(st, n, par):
                for u in range(2):
                    dve.wait_ge(o_done, n * 2 + (u + 1))
                    st.link(v.scalar_tensor_tensor(res[:, u, :], p_o[:, u, :], i2[:, par, u:u + 1], xr[:, par, u, :], ALU.mult, ALU.add))
                    last = v.bn_stats(stats[:, u, :], res[:, u, :])
                    if u == 0:
                        st.link(last)
                    else:
                        last.then_inc(res_ready, 1)
                dve.wait_ge(res_ready, n + 1)
                stand(dve, passed)
                for u in range(2):
                    v.bn_aggr(mv[:, u, :], stats[:, u, :]).then_inc(var_ready, 1)

            def tail_b(st, n):
                dve.wait_ge(std_ready, n + 1)
                st.link(v.reciprocal(rstd[:], std[:]))
                for u in range(2):
                    at_least(dve, x_out[u], n * 16)
                    v.tensor_scalar(xo[:, u, :], res[:, u, :], mv[:, u, 0:1], rstd[:, u:u + 1], ALU.subtract, ALU.mult).then_inc(out_ready, 1)
                dve.wait_ge(out_ready, n * 2 + 2)

            def body(b, k, n):
                par = k % 2
                st = Steps(dve, step, 0 if isinstance(n, int) and n == 0 else n * NSTEP - TAIL)
                lo, hi = halo(k)
                dve.wait_ge(t_in[par], b * (PB // 2 * 48) + (k // 2 * 48 + 48))

                def dequantize(f):
                    j = n * FT + f
                    at_least(dve, c3_ready, j - 1)
                    dve.wait_ge(h_done, j + 1)
                    v.tensor_tensor(hs[:, f % 2, lo:hi], p_h[:, f % 2, lo:hi], rs[:, par, lo:hi], ALU.mult).then_inc(hs_ready, 1)

                if k in (0, PB - 1):
                    dve.wait_ge(c3_ready, n * FT) if not (isinstance(n, int) and n == 0) else None
                    col = 0 if k == 0 else WB + 1
                    st.link(v.memset(hs[:, :, col:col + 1], 0.0))
                else:
                    st.link(v.memset(rstd[:], 0.0))
                dequantize(0)
                for f in range(FT):
                    j = n * FT + f
                    if f + 1 < FT:
                        dequantize(f + 1)
                    dve.wait_ge(c1_ready, j + 1)
                    dve.wait_ge(hs_ready, j + 1)
                    v.scalar_tensor_tensor(c2[:, f % 2, :], hs[:, f % 2, 0:WB], cw[:, f, 0:1], c1[:, f % 2, :], ALU.mult, ALU.add).then_inc(conv_step, 1)
                    dve.wait_ge(conv_step, j + 1)
                    at_least(dve, sl_ready, j - 1)
                    v.scalar_tensor_tensor(c3[:, f % 2, :], hs[:, f % 2, 2:WB + 2], cw[:, f, 2:3], c2[:, f % 2, :], ALU.mult, ALU.add).then_inc(c3_ready, 1)
                    if f == 12 and not (isinstance(n, int) and n == 0):
                        tail_a(st, n - 1, 1 - par)
                if not (isinstance(n, int) and n == 0):
                    tail_b(st, n - 1)
                dve.wait_ge(sl_ready, n * FT + FT)
                v.tensor_reduce(mx[:], sl[:].rearrange("p f t -> p t f"), AX.X, ALU.max,
                                apply_absolute_value=True).then_inc(mx_ready, 1)
                dve.wait_ge(mt_done, n + 1)
                st.link(v.tensor_reduce(a2[:], p_m, AX.X, ALU.max))
                st.link(v.tensor_scalar(a2[:], a2[:], 1e-5, None, ALU.max))
                st.link(v.reciprocal(a2[:], a2[:]))
                st.link(v.tensor_scalar(s2[:], a2[:], 127.0, None, ALU.mult))
                st.link(v.reciprocal(i2[:, par, :], s2[:]))
                st.link(v.tensor_scalar(i2[:, par, :], i2[:, par, :], wm[:, 1:2], None, ALU.mult))
                st.link(v.tensor_scalar(dg[:, 0, :], ident[:], s2[:, 0:1], None, ALU.mult))
                v.tensor_scalar(dg[:, 1, :], ident[:], s2[:, 1:2], None, ALU.mult).then_inc(dg_ready, 1)
                dve.wait_ge(b_done, n + 1)
                at_least(dve, q2_ready, n)
                v.tensor_tensor(sq[:], sl[:], p_b.unsqueeze(1).to_broadcast([P, FT, WB]), ALU.mult).then_inc(sq_ready, 1)
                dve.wait_ge(sq_ready, n + 1)
                at_least(dve, o_done, n * 2)
                v.tensor_scalar(q2[:], sq[:], MAGIC, MAGIC, ALU.add, ALU.subtract).then_inc(q2_ready, 1)
                assert st.n == (NSTEP - TAIL if isinstance(n, int) and n == 0 else NSTEP), st.n

            def padded(b, k, n):
                body(b, k, n)

            blocks(dve, body)
            st = Steps(dve, step, NB * NSTEP - TAIL)
            tail_a(st, NB - 1, 1)
            tail_b(st, NB - 1)

        @block.gpsimd
        def _(pool):
            pool.wait_ge(consts, 5)

            def store(n, row):
                for u in range(2):
                    pool.wait_ge(out_ready, n * 2 + (u + 1))
                    pool.dma_start(out[bass.ds(row + u * P, P), :], xo[:, u, :]).then_inc(x_out[u], 16)

            def body(b, k, n):
                if not (isinstance(n, int) and n == 0):
                    store(n - 1, n * WB - WB)
            blocks(pool, body)
            store(NB - 1, NB * WB - WB)
            for u in range(2):
                pool.wait_ge(x_out[u], 16 * NB)


def decoder(nc, a):
    def dram(name, shape, dt=F32):
        return nc.dram_tensor(name, shape, dt).ap()

    x1, xm, ys, x2 = (dram(n, (TOK, D)) for n in ("x1", "xm", "ys", "x2"))
    mod_out = dram("mod_out", (TOK, 2 * D))
    keysT, film_w = dram("keysT", (P, B * N2)), dram("film_w", (DV, 4 * D))
    film_b, mask_row = dram("film_b", (1, 4 * D)), dram("mask_row", (B, N2), BF16)
    conv_k = dram("conv_k", (D, S))
    w1q, w2q, wmean = dram("w1q", (P, KD * F), BF16), dram("w2q", (P, FT * D), BF16), dram("wmean", (P, 2))
    q1T, inv_rows = dram("q1T", (D, TOK), BF16), dram("inv_rows", (1, TOK))

    attention(nc, a["x"], a["xT"], a["W_attn"], a["b_attn"], a["W_proj"], a["b_proj"], a["tri"], a["blockdiag"],
              a["eye"], x1)
    prepare(nc, a["ctxT"], a["Wk"], a["WvT"], a["W_film_in"], a["b_film_in"], a["W_film_out"], a["b_film_out"],
            a["gate"], a["mask2"], keysT, film_w, film_b, mask_row)
    cross(nc, x1, keysT, a["ctx"], film_w, film_b, mask_row, a["mask1"], a["Wq"], a["g_in"], a["b_in"], a["eye"],
          xm, mod_out)
    ssm_kernel(nc, a["log_dt"], a["A_re"], a["A_im"], a["C_re"], a["C_im"], a["angles"], conv_k)
    convolve(nc, xm, conv_k, a["D_skip"], a["dft"], a["idft"], a["eye"], ys)
    feed_forward(nc, x1, ys, mod_out, a["W1"], a["b1T"], a["W2"], a["b2"], a["g_ffn"], a["b_ffn"], a["g_out"],
                 a["b_out"], a["eye"], x2, q1T, inv_rows)
    quantize_weights(nc, a["w1T"], a["w2T"], w1q, w2q, wmean)
    bit_ffn(nc, x2, q1T, inv_rows, w1q, w2q, wmean, a["conv_w"], a["conv_b"], a["eye"], a["out"])


def shape_constants():
    tri = np.triu(np.ones((P, P), np.float32))
    blockdiag = np.zeros((P, 4 * VW), np.float32)
    for r in range(4):
        blockdiag[DH * r:DH * r + DH, VW * r:VW * r + VW] = 1
    angles = np.zeros((P, 6 + 64), np.float32)
    for n, (re, im) in enumerate(((.25, .5), (.25, 0), (.5, .25))):
        angles[:NS, n], angles[NS:, n] = re, im
        angles[:, 3 + n] = angles[:, n] * np.float32(TWO_PI)
    angles[:, 6:38] = np.arange(32) * 32
    angles[:, 38:70] = np.arange(32)
    k, l = np.arange(S)[:, None], np.arange(S)[None]
    turn = 2 * np.pi * (((4 * k + 1) * l) % (4 * S)) / (4 * S)
    m = np.stack([np.cos(turn), -np.sin(turn)]).reshape(2, S // P, P, S // P, P)
    dft = np.ascontiguousarray(m.transpose(1, 4, 0, 3, 2).astype(np.float32))
    idft = np.ascontiguousarray((m / S).transpose(3, 2, 0, 1, 4).astype(np.float32))
    return dict(tri=tri, blockdiag=blockdiag, eye=np.eye(P, dtype=np.float32), angles=angles, dft=dft, idft=idft)


def kernel(**inputs):
    import concourse.bacc as bacc
    from concourse.bass_utils import run_bass_kernel_spmd

    c = np.ascontiguousarray
    i = {k: np.asarray(v) for k, v in inputs.items()}
    X, A, N = "L0_xattn_", "L0_attn_", "L0_ffn_"
    x, ctx = i["x"].reshape(TOK, D), i["ctx_768"].reshape(B * N2, DV)

    def rows_of(wT):
        return c(wT.reshape(-1, P, wT.shape[1]).transpose(1, 0, 2).reshape(P, -1))

    arrays = dict(
        x=c(x), xT=c(x.T), ctx=c(ctx), ctxT=c(ctx.T),
        W_attn=i[A + "W_attn"], b_attn=i[A + "b_attn"], W_proj=i[A + "W_proj"], b_proj=i[A + "b_proj"],
        Wq=i[X + "Wq"], Wk=i[X + "Wk"], WvT=c(i[X + "Wv"].T),
        W_film_in=i[X + "W_film_in"], b_film_in=i[X + "b_film_in"],
        W_film_out=i[X + "W_film_out"], b_film_out=i[X + "b_film_out"], gate=i[X + "mod_gate"].reshape(1, 1),
        mask1=c(i["mask_BxS_bf1"].view(np.uint8).reshape(TOK // P, P).T), mask2=c(i["mask_BxS2_bf1"].view(np.uint8)),
        g_in=i[X + "g_norm_in"], b_in=i[X + "b_norm_in"], g_out=i[X + "g_norm_out"], b_out=i[X + "b_norm_out"],
        g_ffn=i[X + "g_ffn"], b_ffn=i[X + "b_ffn"], W1=i[X + "W1"], b1T=c(i[X + "b1"].reshape(FT, P).T),
        W2=i[X + "W2"], b2=i[X + "b2"], log_dt=i[X + "log_dt"], A_re=c(i[X + "A_re"].T), A_im=c(i[X + "A_im"].T),
        C_re=c(i[X + "C_re"].T), C_im=c(i[X + "C_im"].T), D_skip=i[X + "D_skip"],
        w1T=rows_of(i[N + "w1"].T), w2T=rows_of(i[N + "w2"].T),
        conv_w=c(i[N + "conv_w"].reshape(FT, P, 3).transpose(1, 0, 2)), conv_b=c(i[N + "conv_b"].reshape(FT, P).T),
        **shape_constants())
    arrays = {k: c(v) for k, v in arrays.items()}
    nc = bacc.Bacc("TRN2", target_bir_lowering=False, num_devices=1)
    a = {k: nc.dram_tensor("in_" + k, v.shape, mybir.dt.from_np(v.dtype), kind="ExternalInput").ap()
         for k, v in arrays.items()}
    a["out"] = nc.dram_tensor("out", (TOK, D), F32, kind="ExternalOutput").ap()
    decoder(nc, a)
    r = run_bass_kernel_spmd(nc, [{"in_" + k: v for k, v in arrays.items()}], core_ids=[0])
    return r.results[0]["out"].reshape(B, S, D)
```

```python
import math
from contextlib import ExitStack

import concourse.bass as bass
import numpy as np
from concourse import mybir

ALU = mybir.AluOpType
ACT = mybir.ActivationFunctionType
AX = mybir.AxisListType
F32 = mybir.dt.float32
BF16 = mybir.dt.bfloat16
U8 = mybir.dt.uint8

P = 128
B, S, D = 4, 1024, 512
TOK = B * S
CH = S // P
KD = D // P
H, DH = 16, 32
G = H // 4
VW = DH + 1
LN_EPS = 1e-5
BR = 65


class Steps:

    def __init__(self, eng, sem, base):
        self.eng, self.sem, self.base, self.n = eng, sem, base, 0

    def mark(self, ins):
        self.n += 1
        ins.then_inc(self.sem, 1)

    def wait(self):
        self.eng.wait_ge(self.sem, self.base + self.n)

    def link(self, ins):
        self.mark(ins)
        self.wait()


def stand(eng, passed):
    eng.sem_inc(passed, 1)


def at_least(eng, sem, count):
    if isinstance(count, int) and count <= 0:
        return
    eng.wait_ge(sem, count)


class Alloc:

    def __init__(self, nc, ctx, tag):
        self.nc, self.ctx, self.tag, self.sems = nc, ctx, tag, []
        ctx.callback(self.finish)

    def sb(self, name, shape, dt=F32):
        return self.ctx.enter_context(self.nc.sbuf_tensor(self.tag + name, shape, dt))

    def ps(self, name, shape, dt=F32):
        return self.ctx.enter_context(self.nc.psum_tensor(self.tag + name, shape, dt))

    def sem(self, name):
        self.sems.append(self.nc.alloc_semaphore(self.tag + name))
        return self.sems[-1]

    def finish(self):
        self.nc.clear_and_free_semaphores(self.sems)
        self.nc.all_engine_barrier()

    def store_sem(self, name):
        return self.nc.alloc_semaphore(self.tag + name)


def rows(ap, t):
    return ap[bass.ds(t * P, P), :]


class BiasRows:

    def __init__(self, m, name, n):
        self.raw = m.sb(name + "_raw", [BR, n])
        self.part = m.sb(name + "_part", [BR, n], BF16)
        self.rows = m.sb(name + "_rows", [BR, n], BF16)

    def split(self, dve, sem, base=0):
        v, raw, part, rows = dve, self.raw, self.part, self.rows
        st = Steps(dve, sem, base)
        st.link(v.memset(rows[:], 0.0))
        for n in range(2):
            st.link(v.tensor_copy(part[:], raw[:]))
            st.link(v.tensor_copy(rows[32 * n:32 * n + 1, :], part[32 * n:32 * n + 1, :]))
            st.link(v.tensor_tensor(raw[:], raw[:], part[:], ALU.subtract))
        st.link(v.tensor_copy(rows[64:65, :], raw[64:65, :]))
        return st.n


def attention(nc, x, xT, W_attn, b_attn, W_proj, b_proj, tri, blockdiag, eye, x1):
    with ExitStack() as ctx:
        m = Alloc(nc, ctx, "a_")
        w = m.sb("w", [P, KD, 3 * D])
        wp = m.sb("wp", [P, KD, D])
        bias_attn, bias_proj = BiasRows(m, "bias_attn", 3 * D), BiasRows(m, "bias_proj", D)
        ba, bp = bias_attn.rows, bias_proj.rows
        trib = m.sb("trib", [P, P])
        bd = m.sb("bd", [P, 4 * VW])
        ident = m.sb("ident", [P, P])
        ones = m.sb("ones", [BR, P], BF16)
        eps = m.sb("eps", [P, 1])
        xt = m.sb("xt", [P, 2, KD, P])
        xr = m.sb("xr", [P, 2, D])
        neg = m.sb("neg", [P, 8, P])
        ex = m.sb("ex", [P, 8, P])
        phi = m.sb("phi", [P, 8, P])
        kk = m.sb("kk", [P, D])
        vv = m.sb("vv", [P, H, VW])
        am = m.sb("am", [P, 4, 4, P])
        kv = m.sb("kv", [P, G, 4 * VW])
        kvn = m.sb("kvn", [P, G, 4 * VW])
        den = m.sb("den", [P, H])
        y = m.sb("y", [P, D])
        yT = m.sb("yT", [P, KD, P])
        res = m.sb("res", [P, D])
        stats = m.sb("stats", [P, 6])
        mv = m.sb("mv", [P, 2])
        std = m.sb("std", [P, 1])
        rstd = m.sb("rstd", [P, 1])
        out = m.sb("out", [P, 2, D])
        p_z = m.ps("p_z", [P, 8, P])
        p_v = m.ps("p_v", [P, D])
        p_k = m.ps("p_k", [P, D])
        p_a = m.ps("p_a", [P, 4, 4, P])
        p_n = p_z[:, :, :].rearrange("p a b -> p (a b)").rearrange("p (u n) -> p u n", u=2)
        p_kv = p_a[:, 0:2, :, :].rearrange("p a b c -> p a (b c)")
        p_yT = p_v
        p_o = p_k

        (weights_in, consts, z_done, neg_done, exp_done, phi_done, v_done, v_copied, kT_done, k_copied,
         a_done, a_masked, num_done, y_ready, kv_done, kv_ready, kv_clear, yT_done, yT_copied, o_done,
         var_ready, std_ready, out_ready, dve_step, passed, bias_step) = [
            m.sem(n) for n in (
                "weights_in consts z_done neg_done exp_done phi_done v_done v_copied kT_done k_copied "
                "a_done a_masked num_done y_ready kv_done kv_ready kv_clear yT_done yT_copied o_done "
                "var_ready std_ready out_ready dve_step passed bias_step").split()]
        x_in = [m.sem(f"x_in{u}") for u in range(2)]
        x1_out = [m.store_sem(f"x1_out{u}") for u in range(2)]
        PAIRS = TOK // P // 2
        block = ctx.enter_context(nc.Block())

        def tiles(eng, start, tile):
            def pair(b, i):
                for u in range(2):
                    tile(b, i, u, not (isinstance(i, int) and u == 1))

            with eng.Fori(0, B - 1) as b:
                start(b)
                with eng.Fori(0, CH // 2) as c:
                    pair(b, b * (CH // 2) + c)
            start(B - 1)
            with eng.Fori(PAIRS - CH // 2, PAIRS - 1) as i:
                pair(B - 1, i)
            pair(B - 1, PAIRS - 1)

        @block.sync
        def _(sp):
            def load(u, col):
                sp.dma_start(xt[:, u], xT.rearrange("(k p) n -> p k n", p=P)[:, :, bass.ds(col, P)]).then_inc(x_in[u], 16)
                sp.dma_start(xr[:, u, :], x[bass.ds(col, P), :]).then_inc(x_in[u], 16)

            for u in range(2):
                load(u, u * P)
            for dst, src in ((w[:], W_attn.rearrange("(k p) n -> p k n", p=P)),
                             (wp[:], W_proj.rearrange("(k p) n -> p k n", p=P)),
                             (bias_attn.raw[:], b_attn.rearrange("(a n) -> a n", a=1).to_broadcast([BR, 3 * D])),
                             (bias_proj.raw[:], b_proj.rearrange("(a n) -> a n", a=1).to_broadcast([BR, D])),
                             (trib[:], tri), (bd[:], blockdiag), (ident[:], eye)):
                sp.dma_start(dst, src).then_inc(weights_in, 16)
            with sp.Fori(0, PAIRS - 1) as i:
                for u in range(2):
                    done = sp.snap(i * 2 + (u + 1))
                    col = sp.snap(i * (2 * P) + (u + 2) * P)
                    sp.wait_ge(var_ready, done)
                    load(u, col)

        @block.gpsimd
        def _(pool):
            pool.memset(ones[:], 1.0).then_inc(consts, 1)
            pool.memset(eps[:], LN_EPS).then_inc(consts, 1)
            pool.memset(vv[:], 1.0).then_inc(consts, 1)
            with pool.Fori(0, PAIRS) as i:
                for u in range(2):
                    pool.wait_ge(out_ready, i * 2 + (u + 1))
                    pool.dma_start(x1[bass.ds(i * (2 * P) + u * P, P), :], out[:, u, :]).then_inc(x1_out[u], 16)
            for u in range(2):
                pool.wait_ge(x1_out[u], 16 * PAIRS)

        @block.tensor
        def _(pe):
            pe.wait_ge(weights_in, 16 * 7)
            pe.wait_ge(consts, 3)
            mm = nc.tensor.matmul

            def z(i, u):
                t = i * 2 + u
                pe.wait_ge(x_in[u], i * 32 + 32)
                at_least(pe, y_ready, t)
                for f in range(8):
                    for k in range(KD):
                        mm(p_z[:, f, :], w[:, k, f * P:(f + 1) * P], xt[:, u, k, :],
                           start=(f % 4 == 0 and k == 0), stop=False, skip_group_check=True)
                    last = mm(p_z[:, f, :], ba[:, f * P:(f + 1) * P], ones[:], start=False,
                              stop=(f % 4 == 3), skip_group_check=True)
                last.then_inc(z_done, 1)

            def values(i, u):
                at_least(pe, yT_copied, i * 2 + u)
                for k in range(KD):
                    mm(p_v[:], xt[:, u, k, :], w[:, k, 2 * D:], start=(k == 0), stop=False)
                mm(p_v[:], ones[:], ba[:, 2 * D:], start=False, stop=True).then_inc(v_done, 1)

            def tile(b, i, u, more):
                t = i * 2 + u
                ahead = (i + u, 1 - u)
                pe.wait_ge(phi_done, t + 1)
                at_least(pe, var_ready, t)
                for g in range(G):
                    last = nc.tensor.transpose(p_k[:, g * P:(g + 1) * P], phi[:, 4 + g, :], ident[:])
                last.then_inc(kT_done, 1)
                at_least(pe, kv_ready, t)
                for g in range(G):
                    for r in range(4):
                        last = mm(p_a[:, r, g, :], phi[32 * r:32 * r + 32, 4 + g, :],
                                  phi[32 * r:32 * r + 32, g, :], start=True, stop=True,
                                  skip_group_check=True)
                last.then_inc(a_done, 1)
                pe.wait_ge(kv_clear, b + 1)
                for g in range(G):
                    mm(p_n[:, g // 2, (g % 2) * 4 * VW:(g % 2 + 1) * 4 * VW], phi[:, g, :], kv[:, g, :],
                       start=(g % 2 == 0), stop=False, skip_group_check=True)
                pe.wait_ge(v_copied, t + 1)
                pe.wait_ge(a_masked, t + 1)
                for h in range(H):
                    last = mm(p_n[:, h // 8, (h % 8) * VW:(h % 8 + 1) * VW], am[:, h % 4, h // 4, :],
                              vv[:, h, :], start=False, stop=(h % 8 == 7), skip_group_check=True)
                last.then_inc(num_done, 1)
                pe.wait_ge(k_copied, t + 1)
                for g in range(G):
                    last = mm(p_kv[:, g // 2, (g % 2) * 4 * VW:(g % 2 + 1) * 4 * VW],
                              kk[:, g * P:(g + 1) * P], vv[:, 4 * g:4 * g + 4, :],
                              start=(g % 2 == 0), stop=(g % 2 == 1), skip_group_check=True)
                last.then_inc(kv_done, 1)
                pe.wait_ge(y_ready, t + 1)
                for g in range(KD):
                    last = nc.tensor.transpose(p_yT[:, g * P:(g + 1) * P], y[:, g * P:(g + 1) * P], ident[:])
                last.then_inc(yT_done, 1)
                if more:
                    z(*ahead)
                pe.wait_ge(yT_copied, t + 1)
                for k in range(KD):
                    mm(p_o[:], yT[:, k, :], wp[:, k, :], start=(k == 0), stop=False)
                mm(p_o[:], ones[:], bp[:], start=False, stop=True).then_inc(o_done, 1)
                if more:
                    values(*ahead)

            pe.wait_ge(bias_step, 16)
            z(0, 0)
            values(0, 0)
            tiles(pe, lambda b: None, tile)

        @block.scalar
        def _(act):
            act.wait_ge(consts, 3)
            a = nc.scalar.activation

            def exps(t):
                act.wait_ge(neg_done, t + 1)
                a(ex[:], neg[:], ACT.Exp).then_inc(exp_done, 1)

            def copy_v(t):
                act.wait_ge(v_done, t + 1)
                at_least(act, kv_done, t)
                a(vv[:, :, 0:DH], p_v[:].rearrange("p (h d) -> p h d", h=H), ACT.Copy).then_inc(v_copied, 1)

            def tile(b, i, u, more):
                t = i * 2 + u
                act.wait_ge(kT_done, t + 1)
                a(kk[:], p_k[:], ACT.Copy).then_inc(k_copied, 1)
                act.wait_ge(yT_done, t + 1)
                at_least(act, o_done, t)
                a(yT[:].rearrange("p a b -> p (a b)"), p_yT[:], ACT.Copy).then_inc(yT_copied, 1)
                if more:
                    exps(t + 1)
                act.wait_ge(var_ready, t + 1)
                a(std[:], mv[:, 1:2], ACT.Sqrt, bias=eps[:]).then_inc(std_ready, 1)
                if more:
                    copy_v(t + 1)

            exps(0)
            copy_v(0)
            tiles(act, lambda b: None, tile)

        @block.vector
        def _(dve):
            v = nc.vector
            dve.wait_ge(weights_in, 16 * 7)
            dve.wait_ge(consts, 3)
            NSTEP = 8

            def features(t):
                dve.wait_ge(z_done, t + 1)
                v.tensor_scalar(neg[:], p_z[:], 0.0, None, ALU.min).then_inc(neg_done, 1)
                dve.wait_ge(exp_done, t + 1)
                v.scalar_tensor_tensor(phi[:], p_z[:], 0.0, ex[:], ALU.max, ALU.add).then_inc(phi_done, 1)

            def tile(b, i, u, more):
                t = i * 2 + u
                s = Steps(dve, dve_step, t * NSTEP)
                dve.wait_ge(a_done, t + 1)
                v.tensor_tensor(am[:].rearrange("p a b c -> p (a b) c"),
                                p_a[:].rearrange("p a b c -> p (a b) c"),
                                trib[:].unsqueeze(1).to_broadcast([P, 16, P]),
                                ALU.mult).then_inc(a_masked, 1)
                dve.wait_ge(num_done, t + 1)
                nd = p_n[:, :, 0:8 * VW].rearrange("p u (h e) -> p u h e", e=VW)
                dv = den[:].rearrange("p (u h) -> p u h", u=2)
                s.link(v.tensor_scalar(dv, nd[:, :, :, DH], 1e-6, None, ALU.add))
                s.link(v.reciprocal(den[:], den[:]))
                for q in range(2):
                    last = v.tensor_tensor(y[:, 256 * q:256 * q + 256].rearrange("p (h d) -> p h d", d=DH),
                                           nd[:, q, :, 0:DH],
                                           den[:, 8 * q:8 * q + 8].unsqueeze(2).to_broadcast([P, 8, DH]), ALU.mult)
                    if q == 0:
                        s.link(last)
                last.then_inc(y_ready, 1)
                dve.wait_ge(kv_done, t + 1)
                for q in range(2):
                    s.link(v.tensor_tensor(kvn[:, 2 * q:2 * q + 2, :],
                                           p_kv[:, q, 0:8 * VW].rearrange("p (a b) -> p a b", a=2),
                                           bd[:].unsqueeze(1).to_broadcast([P, 2, 4 * VW]), ALU.mult))
                v.tensor_tensor(kv[:], kv[:], kvn[:], ALU.add).then_inc(kv_ready, 1)
                if more:
                    features(t + 1)
                dve.wait_ge(o_done, t + 1)
                s.link(v.tensor_tensor(res[:], p_o[:], xr[:, u, :], ALU.add))
                s.link(v.bn_stats(stats[:], res[:]))
                stand(dve, passed)
                v.bn_aggr(mv[:], stats[:]).then_inc(var_ready, 1)
                dve.wait_ge(std_ready, t + 1)
                s.link(v.reciprocal(rstd[:], std[:]))
                at_least(dve, x1_out[u], i * 16)
                v.tensor_scalar(out[:, u, :], res[:], mv[:, 0:1], rstd[:], ALU.subtract,
                                ALU.mult).then_inc(out_ready, 1)
                dve.wait_ge(out_ready, t + 1)
                dve.wait_ge(kv_ready, t + 1)
                assert s.n == NSTEP, s.n

            def start(b):
                v.memset(kv[:], 0.0).then_inc(kv_clear, 1)
                dve.wait_ge(kv_clear, b + 1)
                stand(dve, passed)

            base = bias_attn.split(dve, bias_step)
            bias_proj.split(dve, bias_step, base)
            features(0)
            tiles(dve, start, tile)


N2, DV, NH2 = 2048, 384, 4
KV3 = DV // P
HS = P // NH2
GB = N2 // P
NEG = -3.0e38


def prepare(nc, ctxT, Wk, WvT, W_film_in, b_film_in, W_film_out, b_film_out, gate, mask2, keysT, film_w, film_b, mask_row):
    with ExitStack() as ctx:
        m = Alloc(nc, ctx, "p_")
        wk = m.sb("wk", [P, KV3, P])
        ct = m.sb("ct", [P, 2, KV3, 512])
        ko = m.sb("ko", [P, 2, 512])
        wv = m.sb("wv", [P, KD, DV])
        wf = m.sb("wf", [P, KD, 4 * D])
        fo = m.sb("fo", [P, KV3, 4 * D])
        g = m.sb("g", [P, 1])
        fb = m.sb("fb", [1, 4 * D])
        m8 = m.sb("m8", [B, N2], U8)
        mf = m.sb("mf", [B, N2])
        mb = m.sb("mb", [B, N2], BF16)
        p_k = m.ps("p_k", [P, 2, 512])
        p_f = m.ps("p_f", [P, 2, 512])
        weights_in, k_done, k_copied, f_done, f_copied, m_step = [
            m.sem(n) for n in "weights_in k_done k_copied f_done f_copied m_step".split()]
        stored = m.store_sem("stored")
        c_in = [m.sem(f"c_in{u}") for u in range(2)]
        k_out = [m.store_sem(f"k_out{u}") for u in range(2)]
        NC = B * N2 // 512
        block = ctx.enter_context(nc.Block())

        @block.sync
        def _(sp):
            src = ctxT.rearrange("(k p) n -> p k n", p=P)
            sp.dma_start(wk[:], Wk.rearrange("(k p) n -> p k n", p=P)).then_inc(weights_in, 16)
            for u in range(2):
                sp.dma_start(ct[:, u], src[:, :, 512 * u:512 * u + 512]).then_inc(c_in[u], 16)
            sp.dma_start(wv[:], WvT.rearrange("(k p) n -> p k n", p=P)).then_inc(weights_in, 16)
            sp.dma_start(wf[:, :, 0:2 * D], W_film_in.rearrange("(k p) n -> p k n", p=P)).then_inc(weights_in, 16)
            sp.dma_start(wf[:, :, 2 * D:], W_film_out.rearrange("(k p) n -> p k n", p=P)).then_inc(weights_in, 16)
            sp.dma_start(g[:], gate.to_broadcast([P, 1])).then_inc(weights_in, 16)
            sp.dma_start(fb[:, 0:2 * D], b_film_in.rearrange("(a n) -> a n", a=1)).then_inc(weights_in, 16)
            sp.dma_start(fb[:, 2 * D:], b_film_out.rearrange("(a n) -> a n", a=1)).then_inc(weights_in, 16)
            sp.dma_start(m8[:], mask2).then_inc(weights_in, 16)
            with sp.Fori(0, NC // 2 - 1) as i:
                for u in range(2):
                    done = sp.snap(i * 2 + (u + 1))
                    col = sp.snap(i * 1024 + (u + 2) * 512)
                    sp.wait_ge(k_done, done)
                    sp.dma_start(ct[:, u], src[:, :, bass.ds(col, 512)]).then_inc(c_in[u], 16)

        @block.gpsimd
        def _(pool):
            with pool.Fori(0, NC // 2) as i:
                for u in range(2):
                    pool.wait_ge(k_copied, i * 2 + (u + 1))
                    pool.dma_start(keysT[:, bass.ds(i * 1024 + u * 512, 512)], ko[:, u, :]).then_inc(k_out[u], 16)
            pool.wait_ge(m_step, 4)
            pool.dma_start(film_b, fb[:]).then_inc(stored, 16)
            pool.dma_start(mask_row, mb[:]).then_inc(stored, 16)
            pool.wait_ge(f_copied, 12)
            pool.dma_start(film_w.rearrange("(k p) n -> p k n", p=P), fo[:]).then_inc(stored, 16)
            pool.wait_ge(stored, 48)
            for u in range(2):
                pool.wait_ge(k_out[u], 16 * (NC // 2))

        @block.tensor
        def _(pe):
            mm = nc.tensor.matmul
            pe.wait_ge(weights_in, 128)
            with pe.Fori(0, NC // 2) as i:
                for u in range(2):
                    pe.wait_ge(c_in[u], i * 16 + 16)
                    pe.wait_ge(k_copied, i * 2)
                    for k in range(KV3):
                        last = mm(p_k[:, u, :], wk[:, k, :], ct[:, u, k, :], start=(k == 0), stop=(k == KV3 - 1))
                    last.then_inc(k_done, 1)
            for n in range(12):
                r, c = n // 4, n % 4
                at_least(pe, f_copied, n - 1)
                for k in range(KD):
                    last = mm(p_f[:, n % 2, :], wv[:, k, r * P:(r + 1) * P], wf[:, k, c * 512:(c + 1) * 512],
                              start=(k == 0), stop=(k == KD - 1))
                last.then_inc(f_done, 1)

        @block.scalar
        def _(act):
            with act.Fori(0, NC // 2) as i:
                for u in range(2):
                    act.wait_ge(k_done, i * 2 + (u + 1))
                    act.wait_ge(k_out[u], i * 16)
                    nc.scalar.activation(ko[:, u, :], p_k[:, u, :], ACT.Copy).then_inc(k_copied, 1)

        @block.vector
        def _(dve):
            v = nc.vector
            dve.wait_ge(weights_in, 128)
            v.tensor_scalar(fb[:], fb[:], g[0:1, :], None, ALU.mult).then_inc(m_step, 1)
            v.tensor_copy(mf[:], m8[:]).then_inc(m_step, 1)
            dve.wait_ge(m_step, 2)
            v.tensor_scalar(mf[:], mf[:], -1.0, 3e38, ALU.add, ALU.mult).then_inc(m_step, 1)
            dve.wait_ge(m_step, 3)
            v.tensor_scalar(mb[:], mf[:], 10.0, None, ALU.mult).then_inc(m_step, 1)
            for n in range(12):
                dve.wait_ge(f_done, n + 1)
                v.tensor_scalar(fo[:, n // 4, (n % 4) * 512:(n % 4 + 1) * 512], p_f[:, n % 2, :], g[:], None,
                                ALU.mult).then_inc(f_copied, 1)


def cross(nc, x1, keysT, values, film_w, film_b, mask_row, text_mask, Wq, g_in, b_in, eye, xm, mod_out):
    with ExitStack() as ctx:
        m = Alloc(nc, ctx, "c_")
        SCALE = float(HS) ** -0.5
        wq = m.sb("wq", [P, KD, P])
        kt = m.sb("kt", [P, N2])
        vals = m.sb("vals", [P, GB, DV])
        wf = m.sb("wf", [P, KV3, 4 * D])
        fb = m.sb("fb", [1, 4 * D])
        mrow = m.sb("mrow", [P, N2], BF16)
        oneb = m.sb("oneb", [P, P], BF16)
        ones = m.sb("ones", [1, P])
        eps = m.sb("eps", [P, 1])
        tm8 = m.sb("tm8", [P, TOK // P], U8)
        tm = m.sb("tm", [P, TOK // P])
        gb = m.sb("gb", [P, 2, D])
        ident = m.sb("ident", [P, P])
        xt = m.sb("xt", [P, 2, D])
        xT = m.sb("xT", [P, D])
        qT = m.sb("qT", [P, P])
        s = m.sb("s", [P, 2, N2])
        z = m.sb("z", [P, 2, N2])
        e = m.sb("e", [P, 2, N2])
        ez = m.sb("ez", [P, N2])
        top = m.sb("top", [P, 2, 32])
        topx = m.sb("topx", [P, 32])
        nb = m.sb("nb", [P, 2])
        den = m.sb("den", [P, 2])
        rd = m.sb("rd", [P, 1])
        diag = m.sb("diag", [P, 2, P])
        aT = m.sb("aT", [P, GB, P])
        uT = m.sb("uT", [P, KV3, P])
        fi = m.sb("fi", [P, 2, D])
        fo = m.sb("fo", [P, 2, 2 * D])
        xl = m.sb("xl", [P, D])
        xo = m.sb("xo", [P, 2, D])
        stats = m.sb("stats", [P, 6])
        mv = m.sb("mv", [P, 2])
        std = m.sb("std", [P, 1])
        rstd = m.sb("rstd", [P, 1])
        p_s = m.ps("p_s", [P, 2, 512])
        p_a = m.ps("p_a", [P, GB, P])
        p_m = m.ps("p_m", [P, 2, 512])

        (weights_in, consts, keys_in, values_in, s_done, s_copied, s_read, nb_ready, z_done, e_done, ez_done,
         sum_done, w_ready, diag_ready, attn_done, aT_copied, uT_done, uT_copied, xT_done, xT_copied,
         q_done, q_copied, fi_done, fi_copied, fo_done, fo_copied, var_ready, std_ready, ln_done,
         xm_ready, passed, dve_step, pool_step) = [
            m.sem(n) for n in (
                "weights_in consts keys_in values_in s_done s_copied s_read nb_ready z_done e_done ez_done "
                "sum_done w_ready diag_ready attn_done aT_copied uT_done uT_copied xT_done xT_copied "
                "q_done q_copied fi_done fi_copied fo_done fo_copied var_ready std_ready ln_done "
                "xm_ready passed dve_step pool_step").split()]
        x_in = [m.sem(f"x_in{u}") for u in range(2)]
        fo_out = [m.store_sem(f"fo_out{u}") for u in range(2)]
        xm_out = [m.store_sem(f"xm_out{u}") for u in range(2)]
        TILES = TOK // P
        PAIRS = TILES // 2
        block = ctx.enter_context(nc.Block())

        def pairs(eng, pair):
            pair(0)
            with eng.Fori(1, PAIRS - 1) as i:
                pair(i)
            pair(PAIRS - 1)

        @block.sync
        def _(sp):
            def bc(ap, n):
                return ap.rearrange("(a n) -> a n", a=1).to_broadcast([P, n])
            for dst, src in ((wq[:], Wq.rearrange("(k p) n -> p k n", p=P)),
                             (wf[:], film_w.rearrange("(k p) n -> p k n", p=P)), (fb[:], film_b),
                             (tm8[:], text_mask), (gb[:, 0, :], bc(g_in, D)), (gb[:, 1, :], bc(b_in, D)),
                             (ident[:], eye)):
                sp.dma_start(dst, src).then_inc(weights_in, 16)
            vsrc = values.rearrange("(b j p) n -> b p j n", p=P, j=GB)

            def load_x(u, free, row):
                at_least(sp, ln_done, free)
                sp.dma_start(xt[:, u, :], x1[bass.ds(row, P), :]).then_inc(x_in[u], 16)

            def batch(b):
                snap = (lambda a: a) if isinstance(b, int) else sp.snap
                used, col = snap(b * (CH * NH2 * 4)), snap(b * N2)
                at_least(sp, s_done, used)
                sp.dma_start(kt[:], keysT[:, bass.ds(col, N2)]).then_inc(keys_in, 16)
                for h in range(NH2):
                    sp.dma_start(mrow[HS * h:HS * h + 1, :], mask_row[bass.ds(b, 1), :]).then_inc(keys_in, 16)
                got = snap(b * 80 + 80)
                sp.wait_ge(keys_in, got)
                sp.wait_ge(weights_in, 16 * 7)
                load_x(0, snap(b * CH - 1), snap(b * S))
                used, row = snap(b * CH), snap(b * N2)
                at_least(sp, uT_done, used)
                sp.dma_start(vals[:], vsrc[b] if isinstance(b, int) else vsrc[bass.ds(b, 1)].squeeze(0) ).then_inc(values_in, 16)
                got = snap(b * 16 + 16)
                sp.wait_ge(values_in, got)
                sp.wait_ge(weights_in, 16 * 7)
                load_x(1, snap(b * CH), snap(b * S + P))
                with sp.Fori(1, CH // 2) as c:
                    for u in range(2):
                        load_x(u, sp.snap(c * 2 + (b * CH + (u - 1))), sp.snap(c * (2 * P) + (b * S + u * P)))

            for b in range(B):
                batch(b)

        @block.tensor
        def _(pe):
            mm = nc.tensor.matmul
            pe.wait_ge(weights_in, 16 * 7)
            pe.wait_ge(consts, 4)

            def queries(t, i, u):
                pe.wait_ge(x_in[u], i * 16 + 16)
                at_least(pe, fo_copied, t - 1)
                for k in range(KD):
                    last = nc.tensor.transpose(p_m[:, 0, k * P:(k + 1) * P], xt[:, u, k * P:(k + 1) * P], ident[:])
                last.then_inc(xT_done, 1)
                pe.wait_ge(xT_copied, t + 1)
                for k in range(KD):
                    last = mm(p_m[:, 1, 0:P], wq[:, k, :], xT[:, k * P:(k + 1) * P], start=(k == 0), stop=(k == KD - 1))
                last.then_inc(q_done, 1)
                pe.wait_ge(q_copied, t + 1)

            def scores(j, h):
                for c in range(4):
                    at_least(pe, s_copied, j * 4 + (c - 1))
                    mm(p_s[:, c % 2, :], qT[HS * h:HS * h + HS, :], kt[HS * h:HS * h + HS, c * 512:(c + 1) * 512],
                       start=True, stop=False)
                    mm(p_s[:, c % 2, :], oneb[HS * h:HS * h + 1, :], mrow[HS * h:HS * h + 1, c * 512:(c + 1) * 512],
                       start=False, stop=True).then_inc(s_done, 1)

            def attn(t, j, h):
                pe.wait_ge(diag_ready, j + 1)
                pe.wait_ge(w_ready, j + 1)
                at_least(pe, aT_copied, t)
                for n in range(GB):
                    last = mm(p_a[:, n, :], e[:, h % 2, n * P:(n + 1) * P], diag[:, h % 2, :],
                              start=(h == 0 and n % 4 == 0), stop=(h == NH2 - 1 and n % 4 == 3),
                              skip_group_check=True)
                last.then_inc(attn_done, 1)

            def context(t):
                pe.wait_ge(aT_copied, t + 1)
                for k in range(KV3):
                    for n in range(GB):
                        last = mm(p_m[:, 0, k * P:(k + 1) * P], vals[:, n, k * P:(k + 1) * P], aT[:, n, :],
                                  start=(k == 0 and n == 0), stop=(k == KV3 - 1 and n == GB - 1),
                                  skip_group_check=True)
                last.then_inc(uT_done, 1)

            def film(t, part):
                if part == 0:
                    pe.wait_ge(uT_copied, t + 1)
                else:
                    pe.wait_ge(fi_copied, t + 1)
                for n in range(2):
                    c = 2 * part + n
                    for k in range(KV3):
                        mm(p_m[:, n, :], uT[:, k, :], wf[:, k, c * D:(c + 1) * D], start=(k == 0), stop=False)
                    last = mm(p_m[:, n, :], ones[:], fb[:, c * D:(c + 1) * D], start=False, stop=True)
                last.then_inc(fo_done if part else fi_done, 1)

            def extra(t, h):
                if h == 0:
                    context(t)
                elif h < 3:
                    film(t, h - 1)

            def pair(i):
                for u in range(2):
                    t = i * 2 + u
                    for h in range(NH2):
                        j = t * 4 + h
                        if h < NH2 - 1:
                            scores(j + 1, h + 1)
                        elif not (isinstance(t, int) and t == TILES - 1):
                            queries(t + 1, i + u, 1 - u)
                            scores(j + 1, 0)
                        if not (isinstance(t, int) and t == 0):
                            extra(t - 1, h)
                        attn(t, j, h)

            queries(0, 0, 0)
            scores(0, 0)
            pairs(pe, pair)
            for h in range(3):
                extra(TILES - 1, h)

        @block.scalar
        def _(act):
            a = nc.scalar.activation
            act.wait_ge(consts, 4)

            def copy_q(t):
                act.wait_ge(xT_done, t + 1)
                a(xT[:], p_m[:, 0, :], ACT.Copy).then_inc(xT_copied, 1)
                act.wait_ge(q_done, t + 1)
                a(qT[:], p_m[:, 1, 0:P], ACT.Copy).then_inc(q_copied, 1)

            def copy_s(j, par):
                at_least(act, s_read, j - 1)
                for c in range(4):
                    act.wait_ge(s_done, j * 4 + (c + 1))
                    a(s[:, par, c * 512:(c + 1) * 512], p_s[:, c % 2, :], ACT.Copy).then_inc(s_copied, 1)

            def exps(j, par):
                act.wait_ge(nb_ready, j + 1)
                at_least(act, attn_done, j - 1)
                a(e[:, par, :], s[:, par, :], ACT.Exp, bias=nb[:, par:par + 1], scale=SCALE).then_inc(e_done, 1)
                act.wait_ge(z_done, j + 1)
                at_least(act, w_ready, j)
                a(ez[:], z[:, par, :], ACT.Exp, bias=nb[:, par:par + 1], scale=SCALE).then_inc(ez_done, 1)
                at_least(act, diag_ready, j - 1)
                a(topx[:], top[:, par, :], ACT.Exp, bias=nb[:, par:par + 1], scale=SCALE,
                  accum_out=den[:, par:par + 1]).then_inc(sum_done, 1)

            def extra(t, i, u, h):
                if h == 0:
                    act.wait_ge(uT_done, t + 1)
                    a(uT[:].rearrange("p a b -> p (a b)"), p_m[:, 0, 0:DV], ACT.Copy).then_inc(uT_copied, 1)
                elif h == 1:
                    act.wait_ge(fi_done, t + 1)
                    at_least(act, xm_ready, t)
                    a(fi[:], p_m[:], ACT.Copy).then_inc(fi_copied, 1)
                elif h == 2:
                    act.wait_ge(fo_done, t + 1)
                    at_least(act, fo_out[u], i * 16)
                    a(fo[:, u, :].rearrange("p (a b) -> p a b", a=2), p_m[:], ACT.Copy).then_inc(fo_copied, 1)

            def pair(i):
                for u in range(2):
                    t = i * 2 + u
                    for h in range(NH2):
                        j = t * 4 + h
                        if h < NH2 - 1:
                            copy_s(j + 1, (h + 1) % 2)
                        elif not (isinstance(t, int) and t == TILES - 1):
                            copy_q(t + 1)
                            copy_s(j + 1, 0)
                        exps(j, h % 2)
                        if h == 3:
                            act.wait_ge(attn_done, t * 4 + 4)
                            a(aT[:], p_a[:], ACT.Copy).then_inc(aT_copied, 1)
                        elif not (isinstance(t, int) and t == 0):
                            extra(t - 1, i - (1 - u), 1 - u, h)
                        if h == 1:
                            act.wait_ge(var_ready, t + 1)
                            a(std[:], mv[:, 1:2], ACT.Sqrt, bias=eps[:]).then_inc(std_ready, 1)

            copy_q(0)
            copy_s(0, 0)
            pairs(act, pair)
            for h in range(3):
                extra(TILES - 1, PAIRS - 1, 1, h)

        @block.vector
        def _(dve):
            v = nc.vector
            v.memset(oneb[:], 1.0).then_inc(consts, 1)
            v.memset(ones[:], 1.0).then_inc(consts, 1)
            v.memset(eps[:], LN_EPS).then_inc(consts, 1)
            dve.wait_ge(weights_in, 16 * 7)
            v.tensor_copy(tm[:], tm8[:]).then_inc(consts, 1)
            dve.wait_ge(consts, 4)
            HSTEP = 9
            TSTEP = NH2 * HSTEP + 2

            def scale_last(st, t, j, par):
                dve.wait_ge(sum_done, j + 1)
                st.link(v.reciprocal(rd[:], den[:, par:par + 1]))
                st.link(v.tensor_scalar(rd[:], rd[:], 1.0 / NH2, tm[:, t:t + 1] if isinstance(t, int) else tm[:, bass.ds(t, 1)],
                                        ALU.mult, ALU.mult))
                at_least(dve, attn_done, j - 1)
                v.tensor_scalar(diag[:, par, :], ident[:], rd[:], None, ALU.mult).then_inc(diag_ready, 1)

            def pair(i):
                for u in range(2):
                    t = i * 2 + u
                    for h in range(NH2):
                        j = t * 4 + h
                        par = h % 2
                        st = Steps(dve, dve_step, t * TSTEP + (HSTEP * h + max(h - 1, 0)))
                        best = lambda n: top[:, par, 8 * n:8 * n + 8]
                        dve.wait_ge(s_copied, j * 4 + 4)
                        stand(dve, passed)
                        st.link(v.max(best(0), s[:, par, :]))
                        v.tensor_scalar(nb[:, par:par + 1], best(0)[:, 0:1], -SCALE, None, ALU.mult).then_inc(nb_ready, 1)
                        at_least(dve, ez_done, j - 1)
                        stand(dve, passed)
                        v.match_replace(z[:, par, :], best(0), s[:, par, :], NEG).then_inc(s_read, 1)
                        dve.wait_ge(s_read, j + 1)
                        if not (isinstance(j, int) and j == 0):
                            scale_last(st, t - 1 if h == 0 else t, j - 1, 1 - par)
                        else:
                            for _ in range(2):
                                st.link(v.memset(rd[:], 0.0))
                        for n in range(1, 4):
                            stand(dve, passed)
                            st.link(v.max(best(n), z[:, par, :]))
                            stand(dve, passed)
                            last = v.match_replace(z[:, par, :], best(n), z[:, par, :], NEG)
                            if n < 3:
                                st.link(last)
                        last.then_inc(z_done, 1)
                        assert st.n == HSTEP - 1, st.n
                        st.link(v.tensor_copy(rd[:], rd[:]))
                        if h == 1:
                            dve.wait_ge(x_in[u], i * 16 + 16)
                            st.link(v.bn_stats(stats[:], xt[:, u, :]))
                            stand(dve, passed)
                            v.bn_aggr(mv[:], stats[:]).then_inc(var_ready, 1)
                        if h == 2:
                            dve.wait_ge(std_ready, t + 1)
                            st.link(v.reciprocal(rstd[:], std[:]))
                            at_least(dve, xm_ready, t)
                            v.tensor_scalar(xl[:], xt[:, u, :], mv[:, 0:1], rstd[:], ALU.subtract, ALU.mult).then_inc(ln_done, 1)
                            dve.wait_ge(ln_done, t + 1)

            pairs(dve, pair)
            st = Steps(dve, dve_step, TILES * TSTEP)
            scale_last(st, TILES - 1, TILES * 4 - 1, 1)

        @block.gpsimd
        def _(pool):
            pool.wait_ge(weights_in, 16 * 7)

            def modulate(t, i, u):
                st = Steps(pool, pool_step, t * 4)
                pool.wait_ge(ln_done, t + 1)
                st.link(pool.tensor_tensor(xl[:], xl[:], gb[:, 0, :], ALU.mult))
                st.link(pool.tensor_tensor(xl[:], xl[:], gb[:, 1, :], ALU.add))
                pool.wait_ge(fi_copied, t + 1)
                at_least(pool, xm_out[u], i * 16)
                st.link(pool.tensor_tensor(xo[:, u, :], xl[:], fi[:, 0, :], ALU.mult))
                st.link(pool.tensor_tensor(xo[:, u, :], xo[:, u, :], fi[:, 1, :], ALU.add))
                pool.tensor_tensor(xo[:, u, :], xo[:, u, :], xl[:], ALU.add).then_inc(xm_ready, 1)
                pool.wait_ge(xm_ready, t + 1)
                pool.dma_start(xm[bass.ds(t * P, P), :], xo[:, u, :]).then_inc(xm_out[u], 16)

            def store_mod(t, u):
                pool.wait_ge(fo_copied, t + 1)
                pool.dma_start(mod_out[bass.ds(t * P, P), :], fo[:, u, :]).then_inc(fo_out[u], 16)

            def pair(i):
                for u in range(2):
                    t = i * 2 + u
                    for h in range(NH2):
                        j = t * 4 + h
                        pool.wait_ge(e_done, j + 1)
                        pool.wait_ge(ez_done, j + 1)
                        pool.tensor_tensor(e[:, h % 2, :], e[:, h % 2, :], ez[:], ALU.subtract).then_inc(w_ready, 1)
                        if not (isinstance(t, int) and t == 0):
                            if h == 1:
                                modulate(t - 1, i - (1 - u), 1 - u)
                            if h == 2:
                                store_mod(t - 1, 1 - u)

            pairs(pool, pair)
            modulate(TILES - 1, PAIRS - 1, 1)
            store_mod(TILES - 1, 1)
            for u in range(2):
                pool.wait_ge(xm_out[u], 16 * PAIRS)
                pool.wait_ge(fo_out[u], 16 * PAIRS)


NS = 64
HALF = S // 32
DCH = 64
LOG = 10
LN2_HI = 0.693145751953125
MAGIC = 12582912.0
TWO_PI = 6.283185


def ssm_kernel(nc, log_dt, A_re, A_im, C_re, C_im, cst, conv_k):
    with ExitStack() as ctx:
        m = Alloc(nc, ctx, "k_")
        ld = m.sb("ld", [P, D])
        are, aim, cre, cim = (m.sb(n, [P, D]) for n in "are aim cre cim".split())
        cs = m.sb("cs", [P, 6 + 64])
        t = [m.sb(f"t{n}", [P, D]) for n in range(8)]
        th = m.sb("th", [P, 2, D])
        grow = m.sb("grow", [P, LOG, D])
        ar, tau, dcr, dci = (m.sb(n, [P, D]) for n in "ar tau dcr dci".split())
        x = m.sb("x", [P, DCH, 32])
        f = [m.sb(f"f{n}", [P, DCH, 32]) for n in range(3)]
        ea = m.sb("ea", [P, 2, DCH, 32])
        sn = [m.sb(f"sn{n}", [P, DCH, 32]) for n in range(3)]
        U = m.sb("U", [P, DCH, 32])
        W = m.sb("W", [P, DCH, 32])
        W2 = m.sb("W2", [P, DCH, 32])
        ko = m.sb("ko", [32, DCH, 32])
        p_k = m.ps("p_k", [32, DCH, 32])
        params_in, angles_ready, sines_done, step, u_ready, w_ready, k_done, k_copied, k_out, arg_ready, sin_done, th_done, th_used, w_half, passed = [
            m.sem(n) for n in "params_in angles_ready sines_done step u_ready w_ready k_done k_copied k_out arg_ready sin_done th_done th_used w_half passed".split()]
        NCHUNK = D // DCH
        offs = {"u": cs[:, 0:1], "w1": cs[:, 1:2], "w2": cs[:, 2:3]}
        bias = {"u": cs[:, 3:4], "w1": cs[:, 4:5], "w2": cs[:, 5:6]}
        la, lb = cs[:, 6:38], cs[:, 38:70]
        block = ctx.enter_context(nc.Block())

        @block.sync
        def _(sp):
            sp.dma_start(ld[:], log_dt.rearrange("(a n) -> a n", a=1).to_broadcast([P, D])).then_inc(params_in, 16)
            for dst, src in ((are, A_re), (aim, A_im), (cre, C_re), (cim, C_im)):
                for part in range(2):
                    sp.dma_start(dst[NS * part:NS * part + NS, :], src).then_inc(params_in, 16)
            sp.dma_start(cs[:], cst).then_inc(params_in, 16)
            with sp.Fori(0, NCHUNK) as c:
                done, row = sp.snap(c + 1), sp.snap(c * DCH)
                sp.wait_ge(k_copied, done)
                sp.dma_start(conv_k[bass.ds(row, DCH), :].rearrange("d (a b) -> a d b", b=32), ko[:]).then_inc(k_out, 16)
            sp.wait_ge(k_out, 16 * NCHUNK)

        @block.scalar
        def _(act):
            a = nc.scalar.activation
            act.wait_ge(params_in, 160)
            act.wait_ge(angles_ready, 1)
            for k in range(LOG):
                at_least(act, th_used, k - 1)
                a(th[:, k % 2, :], ar[:], ACT.Tanh, scale=0.5 * 2 ** k).then_inc(th_done, 1)
            act.wait_ge(angles_ready, 4)
            for n in (1, 2, 7):
                a(t[n][:], t[n][:], ACT.Sin, scale=TWO_PI).then_inc(sines_done, 1)
            with act.Fori(0, NCHUNK) as c:
                for n, key in enumerate(("u", "w1", "w2")):
                    act.wait_ge(arg_ready, c * 3 + (n + 1))
                    a(sn[n][:], f[n][:], ACT.Sin, bias=bias[key], scale=-TWO_PI).then_inc(sin_done, 1)
                act.wait_ge(k_out, c * 16)
                act.wait_ge(k_done, c + 1)
                a(ko[:], p_k[:], ACT.Copy).then_inc(k_copied, 1)

        @block.tensor
        def _(pe):
            with pe.Fori(0, NCHUNK) as c:
                pe.wait_ge(u_ready, c + 1)
                pe.wait_ge(w_ready, c + 1)
                pe.wait_ge(k_copied, c)
                for d in range(DCH):
                    last = nc.tensor.matmul(p_k[:, d, :], U[:, d, :], W[:, d, :], start=True, stop=True,
                                            skip_group_check=True)
                last.then_inc(k_done, 1)

        @block.vector
        def _(dve):
            v = nc.vector
            dve.wait_ge(params_in, 160)
            st = Steps(dve, step, 0)
            tt, ts = v.tensor_tensor, v.tensor_scalar
            ki = t[6][:].bitcast(mybir.dt.int32)
            st.link(ts(t[3][:], ld[:], 1.0 / math.log(2.0), MAGIC, ALU.mult, ALU.add))
            st.link(ts(t[3][:], t[3][:], MAGIC, None, ALU.subtract))
            st.link(v.scalar_tensor_tensor(t[4][:], t[3][:], -LN2_HI, ld[:], ALU.mult, ALU.add))
            st.link(v.scalar_tensor_tensor(t[4][:], t[3][:], LN2_HI - math.log(2.0), t[4][:], ALU.mult, ALU.add))
            st.link(ts(t[5][:], t[4][:], 1.0 / math.factorial(8), None, ALU.mult))
            for n in range(7, 0, -1):
                st.link(v.scalar_tensor_tensor(t[5][:], t[5][:], 1.0 / math.factorial(n), t[4][:], ALU.add, ALU.mult))
            st.link(ts(ki, t[3][:], 127.0, None, ALU.add))
            st.link(ts(ki, ki, 23, None, ALU.logical_shift_left))
            st.link(v.scalar_tensor_tensor(ld[:], t[5][:], 1.0, t[6][:], ALU.add, ALU.mult))
            tt(ar[:], ld[:], are[:], ALU.mult).then_inc(angles_ready, 1)
            st.link(tt(tau[:], ld[:], aim[:], ALU.mult))
            st.link(ts(tau[:], tau[:], 1.0 / (2.0 * math.pi), None, ALU.mult))
            st.link(ts(t[3][:], tau[:], 0.25, None, ALU.add))
            st.link(ts(t[5][:], tau[:], 0.5, None, ALU.mult))
            for n, (src, dst) in enumerate(((t[3], t[1]), (tau, t[2]), (t[5], t[7]))):
                st.link(ts(t[4][:], src[:], MAGIC, MAGIC, ALU.add, ALU.subtract))
                tt(dst[:], src[:], t[4][:], ALU.subtract).then_inc(angles_ready, 1)
                dve.wait_ge(angles_ready, n + 2)
            for k in range(LOG):
                dve.wait_ge(th_done, k + 1)
                u = th[:, k % 2, :]
                st.link(ts(t[3][:], u, -1.0, 1.0, ALU.mult, ALU.add))
                st.link(v.reciprocal(t[3][:], t[3][:]))
                if k == 0:
                    st.link(tt(t[0][:], u, t[3][:], ALU.mult))
                v.scalar_tensor_tensor(grow[:, k, :], u, 1.0, t[3][:], ALU.add, ALU.mult).then_inc(th_used, 1)
                dve.wait_ge(th_used, k + 1)
            dve.wait_ge(sines_done, 3)
            st.link(ts(t[0][:], t[0][:], 2.0, None, ALU.mult))
            st.link(tt(t[1][:], t[0][:], t[1][:], ALU.mult))
            st.link(tt(t[7][:], t[7][:], t[7][:], ALU.mult))
            st.link(ts(t[7][:], t[7][:], 2.0, None, ALU.mult))
            st.link(tt(t[1][:], t[1][:], t[7][:], ALU.subtract))
            st.link(ts(t[0][:], t[0][:], 1.0, None, ALU.add))
            st.link(tt(t[2][:], t[0][:], t[2][:], ALU.mult))
            st.link(tt(t[3][:], are[:], are[:], ALU.mult))
            st.link(tt(t[4][:], aim[:], aim[:], ALU.mult))
            st.link(tt(t[3][:], t[3][:], t[4][:], ALU.add))
            st.link(v.reciprocal(t[3][:], t[3][:]))
            st.link(tt(t[4][:], t[1][:], are[:], ALU.mult))
            st.link(tt(t[5][:], t[2][:], aim[:], ALU.mult))
            st.link(tt(t[4][:], t[4][:], t[5][:], ALU.add))
            st.link(tt(t[4][:], t[4][:], t[3][:], ALU.mult))
            st.link(tt(t[5][:], t[2][:], are[:], ALU.mult))
            st.link(tt(t[6][:], t[1][:], aim[:], ALU.mult))
            st.link(tt(t[5][:], t[5][:], t[6][:], ALU.subtract))
            st.link(tt(t[5][:], t[5][:], t[3][:], ALU.mult))
            st.link(tt(t[6][:], cre[:], t[4][:], ALU.mult))
            st.link(tt(t[7][:], cim[:], t[5][:], ALU.mult))
            st.link(tt(dcr[:], t[6][:], t[7][:], ALU.subtract))
            st.link(ts(dcr[:], dcr[:], 2.0, None, ALU.mult))
            st.link(tt(t[6][:], cre[:], t[5][:], ALU.mult))
            st.link(tt(t[7][:], cim[:], t[4][:], ALU.mult))
            st.link(tt(dci[:], t[6][:], t[7][:], ALU.add))
            st.link(ts(dci[:], dci[:], 2.0, None, ALU.mult))
            st.link(v.memset(ea[:], 1.0))
            n0 = st.n
            NSTEP = 17

            with dve.Fori(0, NCHUNK) as c:
                st = Steps(dve, step, c * NSTEP + n0)

                def per_channel(small):
                    return small[:, bass.ds(c * DCH, DCH)].unsqueeze(2).to_broadcast([P, DCH, 32])

                def per_l(vec):
                    return vec.unsqueeze(1).to_broadcast([P, DCH, 32])

                dve.wait_ge(k_done, c)
                for k in range(5):
                    n = 2 ** k
                    for part, power in ((0, 5 + k), (1, k)):
                        g = grow[:, power, bass.ds(c * DCH, DCH)].unsqueeze(2).to_broadcast([P, DCH, n])
                        last = tt(ea[:, part, :, n:2 * n], ea[:, part, :, 0:n], g, ALU.mult)
                        st.mark(last)
                    st.wait()

                def argument(key, out):
                    st.link(ts(out[:], x[:], offs[key], MAGIC, ALU.add, ALU.add))
                    v.scalar_tensor_tensor(out[:], out[:], MAGIC, x[:], ALU.subtract, ALU.subtract).then_inc(arg_ready, 1)

                st.link(tt(x[:], per_channel(tau), per_l(la), ALU.mult))
                argument("u", f[0])
                dve.wait_ge(arg_ready, c * 3 + 1)
                st.link(tt(x[:], per_channel(tau), per_l(lb), ALU.mult))
                argument("w1", f[1])
                argument("w2", f[2])
                dve.wait_ge(sin_done, c * 3 + 1)
                tt(U[:], sn[0][:], ea[:, 0], ALU.mult).then_inc(u_ready, 1)
                st.link(tt(W[:], ea[:, 1], per_channel(dcr), ALU.mult))
                dve.wait_ge(arg_ready, c * 3 + 3)
                st.link(tt(x[:], ea[:, 1], per_channel(dci), ALU.mult))
                dve.wait_ge(sin_done, c * 3 + 3)
                tt(W[:], W[:], sn[1][:], ALU.mult).then_inc(w_half, 1)
                tt(W2[:], x[:], sn[2][:], ALU.mult).then_inc(w_half, 1)
                dve.wait_ge(w_half, c * 2 + 2)
                tt(W[:], W[:], W2[:], ALU.add).then_inc(w_ready, 1)
                dve.wait_ge(w_ready, c + 1)
                dve.wait_ge(u_ready, c + 1)
                stand(dve, passed)
                assert st.n == NSTEP, st.n


def convolve(nc, xm, conv_k, D_skip, dft, idft, eye, ys):
    with ExitStack() as ctx:
        m = Alloc(nc, ctx, "s_")
        KT, Q, DH2 = S // P, 4, D // 2
        BK = 2 * Q
        ident = m.sb("ident", [P, P])
        dsk = m.sb("dsk", [1, 2, DH2])
        xs = m.sb("xs", [P, 2, KT, DH2])
        va = m.sb("va", [P, 2, Q, 2, 2, DH2])
        vb = m.sb("vb", [P, 2, Q, 2, 2, DH2])
        ksp = m.sb("ksp", [P, 2, BK, 2, DH2])
        fm = m.sb("fm", [P, Q, 2, 3, 2, P])
        gm = m.sb("gm", [P, Q, 2, 3, 2, P])
        t4 = m.sb("t4", [P, 2, 2, 2, DH2])
        yo = m.sb("yo", [P, 2, KT, DH2])
        kd = yo[:].rearrange("p a b c -> p (a b c)").rearrange("p (t l) -> p t l", l=S)
        p_x = m.ps("p_x", [P, 4, 2, DH2])
        p_u = m.ps("p_u", [P, 4, 2, DH2])
        (k_in, const_in, kt_done, kt_copied, kernel_ready, twiddled, stage_done, fft_ready, x_done, kf_copied,
         prod_ready, y_ready, inv_done, inv_copied, v_done, w_ready, y_scaled) = [
            m.sem(n) for n in (
                "k_in const_in kt_done kt_copied kernel_ready twiddled stage_done fft_ready x_done kf_copied "
                "prod_ready y_ready inv_done inv_copied v_done w_ready y_scaled").split()]
        x_in = [m.sem(f"x_in{u}") for u in range(2)]
        y_out = [m.sem(f"y_out{u}") for u in range(2)]
        block = ctx.enter_context(nc.Block())
        turn = [2 * math.pi * a / 16 for a in range(Q)]

        def sequences(eng, body):
            body(0)
            with eng.Fori(1, B - 1) as b:
                body(b)
            body(B - 1)

        @block.sync
        def _(sp):
            def cols(ap, b, u):
                return ap[bass.ds(b * S, S), DH2 * u:DH2 * u + DH2].rearrange("(c p) n -> p c n", p=P)

            def load(b, u):
                free, row = (b * 16 + 8 * u + 8, b) if isinstance(b, int) else (sp.snap(b * 16 + (8 * u + 8)), b)
                sp.wait_ge(twiddled, free)
                sp.dma_start(xs[:, u], cols(xm, row, u)).then_inc(x_in[u], 16)

            sp.dma_start(kd, conv_k.rearrange("(t p) l -> p t l", p=P)).then_inc(k_in, 16)
            sp.dma_start(ident[:], eye).then_inc(const_in, 16)
            sp.dma_start(dsk[:], D_skip.rearrange("(a u n) -> a u n", a=1, u=2)).then_inc(const_in, 16)
            sp.dma_start(fm[:], dft).then_inc(const_in, 16)
            sp.dma_start(gm[:], idft).then_inc(const_in, 16)
            for u in range(2):
                load(0, u)

            def body(b):
                last = isinstance(b, int) and b == B - 1
                snap = (lambda a: a) if isinstance(b, int) else sp.snap
                nxt, counts = snap(b + 1), [snap(b * 8 + (4 * u + 4)) for u in range(2)]
                if not last:
                    for u in range(2):
                        load(nxt, u)
                for u in range(2):
                    sp.wait_ge(y_scaled, counts[u])
                    sp.dma_start(cols(ys, b, u), yo[:, u]).then_inc(y_out[u], 16)

            sequences(sp, body)
            for u in range(2):
                sp.wait_ge(y_out[u], 16 * B)

        @block.tensor
        def _(pe):
            mm = nc.tensor.matmul

            def transform(mats, j, src, bank, done):
                k1, h = j // 2, j % 2
                for q in range(2):
                    mm(bank, mats[:, k1, h, 0, q, :], src[:, k1, :, q, :], start=(q == 0), stop=False,
                       skip_group_check=True)
                    mm(bank[:, 0, :], mats[:, k1, h, 2, q, :], src[:, k1, 1, q, :], start=False, stop=False,
                       skip_group_check=True)
                    last = mm(bank[:, 1, :], mats[:, k1, h, 1, q, :], src[:, k1, 0, q, :], start=False,
                              stop=(q == 1), skip_group_check=True)
                last.then_inc(done, 1)

            def forward(n, u):
                pe.wait_ge(fft_ready, n * 6 + 6)
                for j in range(BK):
                    if isinstance(n, int) and n < 2:
                        at_least(pe, kf_copied, n * BK + j - 3)
                    else:
                        at_least(pe, prod_ready, n * BK + (j - 3 - 2 * BK))
                    transform(fm, j, va[:, u], p_x[:, j % 4], x_done)

            def inverse(b, u):
                pe.wait_ge(y_ready, b * (4 * BK) + (u + 1) * 2 * BK)
                for j in range(BK):
                    at_least(pe, inv_copied, b * (2 * BK) + (u * BK + j - 3))
                    transform(gm, j, vb[:, u], p_u[:, j % 4], inv_done)

            pe.wait_ge(const_in, 64)
            pe.wait_ge(k_in, 16)
            for c in range(KT):
                at_least(pe, kt_copied, c - 3)
                for d in range(4):
                    last = nc.tensor.transpose(p_u[:, c % 4, d // 2, (d % 2) * P:(d % 2 + 1) * P],
                                               kd[:, d, c * P:(c + 1) * P], ident[:])
                last.then_inc(kt_done, 1)
            for u in range(2):
                forward(u, u)
            pe.wait_ge(kf_copied, 2 * BK)

            def body(b):
                for u in range(2):
                    forward(b * 2 + (2 + u), u)
                for u in range(2):
                    inverse(b, u)

            sequences(pe, body)

        @block.scalar
        def _(act):
            a = nc.scalar.activation

            def twiddle(u):
                x = [xs[:, u, 2 * n:2 * n + 2, :] for n in range(Q)]
                for n in (1, 3):
                    a(va[:, u, n, 0], x[n], ACT.Copy, scale=math.cos(turn[n])).then_inc(twiddled, 1)
                    a(va[:, u, n, 1], x[n], ACT.Copy, scale=-math.sin(turn[n])).then_inc(twiddled, 1)
                a(va[:, u, 0, 0], x[0], ACT.Copy).then_inc(twiddled, 1)
                a(va[:, u, 2, 0], x[2], ACT.Copy, scale=math.cos(turn[2])).then_inc(twiddled, 1)
                a(vb[:, u, 0, 1], x[2], ACT.Copy, scale=-math.sin(turn[2])).then_inc(twiddled, 1)
                a(vb[:, u, 2, 1], x[2], ACT.Copy, scale=math.sin(turn[2])).then_inc(twiddled, 1)

            def turn_x(b, u):
                act.wait_ge(x_in[u], b * 16 + 16)
                at_least(act, y_scaled, b * 8 + (4 * u - 4))
                twiddle(u)

            def copy_inverse(b, u, js):
                for j in js:
                    act.wait_ge(inv_done, b * (2 * BK) + (u * BK + j + 1))
                    a(va[:, u, j // 2, :, j % 2, :], p_u[:, j % 4], ACT.Copy).then_inc(inv_copied, 1)

            def scale(b, u):
                act.wait_ge(w_ready, b * 6 + (3 * u + 3))
                at_least(act, y_out[u], b * 16)
                for n in range(Q):
                    a(yo[:, u, 2 * n:2 * n + 2, :], va[:, u, n, 0], ACT.Copy,
                      scale=math.cos(turn[n])).then_inc(y_scaled, 1)

            for c in range(KT):
                act.wait_ge(kt_done, c + 1)
                a(xs[:, :, c, :], p_u[:, c % 4], ACT.Copy).then_inc(kt_copied, 1)
            act.wait_ge(kernel_ready, 1)
            for u in range(2):
                twiddle(u)
            for u in range(2):
                for j in range(BK):
                    act.wait_ge(x_done, u * BK + j + 1)
                    a(ksp[:, u, j], p_x[:, j % 4], ACT.Copy).then_inc(kf_copied, 1)
                if u == 0:
                    turn_x(0, 0)

            def body(b):
                first, last = (isinstance(b, int) and b == e for e in (0, B - 1))
                if not first:
                    scale(b - 1, 1)
                turn_x(b, 1)
                copy_inverse(b, 0, range(BK))
                copy_inverse(b, 1, range(3))
                scale(b, 0)
                if not last:
                    turn_x(b + 1, 0)
                copy_inverse(b, 1, range(3, BK))

            sequences(act, body)
            scale(B - 1, 1)

        @block.vector
        def _(dve):
            v = nc.vector
            tt = v.tensor_tensor

            def butterflies(n, u):
                A, Z = va[:, u], vb[:, u]
                dve.wait_ge(twiddled, n * 8 + 8)
                tt(Z[:, 0, 0], A[:, 0, 0], A[:, 2, 0], ALU.add).then_inc(stage_done, 1)
                tt(Z[:, 2, 0], A[:, 0, 0], A[:, 2, 0], ALU.subtract).then_inc(stage_done, 1)
                tt(Z[:, 1], A[:, 1], A[:, 3], ALU.add).then_inc(stage_done, 1)
                tt(Z[:, 3], A[:, 1], A[:, 3], ALU.subtract).then_inc(stage_done, 1)

            def butterflies2(stages, u):
                A, Z = va[:, u], vb[:, u]
                dve.wait_ge(stage_done, stages)
                for out, x, y, op in ((A[:, 0], Z[:, 0], Z[:, 1], ALU.add), (A[:, 2], Z[:, 0], Z[:, 1], ALU.subtract),
                                      (A[:, 1, 0], Z[:, 2, 0], Z[:, 3, 1], ALU.add),
                                      (A[:, 1, 1], Z[:, 2, 1], Z[:, 3, 0], ALU.subtract),
                                      (A[:, 3, 0], Z[:, 2, 0], Z[:, 3, 1], ALU.subtract),
                                      (A[:, 3, 1], Z[:, 2, 1], Z[:, 3, 0], ALU.add)):
                    tt(out, x, y, op).then_inc(fft_ready, 1)

            def product(b, u, js):
                for j in js:
                    dve.wait_ge(x_done, b * (2 * BK) + ((u + 2) * BK + j + 1))
                    at_least(dve, y_ready, b * (4 * BK) + 2 * (u * BK + j - 1))
                    tt(t4[:, j % 2], p_x[:, j % 4].unsqueeze(1).to_broadcast([P, 2, 2, DH2]),
                       ksp[:, u, j].unsqueeze(2).to_broadcast([P, 2, 2, DH2]), ALU.mult).then_inc(prod_ready, 1)

            def combine(b, u, stages):
                A, Z = va[:, u], vb[:, u]
                dve.wait_ge(inv_copied, b * (2 * BK) + (u + 1) * BK)
                for out, x, y, op in ((0, 0, 2, ALU.add), (1, 1, 3, ALU.add), (2, 0, 2, ALU.subtract),
                                      (3, 1, 3, ALU.subtract)):
                    tt(Z[:, out], A[:, x], A[:, y], op).then_inc(stage_done, 1)
                dve.wait_ge(stage_done, stages)
                for out, x, y, op in ((A[:, 0, 0], Z[:, 0, 0], Z[:, 1, 0], ALU.add),
                                      (A[:, 2], Z[:, 0], Z[:, 1], ALU.subtract),
                                      (A[:, 1, 0], Z[:, 2, 0], Z[:, 3, 1], ALU.subtract),
                                      (A[:, 1, 1], Z[:, 2, 1], Z[:, 3, 0], ALU.add),
                                      (A[:, 3, 0], Z[:, 2, 0], Z[:, 3, 1], ALU.add),
                                      (A[:, 3, 1], Z[:, 2, 1], Z[:, 3, 0], ALU.subtract)):
                    tt(out, x, y, op).then_inc(v_done, 1)
                dve.wait_ge(v_done, b * 12 + (6 * u + 6))
                for n in range(1, Q):
                    v.scalar_tensor_tensor(A[:, n, 0], A[:, n, 1], -math.tan(turn[n]), A[:, n, 0], ALU.mult,
                                           ALU.add).then_inc(w_ready, 1)

            dve.wait_ge(const_in, 64)
            dve.wait_ge(kt_copied, KT)
            tt(xs[0:1, :, 0, :], xs[0:1, :, 0, :], dsk[:], ALU.add).then_inc(kernel_ready, 1)
            for n in range(3):
                butterflies(n, n % 2)
                butterflies2(n * 4 + 4, n % 2)
            dve.wait_ge(kf_copied, 2 * BK)

            def body(b):
                first, last = (isinstance(b, int) and b == e for e in (0, B - 1))
                if not first:
                    combine(b - 1, 1, b * 16 + 12)
                product(b, 0, range(4))
                butterflies(b * 2 + 3, 1)
                butterflies2(b * 16 + 16, 1)
                product(b, 0, range(4, BK))
                product(b, 1, range(BK))
                combine(b, 0, b * 16 + 20)
                if not last:
                    butterflies(b * 2 + 4, 0)
                    butterflies2(b * 16 + 24, 0)

            sequences(dve, body)
            combine(B - 1, 1, B * 16 + 8)

        @block.gpsimd
        def _(pool):
            def add(b, u):
                for j in range(BK):
                    pool.wait_ge(prod_ready, b * (2 * BK) + (u * BK + j + 1))
                    for r in range(2):
                        pool.tensor_tensor(vb[:, u, j // 2, r, j % 2, :], t4[:, j % 2, 0, r, :],
                                           t4[:, j % 2, 1, 1 - r, :],
                                           ALU.add if r else ALU.subtract).then_inc(y_ready, 1)

            with pool.Fori(0, B) as b:
                for u in range(2):
                    add(b, u)


F = 2048
FT = F // P
WB = 2 * P


def quantize_weights(nc, w1T, w2T, w1q, w2q, wmean):
    with ExitStack() as ctx:
        m = Alloc(nc, ctx, "q_")
        w = m.sb("w", [P, 2, 16, 512])
        wb = m.sb("wb", [P, 2, 16, 512], BF16)
        part = m.sb("part", [P, 2, 16])
        tot = m.sb("tot", [P, 2])
        ones = m.sb("ones", [P, P])
        mean = m.sb("mean", [P, 2])
        sc = m.sb("sc", [P, 2])
        p_t = m.ps("p_t", [P, 2])
        w_in = [m.sem(f"w_in{n}") for n in range(2)]
        step, tot_ready, sum_done, q_ready, stored = [m.sem(n) for n in "step tot_ready sum_done q_ready stored".split()]
        block = ctx.enter_context(nc.Block())

        @block.sync
        def _(sp):
            for n, src in enumerate((w1T, w2T)):
                sp.dma_start(w[:, n].rearrange("p a b -> p (a b)"), src).then_inc(w_in[n], 16)
            for n, dst in enumerate((w1q, w2q)):
                sp.wait_ge(q_ready, n + 1)
                sp.dma_start(dst, wb[:, n].rearrange("p a b -> p (a b)")).then_inc(stored, 16)
            sp.dma_start(wmean, mean[:]).then_inc(stored, 16)
            sp.wait_ge(stored, 48)

        @block.tensor
        def _(pe):
            pe.wait_ge(tot_ready, 1)
            nc.tensor.matmul(p_t[:], ones[:], tot[:], start=True, stop=True).then_inc(sum_done, 1)

        @block.vector
        def _(dve):
            v = nc.vector
            st = Steps(dve, step, 0)
            st.link(v.memset(ones[:], 1.0))
            for n in range(2):
                dve.wait_ge(w_in[n], 16)
                st.link(v.tensor_reduce(part[:, n], w[:, n], AX.X, ALU.add, apply_absolute_value=True))
            v.tensor_reduce(tot[:], part[:], AX.X, ALU.add).then_inc(tot_ready, 1)
            dve.wait_ge(sum_done, 1)
            st.link(v.tensor_scalar(mean[:], p_t[:], 1.0 / (D * F), 1e-5, ALU.mult, ALU.max))
            st.link(v.reciprocal(sc[:], mean[:]))
            for n in range(2):
                st.link(v.tensor_scalar(w[:, n], w[:, n], sc[:, n:n + 1], MAGIC, ALU.mult, ALU.add))
                st.link(v.tensor_scalar(w[:, n], w[:, n], MAGIC, 1.0, ALU.subtract, ALU.min))
                v.tensor_scalar(wb[:, n], w[:, n], -1.0, None, ALU.max).then_inc(q_ready, 1)


def feed_forward(nc, x1, ys, mod_out, W1, b1T, W2, b2, g_ffn, b_ffn, g_out, b_out, eye, x2, q1T, inv_rows):
    with ExitStack() as ctx:
        m = Alloc(nc, ctx, "f_")
        w1 = m.sb("w1", [P, KD, F])
        w2 = m.sb("w2", [P, FT, D])
        b1c = m.sb("b1c", [P, FT])
        bc = m.sb("bc", [P, 5, D])
        ident = m.sb("ident", [P, P])
        identb = m.sb("identb", [P, P], BF16)
        eps = m.sb("eps", [P, 1])
        xr = m.sb("xr", [P, 2, D])
        yr = m.sb("yr", [P, 2, D])
        mr = m.sb("mr", [P, 2, 2 * D])
        xt = m.sb("xt", [P, 2, D])
        h = m.sb("h", [P, D])
        hT = m.sb("hT", [P, D])
        gT = m.sb("gT", [P, FT, P])
        r2 = m.sb("r2", [P, D])
        r3 = m.sb("r3", [P, D])
        xo = m.sb("xo", [P, 2, D])
        qf = m.sb("qf", [P, D])
        qb = m.sb("qb", [P, D], BF16)
        qT = m.sb("qT", [P, 2, KD, P], BF16)
        stats = m.sb("stats", [P, 3, 6])
        mv = m.sb("mv", [P, 3, 2])
        std = m.sb("std", [P, 3])
        rstd = m.sb("rstd", [P, 3])
        am = m.sb("am", [P, 1])
        qs = m.sb("qs", [P, 1])
        inv = m.sb("inv", [P, TOK // P])
        invT = m.sb("invT", [TOK // P, P])
        p_g = m.ps("p_g", [P, FT, P])
        p_h = m.ps("p_h", [P, D])
        p_o = m.ps("p_o", [P, D])
        p_q = m.ps("p_q", [P, 2 * KD, P], BF16)[:, 0:KD, :]
        (weights_in, consts, h_ready, hT_done, hT_copied, g_done, g_copied, o_done, mod_done, step, pstep, qb_ready,
         qT_done, qT_copied, x2_ready, r3_ready, inv_out, out_norm, inv_done, inv_copied, passed, ln_head, invT_out) = [
            m.sem(n) for n in (
                "weights_in consts h_ready hT_done hT_copied g_done g_copied o_done mod_done step pstep qb_ready "
                "qT_done qT_copied x2_ready r3_ready inv_out out_norm inv_done inv_copied passed ln_head invT_out").split()]
        var = [m.sem(f"var{n}") for n in range(3)]
        stdr = [m.sem(f"stdr{n}") for n in range(3)]
        t_in = [m.sem(f"t_in{u}") for u in range(2)]
        x2_out = [m.store_sem(f"x2_out{u}") for u in range(2)]
        q_out = [m.store_sem(f"q_out{u}") for u in range(2)]
        TILES = TOK // P
        PAIRS = TILES // 2
        block = ctx.enter_context(nc.Block())

        def pairs(eng, pair):
            pair(0)
            with eng.Fori(1, PAIRS - 1) as i:
                pair(i)
            pair(PAIRS - 1)

        def is_last(t):
            return isinstance(t, int) and t == TILES - 1

        def is_first(t):
            return isinstance(t, int) and t == 0

        @block.sync
        def _(sp):
            def bcast(ap):
                return ap.rearrange("(a n) -> a n", a=1).to_broadcast([P, D])

            def load(u, row):
                sp.dma_start(xr[:, u, :], x1[bass.ds(row, P), :]).then_inc(t_in[u], 16)
                sp.dma_start(yr[:, u, :], ys[bass.ds(row, P), :]).then_inc(t_in[u], 16)
                sp.dma_start(mr[:, u, :], mod_out[bass.ds(row, P), :]).then_inc(t_in[u], 16)

            for u in range(2):
                load(u, u * P)
            for dst, src in [(w1[:], W1.rearrange("(k p) n -> p k n", p=P)), (w2[:], W2.rearrange("(k p) n -> p k n", p=P)),
                             (b1c[:], b1T), (ident[:], eye)] + [
                             (bc[:, n, :], bcast(ap)) for n, ap in enumerate((g_ffn, b_ffn, b2, g_out, b_out))]:
                sp.dma_start(dst, src).then_inc(weights_in, 16)
            with sp.Fori(0, PAIRS - 1) as i:
                for u in range(2):
                    done, row = sp.snap(i * 2 + (u + 1)), sp.snap(i * (2 * P) + (u + 2) * P)
                    sp.wait_ge(r3_ready, done)
                    load(u, row)

        @block.tensor
        def _(pe):
            mm = nc.tensor.matmul
            pe.wait_ge(weights_in, 16 * 9)
            pe.wait_ge(consts, 2)

            def turn_h(t):
                pe.wait_ge(h_ready, t + 1)
                for k in range(KD):
                    last = nc.tensor.transpose(p_h[:, k * P:(k + 1) * P], h[:, k * P:(k + 1) * P], ident[:])
                last.then_inc(hT_done, 1)

            def turn_q(t):
                pe.wait_ge(qb_ready, t + 1)
                at_least(pe, qT_copied, t)
                for k in range(KD):
                    last = nc.tensor.transpose(p_q[:, k, :], qb[:, k * P:(k + 1) * P], identb[:])
                last.then_inc(qT_done, 1)

            def slot(t):
                pe.wait_ge(hT_copied, t + 1)
                for f in range(FT):
                    if f % 4 == 0:
                        at_least(pe, g_copied, t * FT - (FT - 4 - f) if not is_first(t) else 0)
                    for k in range(KD):
                        last = mm(p_g[:, f, :], w1[:, k, f * P:(f + 1) * P], hT[:, k * P:(k + 1) * P],
                                  start=(k == 0 and f % 4 == 0), stop=(k == KD - 1 and f % 4 == 3), skip_group_check=True)
                    last.then_inc(g_done, 1)
                if not is_first(t):
                    turn_q(t - 1)
                at_least(pe, var[1], t)
                for f in range(FT):
                    pe.wait_ge(g_copied, t * FT + (f + 1))
                    last = mm(p_o[:], gT[:, f, :], w2[:, f, :], start=(f == 0), stop=(f == FT - 1))
                last.then_inc(o_done, 1)
                if not is_last(t):
                    turn_h(t + 1)

            def pair(i):
                for u in range(2):
                    slot(i * 2 + u)

            turn_h(0)
            pairs(pe, pair)
            turn_q(TILES - 1)
            pe.wait_ge(inv_done, TILES)
            nc.tensor.transpose(p_h[0:TILES, 0:P], inv[:], ident[:]).then_inc(inv_copied, 1)

        @block.scalar
        def _(act):
            a = nc.scalar.activation
            act.wait_ge(consts, 2)
            act.wait_ge(weights_in, 16 * 9)

            def root(n, t):
                act.wait_ge(var[n], t + 1)
                a(std[:, n:n + 1], mv[:, n, 1:2], ACT.Sqrt, bias=eps[:]).then_inc(stdr[n], 1)

            def copy_h(t):
                act.wait_ge(hT_done, t + 1)
                a(hT[:], p_h[:], ACT.Copy).then_inc(hT_copied, 1)

            def slot(t):
                at_least(act, o_done, t)
                for f in range(FT):
                    if f % 4 == 0:
                        act.wait_ge(g_done, t * FT + (f + 4))
                    a(gT[:, f, :], p_g[:, f, :], ACT.Gelu, bias=b1c[:, f:f + 1]).then_inc(g_copied, 1)
                if not is_last(t):
                    root(0, t + 1)
                    copy_h(t + 1)
                root(1, t)
                root(2, t)

            def pair(i):
                for u in range(2):
                    slot(i * 2 + u)

            root(0, 0)
            copy_h(0)
            pairs(act, pair)
            act.wait_ge(inv_copied, 1)
            a(invT[:], p_h[0:TILES, 0:P], ACT.Copy).then_inc(invT_out, 1)
            act.wait_ge(invT_out, 1)
            act.dma_start(inv_rows.rearrange("a (t p) -> (a t) p", p=P), invT[:]).then_inc(inv_out, 16)
            act.wait_ge(inv_out, 16)

        @block.vector
        def _(dve):
            v = nc.vector
            v.memset(eps[:], LN_EPS).then_inc(consts, 1)
            dve.wait_ge(weights_in, 16 * 9)
            v.tensor_copy(identb[:], ident[:]).then_inc(consts, 1)
            dve.wait_ge(consts, 2)
            NSTEP = 12

            def norm(st, n, t, src, dst, sem, free=None):
                st.link(v.bn_stats(stats[:, n, :], src))
                stand(dve, passed)
                v.bn_aggr(mv[:, n, :], stats[:, n, :]).then_inc(var[n], 1)
                dve.wait_ge(stdr[n], t + 1)
                st.link(v.reciprocal(rstd[:, n:n + 1], std[:, n:n + 1]))
                if free:
                    free()
                v.tensor_scalar(dst, src, mv[:, n, 0:1], rstd[:, n:n + 1], ALU.subtract, ALU.mult).then_inc(sem, 1)

            def head(st, t, u):
                dve.wait_ge(mod_done, t + 1)
                norm(st, 0, t, xt[:, u, :], h[:], ln_head, lambda: at_least(dve, hT_done, t))

            def tail(st, t, i, u):
                dve.wait_ge(o_done, t + 1)
                st.link(v.tensor_tensor(r2[:], p_o[:], xt[:, u, :], ALU.add))
                norm(st, 1, t, r2[:], r2[:], out_norm)
                dve.wait_ge(r3_ready, t + 1)
                norm(st, 2, t, r3[:], xo[:, u, :], x2_ready, lambda: at_least(dve, x2_out[u], i * 16))
                dve.wait_ge(x2_ready, t + 1)
                st.link(v.tensor_reduce(am[:], xo[:, u, :], AX.X, ALU.max, apply_absolute_value=True))
                st.link(v.tensor_scalar(am[:], am[:], 1e-5, None, ALU.max))
                st.link(v.reciprocal(qs[:], am[:]))
                st.link(v.tensor_scalar(qs[:], qs[:], 127.0, None, ALU.mult))
                v.reciprocal(inv[:, t:t + 1] if isinstance(t, int) else inv[:, bass.ds(t, 1)], qs[:]).then_inc(inv_done, 1)
                st.link(v.tensor_scalar(qf[:], xo[:, u, :], qs[:], MAGIC, ALU.mult, ALU.add))
                at_least(dve, qT_done, t)
                v.tensor_scalar(qb[:], qf[:], MAGIC, None, ALU.subtract).then_inc(qb_ready, 1)
                dve.wait_ge(qT_done, t + 1)
                at_least(dve, q_out[u], i * 16)
                v.tensor_copy(qT[:, u], p_q).then_inc(qT_copied, 1)

            def pair(i):
                for u in range(2):
                    t = i * 2 + u
                    st = Steps(dve, step, t * NSTEP + 2)
                    if not is_last(t):
                        head(st, t + 1, 1 - u)
                    tail(st, t, i, u)
                    assert is_last(t) or st.n == NSTEP, st.n

            head(Steps(dve, step, 0), 0, 0)
            pairs(dve, pair)

        @block.gpsimd
        def _(pool):
            tt = pool.tensor_tensor
            pool.wait_ge(weights_in, 16 * 9)
            NSTEP = 7

            def modulate(st, t, i, u):
                pool.wait_ge(t_in[u], i * 48 + 48)
                at_least(pool, r3_ready, t - 1)
                st.link(tt(xt[:, u, :], yr[:, u, :], mr[:, u, 0:D], ALU.mult))
                st.link(tt(yr[:, u, :], yr[:, u, :], mr[:, u, D:], ALU.add))
                st.link(tt(xt[:, u, :], xt[:, u, :], yr[:, u, :], ALU.add))
                tt(xt[:, u, :], xt[:, u, :], xr[:, u, :], ALU.add).then_inc(mod_done, 1)
                pool.wait_ge(ln_head, t + 1)
                st.link(tt(h[:], h[:], bc[:, 0, :], ALU.mult))
                tt(h[:], h[:], bc[:, 1, :], ALU.add).then_inc(h_ready, 1)
                st.link(tt(xt[:, u, :], xt[:, u, :], bc[:, 2, :], ALU.add))

            def finish(st, t, u):
                pool.wait_ge(out_norm, t + 1)
                st.link(tt(r3[:], r2[:], bc[:, 3, :], ALU.mult))
                st.link(tt(r3[:], r3[:], bc[:, 4, :], ALU.add))
                tt(r3[:], r3[:], xr[:, u, :], ALU.add).then_inc(r3_ready, 1)

            def store(t, u):
                pool.wait_ge(x2_ready, t + 1)
                pool.dma_start(x2[bass.ds(t * P, P), :], xo[:, u, :]).then_inc(x2_out[u], 16)
                pool.wait_ge(qT_copied, t + 1)
                pool.dma_start(q1T.rearrange("(k p) n -> p k n", p=P)[:, :, bass.ds(t * P, P)], qT[:, u]).then_inc(q_out[u], 16)

            def pair(i):
                for u in range(2):
                    t = i * 2 + u
                    st = Steps(pool, pstep, t * NSTEP + 5)
                    if not is_last(t):
                        modulate(st, t + 1, i + u, 1 - u)
                    finish(st, t, u)
                    assert is_last(t) or st.n == NSTEP, st.n
                    store(t, u)

            st = Steps(pool, pstep, 0)
            modulate(st, 0, 0, 0)
            pairs(pool, pair)
            for u in range(2):
                pool.wait_ge(x2_out[u], 16 * PAIRS)
                pool.wait_ge(q_out[u], 16 * PAIRS)


def bit_ffn(nc, x2, q1T, inv_rows, w1q, w2q, wmean, conv_w, conv_b, eye, out):
    with ExitStack() as ctx:
        m = Alloc(nc, ctx, "b_")
        w1 = m.sb("w1", [P, KD, F], BF16)
        w2 = m.sb("w2", [P, FT, D], BF16)
        wm = m.sb("wm", [P, 2])
        cw = m.sb("cw", [P, FT, 3])
        cb = m.sb("cb", [P, FT])
        ident = m.sb("ident", [P, P])
        ones = m.sb("ones", [P, P])
        eps = m.sb("eps", [P, 1])
        qb = m.sb("qb", [P, 2, KD, WB + 2], BF16)
        rs = m.sb("rs", [P, 2, WB + 2])
        xr = m.sb("xr", [P, 2, 2, D])
        NBUF = 4
        hs = m.sb("hs", [P, NBUF, WB + 2])
        c1, c2, c3 = (m.sb(n, [P, NBUF, WB]) for n in ("c1", "c2", "c3"))
        sl = m.sb("sl", [P, FT, WB])
        sq = m.sb("sq", [P, FT, WB])
        q2 = m.sb("q2", [P, FT, WB], BF16)
        mx = m.sb("mx", [P, WB])
        a2 = m.sb("a2", [P, 2])
        s2 = m.sb("s2", [P, 2])
        i2 = m.sb("i2", [P, 2, 2])
        dg = m.sb("dg", [P, 2, P])
        res = m.sb("res", [P, 2, D])
        stats = m.sb("stats", [P, 2, 6])
        mv = m.sb("mv", [P, 2, 2])
        std = m.sb("std", [P, 2])
        rstd = m.sb("rstd", [P, 2])
        xo = m.sb("xo", [P, 2, D])
        p_h = m.ps("p_h", [P, NBUF, 512])
        p_m = m.ps("p_m", [P, 512])[:, 0:WB].rearrange("p (u n) -> p u n", u=2)
        p_b = m.ps("p_b", [P, 512])[:, 0:WB]
        p_o = m.ps("p_o", [P, 2, D])
        (weights_in, consts, h_done, hs_ready, c1_ready, c3_ready, sl_ready, mx_ready, mt_done, dg_ready, b_done,
         sq_ready, q2_ready, o_done, res_ready, var_ready, std_ready, out_ready, step, conv_step, passed) = [
            m.sem(n) for n in (
                "weights_in consts h_done hs_ready c1_ready c3_ready sl_ready mx_ready mt_done dg_ready b_done "
                "sq_ready q2_ready o_done res_ready var_ready std_ready out_ready step conv_step passed").split()]
        t_in = [m.sem(f"t_in{u}") for u in range(2)]
        x_out = [m.store_sem(f"x_out{u}") for u in range(2)]
        PB = S // WB
        NB = B * PB
        block = ctx.enter_context(nc.Block())

        def halo(k):
            return (1 if k == 0 else 0), (WB + 1 if k == PB - 1 else WB + 2)

        @block.sync
        def _(sp):
            for dst, src in ((w1[:].rearrange("p a b -> p (a b)"), w1q), (w2[:].rearrange("p a b -> p (a b)"), w2q),
                             (wm[:], wmean), (cw[:], conv_w), (cb[:], conv_b), (ident[:], eye)):
                sp.dma_start(dst, src).then_inc(weights_in, 16)
            qv = q1T.rearrange("(k p) n -> p k n", p=P)
            xv = x2.rearrange("(t p) n -> p t n", p=P)

            def load(b, k):
                snap = (lambda a: a) if isinstance(b, int) else sp.snap
                u = k % 2
                lo, hi = halo(k)
                used = snap(b * PB + (k - 1))
                col = snap(b * S + (k * WB - 1 + lo))
                tile_ = snap(b * CH + 2 * k)
                at_least(sp, res_ready, used)
                sp.dma_start(qb[:, u, :, lo:hi], qv[:, :, bass.ds(col, hi - lo)]).then_inc(t_in[u], 16)
                sp.dma_start(rs[:, u, lo:hi], inv_rows[:, bass.ds(col, hi - lo)].to_broadcast([P, hi - lo])).then_inc(t_in[u], 16)
                sp.dma_start(xr[:, u], xv[:, bass.ds(tile_, 2), :]).then_inc(t_in[u], 16)

            for k in range(PB):
                load(0, k)
            with sp.Fori(1, B) as b:
                for k in range(PB):
                    load(b, k)

        def blocks(eng, body):
            for k in range(PB):
                body(0, k, k)
            with eng.Fori(1, B) as b:
                for k in range(PB):
                    body(b, k, b * PB + k)

        @block.tensor
        def _(pe):
            mm = nc.tensor.matmul
            pe.wait_ge(weights_in, 96)
            pe.wait_ge(consts, 5)

            def project(n, u):
                if u == 0:
                    pe.wait_ge(q2_ready, n + 1)
                at_least(pe, res_ready, n)
                for f in range(FT):
                    last = mm(p_o[:, u, :], q2[:, f, u * P:(u + 1) * P], w2[:, f, :], start=(f == 0), stop=(f == FT - 1))
                last.then_inc(o_done, 1)

            def body(b, k, n):
                u = k % 2
                lo, hi = halo(k)
                pe.wait_ge(t_in[u], b * (PB // 2 * 48) + (k // 2 * 48 + 48))
                for f in range(FT):
                    at_least(pe, hs_ready, n * FT + (f - (NBUF - 1)))
                    for d in range(KD):
                        last = mm(p_h[:, f % NBUF, lo:hi], w1[:, d, f * P:(f + 1) * P], qb[:, u, d, lo:hi],
                                  start=(d == 0), stop=(d == KD - 1))
                    last.then_inc(h_done, 1)
                    if f in (3, 7) and not (isinstance(n, int) and n == 0):
                        project(n - 1, f // 4)
                pe.wait_ge(mx_ready, n + 1)
                for w in range(2):
                    last = nc.tensor.transpose(p_m[:, w, :], mx[:, w * P:(w + 1) * P], ident[:])
                last.then_inc(mt_done, 1)
                pe.wait_ge(dg_ready, n + 1)
                last = mm(p_b, ones[:], dg[:].rearrange("p a b -> p (a b)"), start=True, stop=True)
                last.then_inc(b_done, 1)

            blocks(pe, body)
            for u in range(2):
                project(NB - 1, u)

        @block.scalar
        def _(act):
            a = nc.scalar.activation
            act.wait_ge(consts, 5)

            def root(n):
                act.wait_ge(var_ready, n * 2 + 2)
                a(std[:], mv[:, :, 1], ACT.Sqrt, bias=eps[:]).then_inc(std_ready, 1)

            def body(b, k, n):
                def taps(f):
                    j = n * FT + f
                    act.wait_ge(hs_ready, j + 1)
                    at_least(act, conv_step, j - (NBUF - 1))
                    a(c1[:, f % NBUF, :], hs[:, f % NBUF, 1:WB + 1], ACT.Identity, bias=cb[:, f:f + 1], scale=cw[:, f, 1:2]).then_inc(c1_ready, 1)

                def silu(f):
                    j = n * FT + f
                    act.wait_ge(c3_ready, j + 1)
                    if f == 0:
                        at_least(act, sq_ready, n)
                    a(sl[:, f, :], c3[:, f % NBUF, :], ACT.Silu).then_inc(sl_ready, 1)

                taps(0)
                taps(1)
                for f in range(FT):
                    if f + 2 < FT:
                        taps(f + 2)
                    silu(f)
                    if f == 14 and not (isinstance(n, int) and n == 0):
                        root(n - 1)

            blocks(act, body)
            root(NB - 1)

        @block.vector
        def _(dve):
            v = nc.vector
            v.memset(eps[:], LN_EPS).then_inc(consts, 1)
            v.memset(ones[:], 1.0).then_inc(consts, 1)
            v.memset(hs[:], 0.0).then_inc(consts, 1)
            dve.wait_ge(weights_in, 96)
            v.tensor_scalar(cw[:], cw[:], wm[:, 0:1], None, ALU.mult).then_inc(consts, 1)
            v.memset(i2[:], 0.0).then_inc(consts, 1)
            dve.wait_ge(consts, 5)
            NSTEP = 12
            TAIL = 4

            def tail_a(st, n, par):
                for u in range(2):
                    dve.wait_ge(o_done, n * 2 + (u + 1))
                    st.link(v.scalar_tensor_tensor(res[:, u, :], p_o[:, u, :], i2[:, par, u:u + 1], xr[:, par, u, :], ALU.mult, ALU.add))
                    last = v.bn_stats(stats[:, u, :], res[:, u, :])
                    if u == 0:
                        st.link(last)
                    else:
                        last.then_inc(res_ready, 1)
                dve.wait_ge(res_ready, n + 1)
                stand(dve, passed)
                for u in range(2):
                    v.bn_aggr(mv[:, u, :], stats[:, u, :]).then_inc(var_ready, 1)

            def tail_b(st, n):
                dve.wait_ge(std_ready, n + 1)
                st.link(v.reciprocal(rstd[:], std[:]))
                for u in range(2):
                    at_least(dve, x_out[u], n * 16)
                    v.tensor_scalar(xo[:, u, :], res[:, u, :], mv[:, u, 0:1], rstd[:, u:u + 1], ALU.subtract, ALU.mult).then_inc(out_ready, 1)
                dve.wait_ge(out_ready, n * 2 + 2)

            def body(b, k, n):
                par = k % 2
                st = Steps(dve, step, 0 if isinstance(n, int) and n == 0 else n * NSTEP - TAIL)
                lo, hi = halo(k)
                dve.wait_ge(t_in[par], b * (PB // 2 * 48) + (k // 2 * 48 + 48))

                def dequantize(f):
                    j = n * FT + f
                    at_least(dve, c3_ready, j - (NBUF - 1))
                    dve.wait_ge(h_done, j + 1)
                    v.tensor_tensor(hs[:, f % NBUF, lo:hi], p_h[:, f % NBUF, lo:hi], rs[:, par, lo:hi], ALU.mult).then_inc(hs_ready, 1)

                if k in (0, PB - 1):
                    at_least(dve, c3_ready, n * FT)
                    col = 0 if k == 0 else WB + 1
                    st.link(v.memset(hs[:, :, col:col + 1], 0.0))
                else:
                    st.link(v.memset(rstd[:], 0.0))
                def last_tap(f):
                    j = n * FT + f
                    dve.wait_ge(conv_step, j + 1)
                    at_least(dve, sl_ready, j - (NBUF - 1))
                    v.scalar_tensor_tensor(c3[:, f % NBUF, :], hs[:, f % NBUF, 2:WB + 2], cw[:, f, 2:3], c2[:, f % NBUF, :], ALU.mult, ALU.add).then_inc(c3_ready, 1)

                dequantize(0)
                dequantize(1)
                for f in range(FT):
                    j = n * FT + f
                    dve.wait_ge(c1_ready, j + 1)
                    dve.wait_ge(hs_ready, j + 1)
                    v.scalar_tensor_tensor(c2[:, f % NBUF, :], hs[:, f % NBUF, 0:WB], cw[:, f, 0:1], c1[:, f % NBUF, :], ALU.mult, ALU.add).then_inc(conv_step, 1)
                    if f + 2 < FT:
                        dequantize(f + 2)
                    if f:
                        last_tap(f - 1)
                    if f == 12 and not (isinstance(n, int) and n == 0):
                        tail_a(st, n - 1, 1 - par)
                last_tap(FT - 1)
                if not (isinstance(n, int) and n == 0):
                    tail_b(st, n - 1)
                dve.wait_ge(sl_ready, n * FT + FT)
                v.tensor_reduce(mx[:], sl[:].rearrange("p f t -> p t f"), AX.X, ALU.max,
                                apply_absolute_value=True).then_inc(mx_ready, 1)
                dve.wait_ge(mt_done, n + 1)
                st.link(v.tensor_reduce(a2[:], p_m, AX.X, ALU.max))
                st.link(v.tensor_scalar(a2[:], a2[:], 1e-5, None, ALU.max))
                st.link(v.reciprocal(a2[:], a2[:]))
                st.link(v.tensor_scalar(s2[:], a2[:], 127.0, None, ALU.mult))
                st.link(v.reciprocal(i2[:, par, :], s2[:]))
                st.link(v.tensor_scalar(i2[:, par, :], i2[:, par, :], wm[:, 1:2], None, ALU.mult))
                st.link(v.tensor_scalar(dg[:, 0, :], ident[:], s2[:, 0:1], None, ALU.mult))
                v.tensor_scalar(dg[:, 1, :], ident[:], s2[:, 1:2], None, ALU.mult).then_inc(dg_ready, 1)
                dve.wait_ge(b_done, n + 1)
                at_least(dve, q2_ready, n)
                v.tensor_tensor(sq[:], sl[:], p_b.unsqueeze(1).to_broadcast([P, FT, WB]), ALU.mult).then_inc(sq_ready, 1)
                dve.wait_ge(sq_ready, n + 1)
                at_least(dve, o_done, n * 2)
                v.tensor_scalar(q2[:], sq[:], MAGIC, MAGIC, ALU.add, ALU.subtract).then_inc(q2_ready, 1)
                assert st.n == (NSTEP - TAIL if isinstance(n, int) and n == 0 else NSTEP), st.n

            blocks(dve, body)
            st = Steps(dve, step, NB * NSTEP - TAIL)
            tail_a(st, NB - 1, 1)
            tail_b(st, NB - 1)

        @block.gpsimd
        def _(pool):
            pool.wait_ge(consts, 5)

            def store(n, row):
                for u in range(2):
                    pool.wait_ge(out_ready, n * 2 + (u + 1))
                    pool.dma_start(out[bass.ds(row + u * P, P), :], xo[:, u, :]).then_inc(x_out[u], 16)

            def body(b, k, n):
                if not (isinstance(n, int) and n == 0):
                    store(n - 1, n * WB - WB)
            blocks(pool, body)
            store(NB - 1, NB * WB - WB)
            for u in range(2):
                pool.wait_ge(x_out[u], 16 * NB)


def decoder(nc, a):
    def dram(name, shape, dt=F32):
        return nc.dram_tensor(name, shape, dt).ap()

    x1, xm, ys, x2 = (dram(n, (TOK, D)) for n in ("x1", "xm", "ys", "x2"))
    mod_out = dram("mod_out", (TOK, 2 * D))
    keysT, film_w = dram("keysT", (P, B * N2)), dram("film_w", (DV, 4 * D))
    film_b, mask_row = dram("film_b", (1, 4 * D)), dram("mask_row", (B, N2), BF16)
    conv_k = dram("conv_k", (D, S))
    w1q, w2q, wmean = dram("w1q", (P, KD * F), BF16), dram("w2q", (P, FT * D), BF16), dram("wmean", (P, 2))
    q1T, inv_rows = dram("q1T", (D, TOK), BF16), dram("inv_rows", (1, TOK))

    attention(nc, a["x"], a["xT"], a["W_attn"], a["b_attn"], a["W_proj"], a["b_proj"], a["tri"], a["blockdiag"],
              a["eye"], x1)
    prepare(nc, a["ctxT"], a["Wk"], a["WvT"], a["W_film_in"], a["b_film_in"], a["W_film_out"], a["b_film_out"],
            a["gate"], a["mask2"], keysT, film_w, film_b, mask_row)
    cross(nc, x1, keysT, a["ctx"], film_w, film_b, mask_row, a["mask1"], a["Wq"], a["g_in"], a["b_in"], a["eye"],
          xm, mod_out)
    ssm_kernel(nc, a["log_dt"], a["A_re"], a["A_im"], a["C_re"], a["C_im"], a["angles"], conv_k)
    convolve(nc, xm, conv_k, a["D_skip"], a["dft"], a["idft"], a["eye"], ys)
    feed_forward(nc, x1, ys, mod_out, a["W1"], a["b1T"], a["W2"], a["b2"], a["g_ffn"], a["b_ffn"], a["g_out"],
                 a["b_out"], a["eye"], x2, q1T, inv_rows)
    quantize_weights(nc, a["w1T"], a["w2T"], w1q, w2q, wmean)
    bit_ffn(nc, x2, q1T, inv_rows, w1q, w2q, wmean, a["conv_w"], a["conv_b"], a["eye"], a["out"])


def transform_matrices():
    k, q = 4 * np.arange(S // 4)[None, :] + np.arange(4)[:, None], np.arange(S // 4)
    turn = 2 * np.pi * (((4 * k[:, :, None] + 1) * q) % (4 * S)) / (4 * S)

    def parts(re, im):
        m = np.stack([re, im, -im]).reshape(3, 4, 2, P, 2, P)
        return np.ascontiguousarray(m.transpose(5, 1, 2, 0, 4, 3).astype(np.float32))

    back = turn.transpose(0, 2, 1)
    return parts(np.cos(turn), -np.sin(turn)), parts(np.cos(back) / S, np.sin(back) / S)


def shape_constants():
    tri = np.triu(np.ones((P, P), np.float32))
    blockdiag = np.zeros((P, 4 * VW), np.float32)
    for r in range(4):
        blockdiag[DH * r:DH * r + DH, VW * r:VW * r + VW] = 1
    angles = np.zeros((P, 6 + 64), np.float32)
    for n, (re, im) in enumerate(((.25, .5), (.25, 0), (.5, .25))):
        angles[:NS, n], angles[NS:, n] = re, im
        angles[:, 3 + n] = angles[:, n] * np.float32(TWO_PI)
    angles[:, 6:38] = np.arange(32) * 32
    angles[:, 38:70] = np.arange(32)
    dft, idft = transform_matrices()
    return dict(tri=tri, blockdiag=blockdiag, eye=np.eye(P, dtype=np.float32), angles=angles, dft=dft, idft=idft)


def kernel(**inputs):
    import concourse.bacc as bacc
    from concourse.bass_utils import run_bass_kernel_spmd

    c = np.ascontiguousarray
    i = {k: np.asarray(v) for k, v in inputs.items()}
    X, A, N = "L0_xattn_", "L0_attn_", "L0_ffn_"
    x, ctx = i["x"].reshape(TOK, D), i["ctx_768"].reshape(B * N2, DV)

    def rows_of(wT):
        return c(wT.reshape(-1, P, wT.shape[1]).transpose(1, 0, 2).reshape(P, -1))

    arrays = dict(
        x=c(x), xT=c(x.T), ctx=c(ctx), ctxT=c(ctx.T),
        W_attn=i[A + "W_attn"], b_attn=i[A + "b_attn"], W_proj=i[A + "W_proj"], b_proj=i[A + "b_proj"],
        Wq=i[X + "Wq"], Wk=i[X + "Wk"], WvT=c(i[X + "Wv"].T),
        W_film_in=i[X + "W_film_in"], b_film_in=i[X + "b_film_in"],
        W_film_out=i[X + "W_film_out"], b_film_out=i[X + "b_film_out"], gate=i[X + "mod_gate"].reshape(1, 1),
        mask1=c(i["mask_BxS_bf1"].view(np.uint8).reshape(TOK // P, P).T), mask2=c(i["mask_BxS2_bf1"].view(np.uint8)),
        g_in=i[X + "g_norm_in"], b_in=i[X + "b_norm_in"], g_out=i[X + "g_norm_out"], b_out=i[X + "b_norm_out"],
        g_ffn=i[X + "g_ffn"], b_ffn=i[X + "b_ffn"], W1=i[X + "W1"], b1T=c(i[X + "b1"].reshape(FT, P).T),
        W2=i[X + "W2"], b2=i[X + "b2"], log_dt=i[X + "log_dt"], A_re=c(i[X + "A_re"].T), A_im=c(i[X + "A_im"].T),
        C_re=c(i[X + "C_re"].T), C_im=c(i[X + "C_im"].T), D_skip=i[X + "D_skip"],
        w1T=rows_of(i[N + "w1"].T), w2T=rows_of(i[N + "w2"].T),
        conv_w=c(i[N + "conv_w"].reshape(FT, P, 3).transpose(1, 0, 2)), conv_b=c(i[N + "conv_b"].reshape(FT, P).T),
        **shape_constants())
    arrays = {k: c(v) for k, v in arrays.items()}
    nc = bacc.Bacc("TRN2", target_bir_lowering=False, num_devices=1)
    a = {k: nc.dram_tensor("in_" + k, v.shape, mybir.dt.from_np(v.dtype), kind="ExternalInput").ap()
         for k, v in arrays.items()}
    a["out"] = nc.dram_tensor("out", (TOK, D), F32, kind="ExternalOutput").ap()
    decoder(nc, a)
    r = run_bass_kernel_spmd(nc, [{"in_" + k: v for k, v in arrays.items()}], core_ids=[0])
    return r.results[0]["out"].reshape(B, S, D)
```
